# Optimizing a Trainium2 kernel written in Bass

```python
import numpy as np
import jax
import jax.numpy as jnp

def _softmax(x, axis=-1):
    return jax.nn.softmax(x, axis=axis)

def _gelu(x):
    return jax.nn.gelu(x, approximate=True)

def _silu(x):
    return jax.nn.silu(x)

def _sigmoid(x):
    return jax.nn.sigmoid(x)

def _layernorm(x, axis=-1, eps=1e-05):
    m = jnp.mean(x, axis=axis, keepdims=True)
    v = jnp.var(x, axis=axis, keepdims=True)
    return (x - m) / jnp.sqrt(v + eps)

def _scatter_add(tgt, idx, src, axis=0):
    return tgt.at[idx].add(src)

def _segment_sum(src, seg, n):
    return jax.ops.segment_sum(src, seg, n)
kernel_name = 'mk_sandwich_d1_jaxref_r8_4e29d8'

def setup_inputs(seed: int=0):
    np.random.seed(seed)
    _w = jnp.asarray

    def _L0_attn_setup():
        import jax, jax.numpy as jnp
        import numpy as np
        NL, H, N, B, L = (4, 128, 32, 8, 128)

        def _layernorm_channels(z, w, b):
            mu = jnp.mean(z, axis=1, keepdims=True)
            var = jnp.mean((z - mu) ** 2, axis=1, keepdims=True)
            zn = (z - mu) * jax.lax.rsqrt(var + 1e-05)
            return zn * w[None, :, None] + b[None, :, None]

        def _s4d_layer(z, log_dt, A_re_log, A_im, C_re, C_im, D_skip, W, bvec):
            Bz, Hh, Lz = z.shape
            dt = jnp.exp(log_dt)
            A = -jnp.exp(A_re_log) + 1j * A_im
            dtA = A * dt[:, None]
            C = (C_re + 1j * C_im) * (jnp.expm1(dtA) / A)
            l = jnp.arange(Lz, dtype=jnp.float32)
            K = 2.0 * jnp.einsum('hn,hnl->hl', C, jnp.exp(dtA[:, :, None] * l)).real
            kf = jnp.fft.rfft(K, n=2 * Lz)
            uf = jnp.fft.rfft(z, n=2 * Lz)
            y = jnp.fft.irfft(uf * kf, n=2 * Lz)[..., :Lz]
            y = y + z * D_skip[:, None]
            y = jax.nn.gelu(y)
            out = jnp.einsum('oh,bhl->bol', W, y) + bvec[None, :, None]
            return out[:, :Hh] * jax.nn.sigmoid(out[:, Hh:])
        key = jax.random.key(seed)
        ks = jax.random.split(key, 10)
        x = jax.random.normal(ks[0], (B, L, H), dtype=jnp.float32)
        ln_w = jnp.ones((NL, H), jnp.float32)
        ln_b = jnp.zeros((NL, H), jnp.float32)
        log_dt = (jax.random.uniform(ks[1], (NL, H)) * (np.log(0.1) - np.log(0.001)) + np.log(0.001)).astype(jnp.float32)
        A_re_log = jnp.full((NL, H, N), np.log(0.5), jnp.float32)
        A_im = jnp.broadcast_to(np.pi * jnp.arange(N, dtype=jnp.float32), (NL, H, N))
        C_re = jax.random.normal(ks[2], (NL, H, N), jnp.float32) * 0.5 ** 0.5
        C_im = jax.random.normal(ks[3], (NL, H, N), jnp.float32) * 0.5 ** 0.5
        D_skip = jax.random.normal(ks[4], (NL, H), jnp.float32)
        W_out = jax.random.normal(ks[5], (NL, 2 * H, H), jnp.float32) * (1.0 / np.sqrt(H))
        b_out = jnp.zeros((NL, 2 * H), jnp.float32)
        return {'x': x, 'ln_w': ln_w, 'ln_b': ln_b, 'log_dt': log_dt, 'A_re_log': A_re_log, 'A_im': A_im, 'C_re': C_re, 'C_im': C_im, 'D_skip': D_skip, 'W_out': W_out, 'b_out': b_out}
    _L0_attn_in = _L0_attn_setup()

    def _L0_ffn_setup():
        import jax, jax.numpy as jnp
        import numpy as np
        TOPK = 2
        key = jax.random.key(seed)
        k0, k1, k2, k3 = jax.random.split(key, 4)
        B, S, H, I, E = (4, 256, 128, 256, 8)
        return {'hidden_states': jax.random.normal(k0, (B, S, H), dtype=jnp.float32), 'w1': jax.random.normal(k1, (E, 2 * I, H), dtype=jnp.float32) * 0.02, 'w2': jax.random.normal(k2, (E, H, I), dtype=jnp.float32) * 0.02, 'router_w': jax.random.normal(k3, (E, H), dtype=jnp.float32) * 0.02}
    _L0_ffn_in = _L0_ffn_setup()
    _d = {'L0_attn_x': _L0_attn_in['x'], 'L0_attn_ln_w': _L0_attn_in['ln_w'], 'L0_attn_ln_b': _L0_attn_in['ln_b'], 'L0_attn_log_dt': _L0_attn_in['log_dt'], 'L0_attn_A_re_log': _L0_attn_in['A_re_log'], 'L0_attn_A_im': _L0_attn_in['A_im'], 'L0_attn_C_re': _L0_attn_in['C_re'], 'L0_attn_C_im': _L0_attn_in['C_im'], 'L0_attn_D_skip': _L0_attn_in['D_skip'], 'L0_attn_W_out': _L0_attn_in['W_out'], 'L0_attn_b_out': _L0_attn_in['b_out'], 'L0_ffn_w1': _L0_ffn_in['w1'], 'L0_ffn_w2': _L0_ffn_in['w2'], 'L0_ffn_router_w': _L0_ffn_in['router_w']}
    _x0 = _d['L0_attn_x']
    _d['L0_attn_x'] = jax.random.normal(jax.random.fold_in(jax.random.key(seed), 1), (16, 512, 128), dtype=_x0.dtype)
    del _x0
    return _d

def reference(L0_attn_x, L0_attn_ln_w, L0_attn_ln_b, L0_attn_log_dt, L0_attn_A_re_log, L0_attn_A_im, L0_attn_C_re, L0_attn_C_im, L0_attn_D_skip, L0_attn_W_out, L0_attn_b_out, L0_ffn_w1, L0_ffn_w2, L0_ffn_router_w):

    def _L0_attn_ref(x, ln_w, ln_b, log_dt, A_re_log, A_im, C_re, C_im, D_skip, W_out, b_out):
        import jax, jax.numpy as jnp
        import numpy as np
        NL, H, N, B, L = (4, 128, 32, 8, 128)

        def _layernorm_channels(z, w, b):
            mu = jnp.mean(z, axis=1, keepdims=True)
            var = jnp.mean((z - mu) ** 2, axis=1, keepdims=True)
            zn = (z - mu) * jax.lax.rsqrt(var + 1e-05)
            return zn * w[None, :, None] + b[None, :, None]

        def _s4d_layer(z, log_dt, A_re_log, A_im, C_re, C_im, D_skip, W, bvec):
            Bz, Hh, Lz = z.shape
            dt = jnp.exp(log_dt)
            A = -jnp.exp(A_re_log) + 1j * A_im
            dtA = A * dt[:, None]
            C = (C_re + 1j * C_im) * (jnp.expm1(dtA) / A)
            l = jnp.arange(Lz, dtype=jnp.float32)
            K = 2.0 * jnp.einsum('hn,hnl->hl', C, jnp.exp(dtA[:, :, None] * l)).real
            kf = jnp.fft.rfft(K, n=2 * Lz)
            uf = jnp.fft.rfft(z, n=2 * Lz)
            y = jnp.fft.irfft(uf * kf, n=2 * Lz)[..., :Lz]
            y = y + z * D_skip[:, None]
            y = jax.nn.gelu(y)
            out = jnp.einsum('oh,bhl->bol', W, y) + bvec[None, :, None]
            return out[:, :Hh] * jax.nn.sigmoid(out[:, Hh:])
        h = jnp.transpose(x, (0, 2, 1))
        for i in range(NL):
            z = _layernorm_channels(h, ln_w[i], ln_b[i])
            z = _s4d_layer(z, log_dt[i], A_re_log[i], A_im[i], C_re[i], C_im[i], D_skip[i], W_out[i], b_out[i])
            h = z + h
        return jnp.transpose(h, (0, 2, 1))

    def _L0_ffn_ref(hidden_states, w1, w2, router_w):
        import jax, jax.numpy as jnp
        import numpy as np
        TOPK = 2
        orig_shape = hidden_states.shape
        H = orig_shape[-1]
        E = w1.shape[0]
        I = w2.shape[-1]
        dtype = hidden_states.dtype
        x = hidden_states.reshape(-1, H)
        gating = x @ router_w.T
        probs = jax.nn.softmax(gating.astype(jnp.float32), axis=-1)
        topk_weights, selected_experts = jax.lax.top_k(probs, TOPK)
        topk_weights = topk_weights.astype(dtype)
        out = jnp.zeros_like(x)
        for e in range(E):
            ew = jnp.sum(topk_weights * (selected_experts == e), axis=-1, keepdims=True)
            h = x @ w1[e].T
            gate = jax.nn.silu(h[:, :I])
            y = h[:, I:] * gate @ w2[e].T
            out = out + y * ew
        return out.reshape(orig_shape)
    x = L0_attn_x
    x = x + _layernorm(_L0_attn_ref(_layernorm(x, axis=-1), L0_attn_ln_w, L0_attn_ln_b, L0_attn_log_dt, L0_attn_A_re_log, L0_attn_A_im, L0_attn_C_re, L0_attn_C_im, L0_attn_D_skip, L0_attn_W_out, L0_attn_b_out), axis=-1)
    x = x + _layernorm(_L0_ffn_ref(_layernorm(x, axis=-1), L0_ffn_w1, L0_ffn_w2, L0_ffn_router_w), axis=-1)
    return x

_drawn_inputs = setup_inputs


def setup_inputs(seed=0):
    import zlib

    import numpy as np

    out = dict(_drawn_inputs(seed))
    spreads = {'L0_attn_ln_w': (1.0, 0.2),
     'L0_attn_ln_b': (0.0, 0.1),
     'L0_attn_A_re_log': (-0.6931471824645996, 0.2),
     'L0_attn_b_out': (0.0, 0.1)}
    factors = {}
    for name, (base, spread) in spreads.items():
        noise = np.random.default_rng([zlib.crc32(name.encode()), seed]).standard_normal(out[name].shape)
        drawn = base * np.exp(spread * noise) if base else spread * noise
        out[name] = jnp.asarray(drawn.astype(out[name].dtype))
    for name, factor in factors.items():
        out[name] = (out[name] * factor).astype(out[name].dtype)
    return out
```

```python
import concourse.bass as bass
from concourse import mybir
from contextlib import ExitStack

P = 128
NL, H, N = 4, 128, 32
B, L = 16, 512
J = L // P
TILES = J * B
CHUNK = 16
CHUNKS = TILES // CHUNK
QUADS = TILES // 4
E, I = 8, 256
NA, NB = 16, 32
GROUP = 8
GROUPS = H // GROUP
SLOTS = 4
KPAD = 128
KROW = KPAD + L
EPS = 1e-5
F32 = mybir.dt.float32
ALU = mybir.AluOpType
ACT = mybir.ActivationFunctionType
AX = mybir.AxisListType
TWO_PI = 6.283185307179586
TWO_PI_HI = 6.28125
TWO_PI_LO = TWO_PI - TWO_PI_HI
ROUND = 12582912.0
PI = 3.1415925


class Steps:

    def __init__(self, eng, sem, base=0):
        self.eng, self.sem, self.base, self.n = eng, sem, base, 0

    def done(self, ins):
        ins.then_inc(self.sem, 1)
        self.n += 1

    def after(self):
        self.eng.wait_ge(self.sem, self.base + self.n)


def build(nc, x, a_re_log, a_im, c_re, c_im, log_dt, d_skip, ln_w, ln_b, w_out, b_out, w1, w2, router, out):
    kd = nc.dram_tensor("kernels_dram", [NL, H, KROW], F32)
    ctx = ExitStack()
    with ctx:
        def sb(name, shape):
            return ctx.enter_context(nc.sbuf_tensor(name, shape, F32))

        def sem(name):
            return ctx.enter_context(nc.semaphore(name))

        bank = [ctx.enter_context(nc.psum_tensor(f"bank{i}", [P, 512], F32)) for i in range(8)]

        hres = sb("hres", [P, TILES, H])
        zbuf = sb("zbuf", [P, TILES * H])
        ybuf = sb("ybuf", [P, TILES, H])
        toep = sb("toep", [P, SLOTS, GROUP, L])
        z_conv = zbuf[:, :].rearrange("p (h t) -> p h t", h=H)
        z_tok = zbuf[:, :].rearrange("p (t h) -> p t h", h=H)
        toep_flat = toep[:, :, :, :].rearrange("p s g l -> p (s g l)")

        ln_tmp = sb("ln_tmp", [P, CHUNK, H])
        stats = sb("stats", [P, CHUNK, 6])
        mean = sb("mean", [P, CHUNK])
        diff = sb("diff", [P, CHUNK])
        m2 = sb("m2", [P, CHUNK])
        var = sb("var", [P, CHUNK])
        rstd = sb("rstd", [P, CHUNK])
        neg_half = sb("neg_half", [P, CHUNK])
        lnw = sb("lnw", [P, NL + 1, H])
        lnb = sb("lnb", [P, NL + 1, H])
        ident = sb("ident", [P, P])
        wo = sb("wo", [P, NL, 2 * H])
        wo_cur = sb("wo_cur", [P, 2 * H])
        bo = sb("bo", [P, NL, 2])
        bo_half = sb("bo_half", [P, NL, 2])
        bo_cur = sb("bo_cur", [P, 2])
        glu_work = sb("glu_work", [P, 4, 2, 512])
        g_act = glu_work[:, 0].rearrange("p s (t n) -> p s t n", t=4)
        g_tanh, g_lin, g_out = glu_work[:, 1], glu_work[:, 2], glu_work[:, 3]
        half_pi = sb("half_pi", [P, 1])
        one_col = sb("one_col", [P, 1])

        par = sb("par", [P, 6, H])
        sm = sb("sm", [P, 16, H])
        d_row = glu_work[:].rearrange("p a b n -> p (a b n)").rearrange("p (h b) -> p h b", h=H)
        d_in = sb("d_in", [NL, H])
        d_sel = sb("d_sel", [P, NL, NA])
        iota = sb("iota", [P, NB + NA])
        def big(buf, at, n):
            return buf[:, at:at + H * n].rearrange("p (h n) -> p h n", h=H)
        q_re = big(zbuf, 0, NB)
        q_im = big(zbuf, H * NB, NB)
        ybuf_flat = ybuf[:, :, :].rearrange("p t h -> p (t h)")
        cp_re = big(ybuf_flat, 0, NA)
        cp_im = big(ybuf_flat, H * NA, NA)
        q_ang = big(ybuf_flat, 2 * H * NA, NB)
        q_cnt = big(toep_flat, 6 * H * NA, NB)
        p_ang = big(toep_flat, 0, NA)
        p_cnt = big(toep_flat, H * NA, NA)
        p_mag = big(toep_flat, 2 * H * NA, NA)
        p_sin = big(toep_flat, 3 * H * NA, NA)
        p_t1 = big(toep_flat, 4 * H * NA, NA)
        p_t2 = big(toep_flat, 5 * H * NA, NA)
        cp_blk = toep_flat[:, 4 * H * NA:6 * H * NA].rearrange("p (s k c l a) -> p s k c l a", s=2, k=2, c=16, l=NL)
        k_sb = q_ang[0:NL * NA]
        zeros = ln_tmp[:, 0:4, :]

        w1_sb = toep_flat[:, 10240:11264].rearrange("p (s n) -> p s n", s=2)
        w2_sb = toep_flat[:, 11264:11776].rearrange("p (s c n) -> p s c n", s=2, c=2)
        router_sb = sb("router_sb", [P, E])
        route = toep_flat[:, 0:12 * TILES * E].rearrange("p (k t e) -> p k t e", k=12, e=E)
        rank = sb("rank", [P, E])
        gate_act = toep_flat[:, 11776:12800].rearrange("p (c n) -> p c n", c=2)
        inner = toep_flat[:, 8192:8192 + 2048].rearrange("p (s c n) -> p s c n", s=2, c=2)

        s_x, s_par, s_wts, s_dskip = sem("x_loaded"), sem("par_loaded"), sem("weights_loaded"), sem("dskip_loaded")
        s_const, s_iota, s_sel = sem("const_ready"), sem("iota_ready"), sem("sel_ready")
        s_dve, s_ln_dve, s_lay_dve = sem("dve_steps"), sem("ln_steps"), sem("layer_dve_steps")
        s_act, s_wo, s_bo, s_bh = sem("act_steps"), sem("wo_ready"), sem("bo_ready"), sem("bo_halved")
        s_exp1, s_small, s_pmag, s_pcyc = sem("exp_small"), sem("small_ready"), sem("p_mag_in"), sem("p_cycles")
        s_e2 = sem("act_small_done")
        s_qmag_in, s_pmag_done, s_qmag_done = sem("q_mag_in"), sem("p_mag_done"), sem("q_mag_done")
        s_qk, s_qcyc, s_ptrig, s_qtrig = sem("q_count_used"), sem("q_cycles"), sem("p_trig"), sem("q_trig")
        s_cp, s_qready, s_dpad = sem("cp_ready"), sem("q_ready"), sem("dpad_ready")
        s_blk, s_kps, s_ksb = sem("blk_staged"), sem("kernel_psum"), sem("kernel_evacuated")
        s_blk0 = sem("blk_zeroed")
        s_kd, s_kz = sem("kernels_stored"), sem("pad_stored")
        s_var, s_rstd = sem("ln_var"), sem("ln_rstd")
        s_toep = [sem(f"toep_loaded{s}") for s in range(SLOTS)]
        s_z, s_conv, s_y = sem("z_ready"), sem("conv_done"), sem("y_ready")
        s_yT, s_gelu, s_w, s_glu_in = sem("yT_done"), sem("gelu_done"), sem("w_done"), sem("glu_in")
        s_glu, s_back, s_hadd = sem("glu_done"), sem("back_done"), sem("h_added")
        s_x2, s_z2, s_z2T, s_z2sb = sem("x_reloaded"), sem("z2_ready"), sem("z2T_psum"), sem("z2T_ready")
        s_rt, s_rexp_in, s_rexp, s_ew = sem("router_done"), sem("router_exp_in"), sem("router_exp"), sem("ew_ready")
        s_w1 = [sem(f"expert_w{s}") for s in range(2)]
        s_up, s_silu, s_inner, s_yexp, s_acc = (sem("up_done"), sem("silu_done"), sem("inner_ready"),
                                                sem("expert_y"), sem("acc_done"))
        s_res, s_out = sem("result_ready"), sem("out_stored")

        block = ctx.enter_context(nc.Block())

        @block.sync
        def _(sp):
            sp.dma_start(par[:, 0, :], a_re_log).then_inc(s_par, 16)
            for layer in range(NL):
                sp.dma_start(par[layer * N:(layer + 1) * N, 1, :],
                             bass.AP(log_dt.tensor, layer * H, [[0, N], [1, H]])).then_inc(s_par, 16)
            sp.dma_start(par[:, 2, :], a_im).then_inc(s_par, 16)
            sp.dma_start(par[:, 3, :], c_re).then_inc(s_par, 16)
            sp.dma_start(par[:, 4, :], c_im).then_inc(s_par, 16)
            sp.dma_start(d_in[:, :], d_skip).then_inc(s_dskip, 16)
            sp.dma_start(hres[:, :, :], x).then_inc(s_x, 16)
            sp.dma_start(lnw[:, 0:NL, :], bass.AP(ln_w.tensor, 0, [[0, P], [H, NL], [1, H]])).then_inc(s_wts, 16)
            sp.dma_start(lnb[:, 0:NL, :], bass.AP(ln_b.tensor, 0, [[0, P], [H, NL], [1, H]])).then_inc(s_wts, 16)
            sp.dma_start(wo[:, :, :], w_out).then_inc(s_wts, 16)
            sp.dma_start(bo[:, :, :], b_out).then_inc(s_wts, 16)
            sp.dma_start(router_sb[:, :], router).then_inc(s_wts, 16)
            sp.wait_ge(s_const, 1)
            sp.dma_start(kd[:, :, 0:KPAD].rearrange("l h k -> h l k"), zeros).then_inc(s_kz, 16)
            sp.wait_ge(s_ksb, 2 + H // 16)
            for layer in range(NL):
                sp.dma_start(kd[layer, :, KPAD:KROW].rearrange("h (a b) -> a h b", b=NB),
                             k_sb[layer * NA:(layer + 1) * NA]).then_inc(s_kd, 16)
            sp.wait_ge(s_kd, 16 * NL)
            sp.wait_ge(s_kz, 16)
            with sp.Fori(0, NL) as layer:
                with sp.Fori(0, GROUPS // SLOTS) as g:
                    for s in range(SLOTS):
                        sp.wait_ge(s_conv, layer * GROUPS + g * SLOTS + s + 1)
                        first = KPAD - (P - 1)
                        src = bass.AP(kd, layer * (H * KROW) + g * (SLOTS * GROUP * KROW)
                                      + (s * GROUP * KROW + first), [[1, P], [KROW, GROUP], [1, L]])
                        sp.dma_start(toep[:, s, :, :], src).then_inc(s_toep[s], 16)
            sp.wait_ge(s_yT, NL * TILES // 4)
            sp.dma_start(ybuf[:, :, :], x).then_inc(s_x2, 16)
            for e in range(E):
                if e >= 2:
                    sp.wait_ge(s_yexp, (e - 1) * QUADS)
                sp.dma_start(w1_sb[:, e % 2, :], w1[e, :, :]).then_inc(s_w1[e % 2], 16)
                sp.dma_start(w2_sb[:, e % 2, :, :], w2[e, :, :, :]).then_inc(s_w1[e % 2], 16)
            for c in range(CHUNKS):
                sp.wait_ge(s_res, c + 1)
                sp.dma_start(out[:, c * CHUNK:(c + 1) * CHUNK, :], z_tok[:, c * CHUNK:(c + 1) * CHUNK, :]).then_inc(s_out, 16)
            sp.wait_ge(s_out, 16 * CHUNKS)

        @block.gpsimd
        def _(pool):
            nc.gpsimd.memset(ln_tmp[:, 0:4, :], 0.0).then_inc(s_const, 1)
            nc.gpsimd.iota(iota[:, 0:NB], pattern=[[1, NB]], base=0, channel_multiplier=0,
                           allow_small_or_imprecise_dtypes=True).then_inc(s_iota, 1)
            nc.gpsimd.iota(iota[:, NB:NB + NA], pattern=[[NB, NA]], base=0, channel_multiplier=0,
                           allow_small_or_imprecise_dtypes=True).then_inc(s_iota, 1)
            nc.gpsimd.iota(rank[:, :], pattern=[[-1, E]], base=E, channel_multiplier=0,
                           allow_small_or_imprecise_dtypes=True).then_inc(s_iota, 1)
            nc.gpsimd.memset(ident[:, :], 0.0).then_inc(s_sel, 1)
            nc.gpsimd.memset(d_sel[:, :, :], 0.0).then_inc(s_sel, 1)
            nc.gpsimd.memset(neg_half[:, :], -0.5).then_inc(s_sel, 1)
            nc.gpsimd.memset(half_pi[:, :], TWO_PI / 4).then_inc(s_iota, 1)
            nc.gpsimd.memset(lnw[:, NL, :], 1.0).then_inc(s_sel, 1)
            nc.gpsimd.memset(lnb[:, NL, :], 0.0).then_inc(s_sel, 1)
            pool.wait_ge(s_sel, 5)
            nc.gpsimd.affine_select(out=ident[:, :], in_=ident[:, :], compare_op=ALU.not_equal, fill=1.0,
                                    base=0, pattern=[[-1, P]], channel_multiplier=1).then_inc(s_sel, 1)
            nc.gpsimd.affine_select(out=d_sel[:, :, :], in_=d_sel[:, :, :], compare_op=ALU.not_equal, fill=1.0,
                                    base=0, pattern=[[-NA, NL], [-1, NA]], channel_multiplier=NA).then_inc(s_sel, 1)
            pool.wait_ge(s_small, 1)
            pool.wait_ge(s_iota, 2)
            nc.gpsimd.tensor_tensor(p_mag, sm[:, 1, :].unsqueeze(2).to_broadcast([P, H, NA]),
                                    iota[:, NB:NB + NA].unsqueeze(1).to_broadcast([P, H, NA]), ALU.mult).then_inc(s_pmag, 1)
            nc.gpsimd.tensor_tensor(q_re, sm[:, 1, :].unsqueeze(2).to_broadcast([P, H, NB]),
                                    iota[:, 0:NB].unsqueeze(1).to_broadcast([P, H, NB]), ALU.mult).then_inc(s_qmag_in, 1)
            pool.wait_ge(s_cp, 1)
            nc.gpsimd.memset(cp_blk, 0.0).then_inc(s_blk0, 1)
            with pool.Fori(0, 2 * CHUNKS + NL * CHUNKS + 2 * CHUNKS) as i:
                pool.wait_ge(s_var, i + 1)
                nc.gpsimd.tensor_tensor(rstd[:, :], var[:, :], neg_half[:, :], ALU.pow).then_inc(s_rstd, 1)

        @block.scalar
        def _(act):
            A = nc.scalar.activation
            act.wait_ge(s_par, 16 * (4 + NL))
            A(sm[:, 0, :], par[:, 1, :], ACT.Exp).then_inc(s_exp1, 1)
            A(sm[:, 2, :], par[:, 0, :], ACT.Exp).then_inc(s_exp1, 1)
            act.wait_ge(s_small, 1)
            A(sm[:, 3, :], sm[:, 1, :], ACT.Tanh, scale=0.5).then_inc(s_exp1, 1)
            act.wait_ge(s_pmag, 1)
            A(p_mag, p_mag, ACT.Exp).then_inc(s_pmag_done, 1)
            act.wait_ge(s_qmag_in, 1)
            act.wait_ge(s_qcyc, 1)
            A(q_cnt, q_re, ACT.Exp).then_inc(s_qmag_done, 1)
            act.wait_ge(s_iota, 4)
            act.wait_ge(s_pcyc, 2)
            A(sm[:, 5, :], sm[:, 4, :], ACT.Sin).then_inc(s_e2, 1)
            A(sm[:, 6, :], sm[:, 4, :], ACT.Sin, scale=0.5).then_inc(s_e2, 1)
            A(sm[:, 7, :], sm[:, 4, :], ACT.Abs).then_inc(s_act, 1)
            A(p_sin, p_ang, ACT.Sin).then_inc(s_ptrig, 1)
            act.wait_ge(s_ptrig, 1)
            A(p_ang, p_ang, ACT.Abs).then_inc(s_act, 1)
            act.wait_ge(s_act, 2)
            A(sm[:, 8, :], sm[:, 7, :], ACT.Sin, bias=half_pi[:, 0:1], scale=-1.0).then_inc(s_e2, 1)
            A(p_cnt, p_ang, ACT.Sin, bias=half_pi[:, 0:1], scale=-1.0).then_inc(s_ptrig, 1)
            act.wait_ge(s_qcyc, 2)
            A(q_im, q_ang, ACT.Sin, scale=-1.0).then_inc(s_qtrig, 1)
            act.wait_ge(s_qtrig, 1)
            A(q_ang, q_ang, ACT.Abs).then_inc(s_act, 1)
            act.wait_ge(s_act, 3)
            act.wait_ge(s_qmag_done, 1)
            A(q_re, q_ang, ACT.Sin, bias=half_pi[:, 0:1], scale=-1.0).then_inc(s_qtrig, 1)
            act.wait_ge(s_cp, 1)
            act.wait_ge(s_blk0, 1)
            for g in range(H // 16):
                act.wait_ge(s_kps, g + 1)
                for layer in range(NL):
                    rows = slice(layer * N, (layer + 1) * N)
                    for k, src in ((0, cp_re), (1, cp_im)):
                        A(cp_blk[rows, g % 2, k, :, layer, :], src[rows, g * 16:(g + 1) * 16, :],
                          ACT.Copy).then_inc(s_blk, 1)
            act.wait_ge(s_wts, 16 * 5)
            A(bo_half[:, :, :], bo[:, :, :], ACT.Copy, scale=0.5).then_inc(s_bh, 1)
            act.wait_ge(s_bh, 1)
            act.sem_inc(s_y, 2)
            with act.Fori(0, NL) as layer:
                for g in range(GROUPS):
                    act.wait_ge(s_conv, SLOTS + layer * GROUPS + g + 1)
                    A(ybuf[:, :, g * GROUP:(g + 1) * GROUP],
                      bank[g % 2][:, :].rearrange("p (c t) -> p t c", c=GROUP), ACT.Copy).then_inc(s_y, 1)
                A(wo_cur[:, :], wo[:, bass.ds(layer, 1), :].rearrange("p a n -> p (a n)"), ACT.Copy).then_inc(s_wo, 1)
                A(bo_cur[:, :], bo_half[:, bass.ds(layer, 1), :].rearrange("p a n -> p (a n)"), ACT.Copy).then_inc(s_bo, 1)
                act.wait_ge(s_bo, layer + 1)

                def gelu(q):
                    act.wait_ge(s_yT, layer * QUADS + q + 1)
                    ap = bank[q % 2][:, :]
                    back = bass.AP(ap.tensor, ap.offset + P - 1, [list(ap.ap[0]), [P, 4], [-1, P]])
                    A(g_act[:, q % 2, :, :], back, ACT.Gelu_apprx_tanh).then_inc(s_gelu, 1)

                def halves(q):
                    act.wait_ge(s_w, layer * QUADS + q + 1)
                    act.wait_ge(s_glu, layer * QUADS + q + 1)
                    A(g_tanh[:, q % 2, :], bank[4 + q % 2][:, :], ACT.Tanh, scale=0.5,
                      bias=bo_cur[:, 1:2]).then_inc(s_glu_in, 1)
                    A(g_lin[:, q % 2, :], bank[2 + q % 2][:, :], ACT.Identity, scale=0.5,
                      bias=bo_cur[:, 0:1]).then_inc(s_glu_in, 1)
                for q in range(QUADS + 1):
                    if q < QUADS:
                        gelu(q)
                    if q > 0:
                        halves(q - 1)
            for q in range(QUADS):
                act.wait_ge(s_z2T, q + 1)
                A(zbuf[:, q * 512:(q + 1) * 512], bank[q % 2][:, :], ACT.Copy).then_inc(s_z2sb, 1)
            act.wait_ge(s_rexp_in, 1)
            A(route[:, 1], route[:, 0], ACT.Exp).then_inc(s_rexp, 1)
            with act.Fori(0, E) as e:
                with act.Fori(0, 4) as qc:
                    for k in range(4):
                        for c in range(2):
                            act.wait_ge(s_up, ((e * 4 + qc) * 4 + k) * 2 + c + 1)
                            A(gate_act[:, c, :], bank[2 * c][:, :], ACT.Silu).then_inc(s_silu, 1)

        @block.tensor
        def _(pe):
            MM = nc.tensor.matmul
            pe.sem_inc(s_kps, 2)
            pe.wait_ge(s_dpad, 1)
            pe.wait_ge(s_sel, 7)
            pe.wait_ge(s_qready, 1)
            with pe.Fori(0, 4) as g2:
                for s in range(2):
                    pe.wait_ge(s_blk, (g2 * 2 + s + 1) * 2 * NL)
                    pe.wait_ge(s_ksb, g2 * 2 + s + 1)
                    MM(bank[s][0:NL * NA, :], d_sel[:, :, :].rearrange("p l a -> p (l a)"),
                       d_row[:, bass.ds((g2 * 2 + s) * 16, 16), :], start=True, stop=False)
                    for c in range(16):
                        for k, q in ((0, q_re), (1, q_im)):
                            last = MM(bank[s][0:NL * NA, c * NB:(c + 1) * NB],
                                      cp_blk[:, s, k, c, :, :].rearrange("p l a -> p (l a)"),
                                      q[:, bass.ds((g2 * 2 + s) * 16 + c, 1), :].rearrange("p a b -> p (a b)"),
                                      start=False, stop=(c == 15 and k == 1))
                    last.then_inc(s_kps, 1)
            pe.sem_inc(s_conv, SLOTS)
            pe.wait_ge(s_wts, 16 * 5)
            with pe.Fori(0, NL) as layer:
                with pe.Fori(0, GROUPS // SLOTS) as g:
                    pe.wait_ge(s_z, (layer + 1) * CHUNKS)
                    for s in range(SLOTS):
                        pe.wait_ge(s_toep[s], (layer * (GROUPS // SLOTS) + g + 1) * 16)
                        pe.wait_ge(s_y, layer * GROUPS + g * SLOTS + s + 1)
                        for c in range(GROUP):
                            for d in range(J):
                                last = MM(bank[s % 2][:, c * TILES + d * B:(c + 1) * TILES],
                                          toep[:, s, c, d * P:(d + 1) * P],
                                          z_conv[:, bass.ds((g * SLOTS + s) * GROUP + c, 1), 0:TILES - d * B]
                                          .rearrange("p a t -> p (a t)"), start=(d == 0), stop=(d == J - 1))
                        last.then_inc(s_conv, 1)
                pe.wait_ge(s_y, 2 + (layer + 1) * GROUPS)
                pe.wait_ge(s_wo, layer + 1)

                def forward(q):
                    for t in range(4):
                        last = nc.tensor.transpose(bank[q % 2][:, t * P:(t + 1) * P], ybuf[:, q * 4 + t, :], ident[:, :])
                    last.then_inc(s_yT, 1)

                def weights(q):
                    pe.wait_ge(s_gelu, layer * QUADS + q + 1)
                    g = g_act[:, q % 2, :, :].rearrange("p a t -> p (a t)")
                    MM(bank[2 + q % 2][:, :], wo_cur[:, 0:H], g, start=True, stop=True)
                    MM(bank[4 + q % 2][:, :], wo_cur[:, H:2 * H], g, start=True, stop=True).then_inc(s_w, 1)

                def backward(q):
                    pe.wait_ge(s_glu, 2 + layer * QUADS + q + 1)
                    pe.wait_ge(s_hadd, layer * QUADS + q + 1)
                    for t in range(4):
                        last = nc.tensor.transpose(bank[6 + q % 2][:, t * P:(t + 1) * P],
                                                   g_out[:, q % 2, t * P:(t + 1) * P], ident[:, :])
                    last.then_inc(s_back, 1)
                forward(0)
                for q in range(QUADS + 1):
                    if q + 1 < QUADS:
                        forward(q + 1)
                    if q > 0:
                        backward(q - 1)
                    if q < QUADS:
                        weights(q)
            pe.wait_ge(s_z2, CHUNKS)
            for q in range(QUADS + 1):
                if q < QUADS:
                    if q >= 2:
                        pe.wait_ge(s_z2sb, q - 1)
                    for t in range(4):
                        last = nc.tensor.transpose(bank[q % 2][:, t * P:(t + 1) * P], ybuf[:, q * 4 + t, :], ident[:, :])
                    last.then_inc(s_z2T, 1)
                if q > 0:
                    pe.wait_ge(s_z2sb, q)
                    for t in range(q * 4 - 4, q * 4):
                        last = MM(bank[7][:, t * E:(t + 1) * E], zbuf[:, t * P:(t + 1) * P], router_sb[:, :],
                                  start=True, stop=True)
            last.then_inc(s_rt, 1)
            with pe.Fori(0, E // 2) as e2:
                for s in range(2):
                    with pe.Fori(0, QUADS // 4) as qc:
                        pe.wait_ge(s_w1[s], (e2 + 1) * 32)
                        at = (e2 * 2 + s) * QUADS + qc * 4

                        def up(k, c):
                            pe.wait_ge(s_inner, (at + k) * 2 + c + 1)
                            z = zbuf[:, bass.ds((qc * 4 + k) * 512, 512)]
                            MM(bank[2 * c][:, :], w1_sb[:, s, c * P:(c + 1) * P], z, start=True, stop=True)
                            MM(bank[2 * c + 1][:, :], w1_sb[:, s, I + c * P:I + (c + 1) * P], z,
                               start=True, stop=True).then_inc(s_up, 1)

                        def down(k):
                            pe.wait_ge(s_inner, 2 + (at + k + 1) * 2)
                            pe.wait_ge(s_acc, at + k + 1)
                            for t in range(4):
                                for c in range(2):
                                    last = MM(bank[4 + k % 2][:, t * P:(t + 1) * P], inner[:, k % 2, c, t * P:(t + 1) * P],
                                              w2_sb[:, s, c, :], start=(c == 0), stop=(c == 1))
                            last.then_inc(s_yexp, 1)
                        for k in range(5):
                            if k < 4:
                                up(k, 0)
                            if k > 0:
                                down(k - 1)
                            if k < 4:
                                up(k, 1)

        @block.vector
        def _(dve):
            V = nc.vector
            TT, STT, TS = V.tensor_tensor, V.scalar_tensor_tensor, V.tensor_scalar
            dve.sem_inc(s_ksb, 2)
            dve.sem_inc(s_glu, 2)
            dve.sem_inc(s_hadd, 2)
            dve.sem_inc(s_inner, 2)
            dve.sem_inc(s_acc, 2)
            st = Steps(dve, s_dve)

            def turns(ang, cnt, after_count=None):
                st.done(TS(cnt, ang, 1.0 / TWO_PI, ROUND, ALU.mult, ALU.add))
                st.after()
                st.done(TS(cnt, cnt, ROUND, None, ALU.subtract))
                st.after()
                st.done(STT(ang, cnt, -TWO_PI_HI, ang, ALU.mult, ALU.add))
                st.after()
                st.done(STT(ang, cnt, -TWO_PI_LO, ang, ALU.mult, ALU.add))
                st.after()
                if after_count is not None:
                    dve.sem_inc(after_count, 1)
                return TS(ang, ang, PI, -PI, ALU.min, ALU.max)

            def over(v, n):
                return v.unsqueeze(2).to_broadcast([P, H, n])

            st.done(V.memset(d_row, 0.0))
            dve.wait_ge(s_exp1, 2)
            STT(sm[:, 1, :], sm[:, 2, :], -1.0, sm[:, 0, :], ALU.mult, ALU.mult).then_inc(s_small, 1)
            st.done(TT(sm[:, 9, :], par[:, 2, :], sm[:, 0, :], ALU.mult))
            st.after()
            st.done(V.tensor_copy(sm[:, 4, :], sm[:, 9, :]))
            dve.wait_ge(s_iota, 4)
            st.done(TT(p_ang, over(sm[:, 9, :], NA), iota[:, NB:NB + NA].unsqueeze(1).to_broadcast([P, H, NA]), ALU.mult))
            st.done(TT(q_ang, over(sm[:, 9, :], NB), iota[:, 0:NB].unsqueeze(1).to_broadcast([P, H, NB]), ALU.mult))
            st.after()
            turns(sm[:, 4, :], sm[:, 10, :]).then_inc(s_pcyc, 1)
            turns(p_ang, p_cnt).then_inc(s_pcyc, 1)
            turns(q_ang, q_cnt, s_qcyc).then_inc(s_qcyc, 1)
            dve.wait_ge(s_dskip, 16)
            st.after()
            V.tensor_copy(d_row[0:NL, :, 0:1], d_in[:, :].unsqueeze(2)).then_inc(s_dpad, 1)
            t, sin_y, sin_h, cos_y, e_re, e_im = (sm[:, k, :] for k in (3, 5, 6, 8, 12, 13))
            aim = par[:, 2, :]
            dve.wait_ge(s_exp1, 3)
            dve.wait_ge(s_e2, 3)
            st.done(TS(sm[:, 10, :], t, -1.0, 1.0, ALU.mult, ALU.add))
            st.after()
            st.done(V.reciprocal(sm[:, 10, :], sm[:, 10, :]))
            st.after()
            st.done(STT(sm[:, 11, :], t, 2.0, sm[:, 10, :], ALU.mult, ALU.mult))
            st.done(STT(sm[:, 14, :], sin_h, -2.0, sin_h, ALU.mult, ALU.mult))
            st.after()
            st.done(TT(e_re, sm[:, 11, :], cos_y, ALU.mult))
            st.done(STT(e_im, sm[:, 11, :], 1.0, sin_y, ALU.add, ALU.mult))
            st.after()
            st.done(TT(e_re, e_re, sm[:, 14, :], ALU.add))
            st.after()
            st.done(STT(sm[:, 14, :], e_re, -1.0, sm[:, 2, :], ALU.mult, ALU.mult))
            st.done(TT(sm[:, 15, :], e_im, aim, ALU.mult))
            st.done(STT(sm[:, 10, :], e_im, -1.0, sm[:, 2, :], ALU.mult, ALU.mult))
            st.done(TT(sm[:, 11, :], e_re, aim, ALU.mult))
            st.done(TT(sm[:, 7, :], sm[:, 2, :], sm[:, 2, :], ALU.mult))
            st.done(TT(sm[:, 4, :], aim, aim, ALU.mult))
            st.after()
            st.done(TT(sm[:, 14, :], sm[:, 14, :], sm[:, 15, :], ALU.add))
            st.done(TT(sm[:, 10, :], sm[:, 10, :], sm[:, 11, :], ALU.subtract))
            st.done(TT(sm[:, 7, :], sm[:, 7, :], sm[:, 4, :], ALU.add))
            st.after()
            st.done(V.reciprocal(sm[:, 7, :], sm[:, 7, :]))
            st.after()
            st.done(STT(sm[:, 14, :], sm[:, 14, :], 2.0, sm[:, 7, :], ALU.mult, ALU.mult))
            st.done(STT(sm[:, 10, :], sm[:, 10, :], 2.0, sm[:, 7, :], ALU.mult, ALU.mult))
            st.after()
            st.done(TT(sm[:, 11, :], par[:, 3, :], sm[:, 14, :], ALU.mult))
            st.done(TT(sm[:, 12, :], par[:, 4, :], sm[:, 10, :], ALU.mult))
            st.done(TT(sm[:, 13, :], par[:, 3, :], sm[:, 10, :], ALU.mult))
            st.done(TT(sm[:, 15, :], par[:, 4, :], sm[:, 14, :], ALU.mult))
            st.after()
            st.done(TT(sm[:, 11, :], sm[:, 11, :], sm[:, 12, :], ALU.subtract))
            st.done(TT(sm[:, 13, :], sm[:, 13, :], sm[:, 15, :], ALU.add))
            dve.wait_ge(s_pmag_done, 1)
            dve.wait_ge(s_ptrig, 2)
            st.done(TT(p_cnt, p_cnt, p_mag, ALU.mult))
            st.done(TT(p_sin, p_sin, p_mag, ALU.mult))
            st.after()
            c_r, c_i = over(sm[:, 11, :], NA), over(sm[:, 13, :], NA)
            st.done(TT(p_t1, c_r, p_cnt, ALU.mult))
            st.done(TT(p_t2, c_i, p_sin, ALU.mult))
            st.done(TT(p_ang, c_r, p_sin, ALU.mult))
            st.done(TT(p_mag, c_i, p_cnt, ALU.mult))
            st.after()
            st.done(TT(cp_re, p_t1, p_t2, ALU.subtract))
            TT(cp_im, p_ang, p_mag, ALU.add).then_inc(s_cp, 1)
            dve.wait_ge(s_qmag_done, 1)
            dve.wait_ge(s_qtrig, 2)
            st.done(TT(q_re, q_re, q_cnt, ALU.mult))
            TT(q_im, q_im, q_cnt, ALU.mult).then_inc(s_qready, 1)
            with dve.Fori(0, 4) as g2:
                for s in range(2):
                    dve.wait_ge(s_kps, 2 + g2 * 2 + s + 1)
                    V.tensor_copy(k_sb[:, bass.ds((g2 * 2 + s) * 16, 16), :],
                                  bank[s][0:NL * NA, :].rearrange("p (c b) -> p c b", b=NB)).then_inc(s_ksb, 1)

            def moments(sp, tiles, chunk_no):
                for k in range(CHUNK):
                    sp.done(V.bn_stats(stats[:, k, :], tiles(k)))
                sp.after()
                sp.done(TT(mean[:, :], stats[:, :, 1], stats[:, :, 4], ALU.add))
                sp.done(TT(diff[:, :], stats[:, :, 1], stats[:, :, 4], ALU.subtract))
                sp.done(TT(m2[:, :], stats[:, :, 2], stats[:, :, 5], ALU.add))
                sp.after()
                sp.done(TS(mean[:, :], mean[:, :], 0.5, None, ALU.mult))
                sp.done(STT(diff[:, :], diff[:, :], 0.25, diff[:, :], ALU.mult, ALU.mult))
                sp.done(TS(m2[:, :], m2[:, :], 1.0 / H, EPS, ALU.mult, ALU.add))
                sp.after()
                TT(var[:, :], m2[:, :], diff[:, :], ALU.add).then_inc(s_var, 1)
                dve.wait_ge(s_rstd, chunk_no + 1)

            def layer_norm_affine(sp, tiles, chunk, which, chunk_no, signal):
                moments(sp, tiles, chunk_no)
                w = lnw[:, which, :].rearrange("p a h -> p (a h)")
                b = lnb[:, which, :].rearrange("p a h -> p (a h)")
                for k in range(CHUNK):
                    sp.done(STT(ln_tmp[:, k, :], tiles(k), mean[:, k:k + 1], w, ALU.subtract, ALU.mult))
                sp.after()
                for k in range(CHUNK):
                    dst = z_conv[:, :, bass.ds(chunk * CHUNK + k, 1)].rearrange("p h a -> p (h a)")
                    last = STT(dst, ln_tmp[:, k, :], rstd[:, k:k + 1], b, ALU.mult, ALU.add)
                    if k < CHUNK - 1:
                        sp.done(last)
                last.then_inc(signal, 1)

            def row(buf, t):
                return buf[:, bass.ds(t, 1), :].rearrange("p a h -> p (a h)")

            dve.wait_ge(s_x, 16)
            dve.wait_ge(s_wts, 16 * 5)
            dve.wait_ge(s_sel, 7)
            dve.wait_ge(s_kps, 2 + 8)
            dve.wait_ge(s_kz, 16)
            START_STEPS = 2 * (16 + 6) + 16 + 31
            for c in range(CHUNKS):
                sp = Steps(dve, s_ln_dve, c * START_STEPS)
                tiles = lambda k: hres[:, c * CHUNK + k, :]
                moments(sp, tiles, c * 2)
                for k in range(CHUNK):
                    sp.done(TS(tiles(k), tiles(k), mean[:, k:k + 1], rstd[:, k:k + 1], ALU.subtract, ALU.mult))
                sp.after()
                layer_norm_affine(sp, tiles, c, slice(0, 1), c * 2 + 1, s_z)
                assert sp.n == START_STEPS, sp.n

            LAYER_STEPS = CHUNKS * (22 + 31)
            with dve.Fori(0, NL) as layer:
                sp = Steps(dve, s_lay_dve, layer * LAYER_STEPS)

                def glu(q):
                    dve.wait_ge(s_glu_in, (layer * QUADS + q + 1) * 2)
                    STT(g_out[:, q % 2, :], g_tanh[:, q % 2, :], 1.0, g_lin[:, q % 2, :],
                        ALU.add, ALU.mult).then_inc(s_glu, 1)

                def residual(q):
                    dve.wait_ge(s_back, layer * QUADS + q + 1)
                    h4 = hres[:, q * 4:(q + 1) * 4, :].rearrange("p t h -> p (t h)")
                    TT(h4, bank[6 + q % 2][:, :], h4, ALU.add).then_inc(s_hadd, 1)
                for q in range(QUADS + 1):
                    if q < QUADS:
                        glu(q)
                    if q > 0:
                        residual(q - 1)
                    if q > 0 and q % 4 == 0:
                        c = q // 4 - 1
                        dve.wait_ge(s_hadd, 2 + layer * QUADS + q)
                        layer_norm_affine(sp, lambda k: hres[:, c * CHUNK + k, :], c, bass.ds(layer + 1, 1),
                                          2 * CHUNKS + layer * CHUNKS + c, s_z)
                assert sp.n == LAYER_STEPS, sp.n

            dve.wait_ge(s_x2, 16)
            dve.wait_ge(s_z, (NL + 1) * CHUNKS)
            st.after()
            done = 2 * CHUNKS + NL * CHUNKS
            for c in range(CHUNKS):
                tiles = slice(c * CHUNK, (c + 1) * CHUNK)
                st.done(TT(hres[:, tiles, :], ybuf[:, tiles, :], z_conv[:, :, tiles].rearrange("p h t -> p t h"), ALU.add))
                st.after()
                moments(st, lambda k: hres[:, c * CHUNK + k, :], done + c)
                for k in range(CHUNK):
                    last = TS(ybuf[:, c * CHUNK + k, :], hres[:, c * CHUNK + k, :], mean[:, k:k + 1], rstd[:, k:k + 1],
                              ALU.subtract, ALU.mult)
                    if k < CHUNK - 1:
                        st.done(last)
                last.then_inc(s_z2, 1)
            dve.wait_ge(s_rt, 1)
            gates = bank[7][:, :].rearrange("p (t e) -> p t e", e=E)
            R = [route[:, k] for k in range(12)]
            one = [route[:, k, :, 0:1] for k in range(12)]

            def wide(v):
                return v.to_broadcast([P, TILES, E])
            ranks = rank[:, :].unsqueeze(1).to_broadcast([P, TILES, E])
            st.done(V.tensor_reduce(one[2], gates, AX.X, ALU.max))
            st.after()
            TT(R[0], gates, wide(one[2]), ALU.subtract).then_inc(s_rexp_in, 1)
            dve.wait_ge(s_rexp, 1)
            st.done(V.tensor_reduce(one[3], R[1], AX.X, ALU.add))
            st.after()
            st.done(V.reciprocal(one[4], one[3]))
            st.after()
            st.done(TT(R[5], R[1], wide(one[4]), ALU.mult))
            st.after()
            st.done(V.tensor_copy(R[6], R[5]))
            st.after()
            picks = []
            for hot in (10, 11):
                st.done(V.tensor_reduce(one[7], R[6], AX.X, ALU.max))
                st.after()
                st.done(TT(R[8], R[6], wide(one[7]), ALU.is_equal))
                st.after()
                st.done(TT(R[8], R[8], ranks, ALU.mult))
                st.after()
                st.done(V.tensor_reduce(one[9], R[8], AX.X, ALU.max))
                st.after()
                st.done(TT(R[hot], R[8], wide(one[9]), ALU.is_equal))
                st.after()
                st.done(STT(R[6], R[hot], -2.0, R[6], ALU.mult, ALU.add))
                st.after()
            st.done(TT(R[10], R[10], R[11], ALU.add))
            st.after()
            st.done(TT(R[10], R[10], R[5], ALU.mult))
            st.done(V.memset(ybuf[:, :, :], 0.0))
            st.after()
            with dve.Fori(0, E) as e:
                with dve.Fori(0, QUADS // 4) as qc:
                    at = (e * (QUADS // 4) + qc) * 4

                    def product(k, c):
                        dve.wait_ge(s_silu, (at + k) * 2 + c + 1)
                        TT(inner[:, k % 2, c, :], bank[2 * c + 1][:, :], gate_act[:, c, :], ALU.mult).then_inc(s_inner, 1)

                    def accumulate(k):
                        dve.wait_ge(s_yexp, at + k + 1)
                        dve.wait_ge(s_acc, at + k + 1)
                        for t in range(4):
                            tile = qc * 16 + k * 4 + t
                            acc = row(ybuf, tile)
                            ew = route[:, 10, bass.ds(tile, 1), bass.ds(e, 1)].rearrange("p a b -> p (a b)")
                            last = STT(acc, bank[4 + k % 2][:, t * P:(t + 1) * P], ew, acc, ALU.mult, ALU.add)
                        last.then_inc(s_acc, 1)
                    for k in range(5):
                        if k < 4:
                            product(k, 0)
                        if k > 0:
                            accumulate(k - 1)
                        if k < 4:
                            product(k, 1)
            dve.wait_ge(s_acc, 2 + E * QUADS)
            done += CHUNKS
            for c in range(CHUNKS):
                tiles = slice(c * CHUNK, (c + 1) * CHUNK)
                moments(st, lambda k: ybuf[:, c * CHUNK + k, :], done + c)
                for k in range(CHUNK):
                    t = c * CHUNK + k
                    st.done(TS(ybuf[:, t, :], ybuf[:, t, :], mean[:, k:k + 1], rstd[:, k:k + 1], ALU.subtract, ALU.mult))
                st.after()
                TT(z_tok[:, tiles, :], ybuf[:, tiles, :], hres[:, tiles, :], ALU.add).then_inc(s_res, 1)


_NAMES = ("x", "a_re_log", "a_im", "c_re", "c_im", "log_dt", "d_skip", "ln_w", "ln_b", "w_out", "b_out",
          "w1", "w2", "router")


def kernel(**inputs):
    import numpy as np
    import concourse.bacc as bacc
    from concourse.bass_utils import run_bass_kernel_spmd

    g = {k: np.asarray(v) for k, v in inputs.items()}
    x = g["L0_attn_x"].reshape(B, J, P, H)[:, :, ::-1, :].transpose(2, 1, 0, 3).reshape(P, TILES, H)
    modes = {k: g["L0_attn_" + k].transpose(0, 2, 1).reshape(NL * N, H) for k in ("A_re_log", "A_im", "C_re", "C_im")}
    laid = [x, modes["A_re_log"], modes["A_im"], modes["C_re"], modes["C_im"],
            g["L0_attn_log_dt"], g["L0_attn_D_skip"], g["L0_attn_ln_w"], g["L0_attn_ln_b"],
            g["L0_attn_W_out"].transpose(2, 0, 1), g["L0_attn_b_out"].reshape(NL, 2, H).transpose(2, 0, 1),
            g["L0_ffn_w1"].transpose(0, 2, 1), g["L0_ffn_w2"].reshape(E, H, 2, P).transpose(0, 3, 2, 1),
            g["L0_ffn_router_w"].T]
    nc = bacc.Bacc("TRN2", target_bir_lowering=False, num_devices=1)
    arrays, args = {}, []
    for name, a in zip(_NAMES, laid):
        a = np.ascontiguousarray(a)
        arrays[f"in_{name}"] = a
        args.append(nc.dram_tensor(f"in_{name}", a.shape, mybir.dt.from_np(a.dtype), kind="ExternalInput").ap())
    args.append(nc.dram_tensor("out_0", (P, TILES, H), F32, kind="ExternalOutput").ap())
    build(nc, *args)
    r = run_bass_kernel_spmd(nc, [arrays], core_ids=[0])
    o = np.asarray(r.results[0]["out_0"]).reshape(P, J, B, H).transpose(2, 1, 0, 3)[:, :, ::-1, :]
    return np.ascontiguousarray(o).reshape(B, L, H)
```

```python
import concourse.bass as bass
from concourse import mybir
from contextlib import ExitStack

P = 128
NL, H, N = 4, 128, 32
B, L = 16, 512
J = L // P
TILES = J * B
CHUNK = 16
CHUNKS = TILES // CHUNK
QUADS = TILES // 4
E, I = 8, 256
HALVES = 2
HTILES = TILES // HALVES
XP = 2 * P
XT = 2 * P * HTILES // XP + E
RING = 4
NA, NB = 16, 32
GROUP = 8
GROUPS = H // GROUP
SLOTS = 4
KPAD = 128
KROW = KPAD + L
EPS = 1e-5
F32 = mybir.dt.float32
F16 = mybir.dt.float16
BF16 = mybir.dt.bfloat16
I32 = mybir.dt.int32
U32 = mybir.dt.uint32
ALU = mybir.AluOpType
ACT = mybir.ActivationFunctionType
AX = mybir.AxisListType
TWO_PI = 6.283185307179586
TWO_PI_HI = 6.28125
TWO_PI_LO = TWO_PI - TWO_PI_HI
Z_SCALE = 1024.0
K_SCALE = 8192.0
W_SCALE = 256.0
I_SCALE = 16.0
ROUND = 12582912.0
PI = 3.1415925

FIRST_NORMS = [("x", 0), ("x", 1), ("h", 0), ("x", 2), ("h", 1), ("x", 3), ("h", 2), ("h", 3)]


class Steps:

    def __init__(self, eng, sem, base=0):
        self.eng, self.sem, self.base, self.n = eng, sem, base, 0

    def done(self, ins):
        ins.then_inc(self.sem, 1)
        self.n += 1

    def after(self):
        self.eng.wait_ge(self.sem, self.base + self.n)


def n_at(n):
    return n if isinstance(n, int) else XT // 2


def tile_steps(eng, step):
    def straight(n):
        step(n, n % RING, lambda o, d: (n + o) // d)
    for n in range(6):
        straight(n)
    with eng.Fori(0, (XT - 10) // RING) as i:
        for n in range(6, 6 + RING):
            step(i * RING + n, n % RING, lambda o, d, n=n: i * (RING // d) + (n + o) // d)
    for n in range(6 + (XT - 10) // RING * RING, XT + 2):
        straight(n)


def build(nc, x, a_re_log, a_im, c_re, c_im, log_dt, d_skip, ln_w, ln_b, w_out, b_out, b_rows, w1, w2, router, out):
    kd = nc.dram_tensor("kernels_dram", [NL, H, KROW, 2], F16)
    z_sorted = [nc.dram_tensor(f"z_sorted{h}", [XT * XP, 2 * H], F16) for h in range(HALVES)]
    y_sorted = [nc.dram_tensor(f"y_sorted{h}", [XT * XP, H], F32) for h in range(HALVES)]
    ctx = ExitStack()
    with ctx:
        def sb(name, shape):
            return ctx.enter_context(nc.sbuf_tensor(name, shape, F32))

        def sem(name):
            return ctx.enter_context(nc.semaphore(name))

        bank = [ctx.enter_context(nc.psum_tensor(f"bank{i}", [P, 512], F32)) for i in range(8)]

        hres = sb("hres", [P, TILES, H])
        zbuf = sb("zbuf", [P, TILES * H])
        ybuf = sb("ybuf", [P, TILES, H])
        toep = sb("toep", [P, SLOTS, GROUP, L])
        toep16 = toep[:, :, :, :].bitcast(F16).rearrange("p s g (l k) -> p s g l k", k=2)
        z_conv = zbuf[:, :].bitcast(F16).rearrange("p (h k t) -> p h k t", h=H, k=2)
        z_tok = zbuf[:, :].rearrange("p (t h) -> p t h", h=H)
        toep_flat = toep[:, :, :, :].rearrange("p s g l -> p (s g l)")

        ln_tmp = sb("ln_tmp", [P, CHUNK, H])
        stats = sb("stats", [P, CHUNK, 6])
        mean = sb("mean", [P, CHUNK])
        diff = sb("diff", [P, CHUNK])
        m2 = sb("m2", [P, CHUNK])
        var = sb("var", [P, CHUNK])
        rstd = sb("rstd", [P, CHUNK])
        mean_of, rstd_of, shift_of = (sb(name, [P, CHUNKS, CHUNK]) for name in ("mean_of", "rstd_of", "shift_of"))
        neg_half = sb("neg_half", [P, CHUNK])
        lnw = sb("lnw", [P, NL + 1, H])
        lnb = sb("lnb", [P, NL + 1, H])
        ident = sb("ident", [P, P])
        wo = sb("wo", [P, NL, 2 * H])
        wo_cur = sb("wo_cur", [P, 2 * H])
        bo = sb("bo", [P, NL, 2])
        bo_half = sb("bo_half", [P, NL, 2])
        bo_cur = sb("bo_cur", [P, 2])
        lnw_cur = sb("lnw_cur", [P, 1, H])
        bu_cur = sb("bu_cur", [1, H])
        same_layer = ln_tmp[:, 12, :]
        unscale = sb("unscale", [P, NL])
        unscale_cur = sb("unscale_cur", [P, 1])
        shift = sb("shift", [P, CHUNK])
        glu_work = sb("glu_work", [P, 4, 2, 512])
        g_act = glu_work[:, 0].rearrange("p s (t n) -> p s t n", t=4)
        g_tanh, g_out = glu_work[:, 1], glu_work[:, 2]
        ones = glu_work[0:1, 3, 0, :]
        b_row = glu_work[0:1, 3, 1, :].rearrange("p (l h) -> p l h", l=NL)
        half_pi = sb("half_pi", [P, 1])
        one_col = sb("one_col", [P, 1])

        par = ln_tmp[:, 4:12, :]
        sm = sb("sm", [P, 16, H])
        d_row = glu_work[:].rearrange("p a b n -> p (a b n)").rearrange("p (h b) -> p h b", h=H)
        d_sel = sb("d_sel", [P, NL, NA])
        iota = sb("iota", [P, NB + NA])
        def big(buf, at, n):
            return buf[:, at:at + H * n].rearrange("p (h n) -> p h n", h=H)
        q_re = big(zbuf, 0, NB)
        q_im = big(zbuf, H * NB, NB)
        ybuf_flat = ybuf[:, :, :].rearrange("p t h -> p (t h)")
        cp_re = big(ybuf_flat, 0, NA)
        cp_im = big(ybuf_flat, H * NA, NA)
        q_ang = big(ybuf_flat, 2 * H * NA, NB)
        q_cnt = big(toep_flat, 6 * H * NA, NB)
        p_ang = big(toep_flat, 0, NA)
        p_cnt = big(toep_flat, H * NA, NA)
        p_mag = big(toep_flat, 2 * H * NA, NA)
        p_sin = big(toep_flat, 3 * H * NA, NA)
        p_t1 = big(toep_flat, 4 * H * NA, NA)
        p_t2 = big(toep_flat, 5 * H * NA, NA)
        cp_blk = toep_flat[:, 6 * H * NA:8 * H * NA].rearrange("p (s k c l a) -> p s k c l a", s=2, k=2, c=16, l=NL)
        k_sb = q_ang[0:NL * NA].bitcast(F16).rearrange("p h (b k) -> p h b k", k=2)
        zeros = ln_tmp[:, 0:4, :]
        ln_bufs = [ln_tmp[:, :, :], sm[:, :, :]]

        router_sb = sb("router_sb", [P, E])
        at = [0]

        def part(n, *dims):
            piece = toep_flat[:, at[0]:at[0] + n]
            at[0] += n
            return piece
        w1_stage = glu_work[:].rearrange("p a b n -> p (a b n)").rearrange("p (e n) -> p e n", e=E)
        w2_stage = glu_work[:, 0:2].rearrange("p a b n -> p (a b n)").rearrange("p (e n) -> p e n", e=E)
        w1_16 = part(E * 2 * I).bitcast(F16).rearrange("p (k e n) -> p k e n", k=2, e=E)
        w2_16 = part(E * 2 * H).bitcast(F16).rearrange("p (e k n) -> p k e n", k=2, e=E)
        WE = 2 * I
        w1_row = toep_flat[:, 0:E * WE].bitcast(F16).rearrange("p (k m) -> p k m", k=2)
        w2_row = toep_flat[:, E * WE:E * WE + E * 2 * H].bitcast(F16)
        z_pair = [part(CHUNK * H)] + [ybuf[:, c * CHUNK:(c + 1) * CHUNK, :].rearrange("p t h -> p (t h)")
                                      for c in range(CHUNKS - 1)]
        z_pair = [z.bitcast(F16).rearrange("p (t k h) -> p t k h", k=2, h=H) for z in z_pair]
        ident16 = part(P // 2).bitcast(F16)
        route = part(12 * CHUNK * E).rearrange("p (k t e) -> p k t e", k=12, e=E)
        z2T = part(1024).rearrange("p (s n) -> p s n", s=2)
        x_tile = part(RING * 2 * H).bitcast(F16).rearrange("p (s t k h) -> p s t k h", s=RING, t=2, k=2)
        xT = part(2 * XP).bitcast(F16).rearrange("p (s n) -> p s n", s=2)
        y_tile = part(4 * 2 * H).rearrange("p (s n) -> p s n", s=4)
        tile_work = glu_work[:].rearrange("p a b n -> p (a b n)").rearrange("p (s n) -> p s n", n=I // P * XP)
        gate_act, inner = tile_work[:, 0:2], tile_work[:, 2:4]
        inner16 = tile_work[:, 4:8].bitcast(F16).rearrange("p s (k n) -> p s k n", k=2)
        slot = part(2 * TILES).bitcast(U32).rearrange("p (k t) -> p k t", k=2)
        weight = part(2 * TILES).rearrange("p (k t) -> p k t", k=2)
        slot_f = part(2 * HTILES).rearrange("p (k t) -> p k t", k=2)
        hot_of = part(2 * HTILES * E).rearrange("p (k t e) -> p k t e", k=2, e=E)
        place = part(HTILES * E).rearrange("p (t e) -> p t e", e=E)
        n_tiles, ends, base, work8 = (part(E) for _ in range(4))
        past = part(XT * E).rearrange("p (i e) -> p i e", e=E)
        owner_f = part(XT)
        owner = part(HALVES * XT).bitcast(I32).rearrange("p (c i) -> p c i", c=HALVES)
        mask = part(HTILES * E // 2).bitcast(BF16).rearrange("p (t e) -> p t e", e=E)
        below = part(P // 2).bitcast(BF16)
        all_ones = part(P // 2).bitcast(BF16)
        tile_no = part(XT)
        ones8 = part(E)
        rank = part(E)
        assert at[0] <= SLOTS * GROUP * L, at[0]
        y_of = [y.rearrange("p (k t h) -> p k t h", k=2, h=H) for y in (zbuf[:, :], ybuf_flat)]

        s_x, s_par, s_wts, s_dskip, s_scale = sem("x_loaded"), sem("par_loaded"), sem("weights_loaded"), sem("dskip_loaded"), sem("scale_rows_loaded")
        s_const, s_iota, s_sel = sem("const_ready"), sem("iota_ready"), sem("sel_ready")
        s_dve, s_ln_dve, s_lay_dve = sem("dve_steps"), sem("ln_steps"), sem("layer_dve_steps")
        s_act, s_wo, s_bo, s_bh = sem("act_steps"), sem("wo_ready"), sem("bo_ready"), sem("bo_halved")
        s_exp1, s_small, s_pmag, s_pcyc = sem("exp_small"), sem("small_ready"), sem("p_mag_in"), sem("p_cycles")
        s_e2 = sem("act_small_done")
        s_qmag_in, s_pmag_done, s_qmag_done = sem("q_mag_in"), sem("p_mag_done"), sem("q_mag_done")
        s_qk, s_qcyc, s_ptrig, s_qtrig = sem("q_count_used"), sem("q_cycles"), sem("p_trig"), sem("q_trig")
        s_cp, s_qready, s_dpad = sem("cp_ready"), sem("q_ready"), sem("dpad_ready")
        s_blk, s_kps, s_ksb = sem("blk_staged"), sem("kernel_psum"), sem("kernel_evacuated")
        s_blk0 = sem("blk_zeroed")
        s_same0, s_same, s_bound_in, s_bound, s_pw, s_pwT, s_unscale = (
            sem("same_layer_zeroed"), sem("same_layer_ready"), sem("bound_terms"), sem("bound_psum"),
            sem("unscale_rows"), sem("unscale_psum"), sem("unscale_ready"))
        s_norm_in, s_norm, s_wmul, s_zf, s_z1 = (sem("norm_in"), sem("normalized"), sem("weighted"),
                                                 sem("z_float"), sem("z_high"))
        s_ones = sem("ones_ready")
        s_brow = sem("b_rows_loaded")
        s_lnw_cur = sem("lnw_cur_ready")
        s_lnw, s_k1 = sem("ln_weights_scaled"), sem("kernel_high")
        s_kd, s_kz = sem("kernels_stored"), sem("pad_stored")
        s_var, s_rstd = sem("ln_var"), sem("ln_rstd")
        s_toep = [sem(f"toep_loaded{s}") for s in range(SLOTS)]
        s_z, s_conv, s_y = sem("z_ready"), sem("conv_done"), sem("y_ready")
        s_yT, s_gelu, s_w, s_glu_in = sem("yT_done"), sem("gelu_done"), sem("w_done"), sem("glu_in")
        s_glu, s_back, s_hadd = sem("glu_done"), sem("back_done"), sem("h_added")
        s_x2, s_z2, s_z2T, s_z2sb = sem("x_reloaded"), sem("z2_ready"), sem("z2T_psum"), sem("z2T_ready")
        s_logits, s_lread, s_rexp, s_mask = sem("logits"), sem("logits_read"), sem("router_exp"), sem("mask_ready")
        s_prefix, s_slots, s_mc = sem("prefix_psum"), sem("slots_ready"), sem("moe_const")
        s_fill, s_ew = sem("sorted_zeroed"), sem("expert_weights")
        s_scat = [sem(f"scattered{c}") for c in range(CHUNKS)]
        s_gath = [sem(f"gathered{c}") for c in range(CHUNKS)]
        s_xt = [sem(f"x_tile_loaded{k}") for k in range(RING)]
        s_id16, s_whi, s_wlo, s_zhi, s_zlo = sem("ident16_ready"), sem("weights_high"), sem("weights_low"), sem("z_pair_high"), sem("z_pair_low")
        s_yt = [sem(f"expert_y_stored{k}") for k in range(4)]
        s_xT, s_xTsb, s_hid, s_silu, s_inner = (sem("xT_psum"), sem("xT_ready"), sem("hidden_psum"),
                                                sem("silu_done"), sem("inner_ready"))
        s_ihi, s_ilo, s_yps, s_yout = (sem("inner_high"), sem("inner_low"), sem("expert_y_psum"), sem("expert_y_ready"))
        s_res, s_out = sem("result_ready"), sem("out_stored")

        block = ctx.enter_context(nc.Block())

        @block.sync
        def _(sp):
            sp.dma_start(par[:, 0, :], a_re_log).then_inc(s_par, 16)
            for layer in range(NL):
                sp.dma_start(par[layer * N:(layer + 1) * N, 1, :],
                             bass.AP(log_dt.tensor, layer * H, [[0, N], [1, H]])).then_inc(s_par, 16)
            sp.dma_start(par[:, 2, :], a_im).then_inc(s_par, 16)
            sp.dma_start(par[:, 3, :], c_re).then_inc(s_par, 16)
            sp.dma_start(par[:, 4, :], c_im).then_inc(s_par, 16)
            for k, row_of in ((5, ln_w), (6, ln_b), (7, d_skip)):
                for layer in range(NL):
                    sp.dma_start(par[layer * N:(layer + 1) * N, k, :],
                                 bass.AP(row_of.tensor, layer * H, [[0, N], [1, H]])).then_inc(s_scale, 16)
            sp.dma_start(hres[:, :, :], x).then_inc(s_x, 16)
            sp.dma_start(lnw[:, 0:NL, :], bass.AP(ln_w.tensor, 0, [[0, P], [H, NL], [1, H]])).then_inc(s_wts, 16)
            sp.dma_start(lnb[:, 0:NL, :], bass.AP(ln_b.tensor, 0, [[0, P], [H, NL], [1, H]])).then_inc(s_wts, 16)
            sp.dma_start(wo[:, :, :], w_out).then_inc(s_wts, 16)
            sp.dma_start(bo[:, :, :], b_out).then_inc(s_wts, 16)
            sp.dma_start(router_sb[:, :], router).then_inc(s_wts, 16)
            sp.wait_ge(s_const, 1)
            sp.dma_start(kd[:, :, 0:KPAD, :].rearrange("l h k i -> h l (k i)"),
                         zeros.bitcast(F16)).then_inc(s_kz, 16)
            for half in range(HALVES):
                sp.dma_start(z_sorted[half][:, :].rearrange("(p n k) h -> p n (k h)", p=P, k=4),
                             ln_tmp[:, 0:4, :].rearrange("p a h -> p (a h)").bitcast(F16).unsqueeze(1)
                             .to_broadcast([P, XT * XP // P // 4, 8 * H])).then_inc(s_fill, 16)
            sp.wait_ge(s_ksb, 2 + H // 16)
            sp.dma_start(b_row, b_rows[:, 0, :].rearrange("(o l) h -> o l h", o=1)).then_inc(s_brow, 16)
            for layer in range(NL):
                sp.dma_start(kd[layer, :, KPAD:KROW, :].rearrange("h (a b) k -> a h (b k)", b=NB),
                             k_sb[layer * NA:(layer + 1) * NA].rearrange("p h b k -> p h (b k)")).then_inc(s_kd, 16)
            sp.wait_ge(s_kd, 16 * NL)
            sp.wait_ge(s_kz, 16)
            with sp.Fori(0, NL) as layer:
                with sp.Fori(0, GROUPS // SLOTS) as g:
                    for s in range(SLOTS):
                        sp.wait_ge(s_conv, layer * GROUPS + g * SLOTS + s + 1)
                        first = KPAD - (P - 1)
                        src = bass.AP(kd, layer * (H * KROW * 2) + g * (SLOTS * GROUP * KROW * 2)
                                      + (s * GROUP * KROW + first) * 2, [[2, P], [KROW * 2, GROUP], [1, 2 * L]])
                        sp.dma_start(toep16[:, s].rearrange("p g l k -> p g (l k)"), src).then_inc(s_toep[s], 16)
            sp.wait_ge(s_yT, NL * TILES // 4)
            sp.dma_start(ybuf[:, :, :], x).then_inc(s_x2, 16)
            sp.wait_ge(s_back, NL * QUADS)
            sp.dma_start(w1_stage, w1).then_inc(s_ew, 16)
            sp.wait_ge(s_wlo, 1)
            sp.dma_start(w2_stage, w2.rearrange("p e c n -> p e (c n)")).then_inc(s_ew, 16)

            def rows(buf, n):
                return buf[bass.ds(n * XP, XP), :].rearrange("(p t) h -> p (t h)", t=2)

            def load(half, n, k, transposed):
                if transposed is not None:
                    sp.wait_ge(s_xT, transposed)
                sp.dma_start(x_tile[:, k].rearrange("p t k h -> p (t k h)"), rows(z_sorted[half], n)).then_inc(s_xt[k], 16)

            def store(half, n, k):
                sp.wait_ge(s_yout, n + (half * XT + 1))
                sp.dma_start(rows(y_sorted[half], n), y_tile[:, k, :]).then_inc(s_yt[k], 16)
            LAG = 3
            for half in range(HALVES):
                first = half * XT
                if half == 0:
                    for c in range(2):
                        sp.wait_ge(s_scat[c], 16 * 2 * CHUNK)
                    for k in range(RING):
                        load(0, k, k, None)
                for n in range(RING):
                    load(half, n + RING, n, first + n + 1)
                    if n >= LAG:
                        store(half, n - LAG, n - LAG)
                    elif half > 0:
                        store(half - 1, XT + n - LAG, (n - LAG) % RING)
                with sp.Fori(0, XT // RING - 2) as i:
                    for k in range(RING):
                        load(half, i * RING + (2 * RING + k), k, i * RING + (first + RING + k + 1))
                        store(half, i * RING + (RING + k - LAG), (k - LAG) % RING)
                for k in range(RING):
                    n = XT - RING + k
                    if half + 1 < HALVES:
                        if k == 0:
                            for c in (2, 3):
                                sp.wait_ge(s_scat[c], 16 * 2 * CHUNK)
                        load(half + 1, k, k, first + n + 1)
                    store(half, n - LAG, (k - LAG) % RING)
            for n in range(XT - LAG, XT):
                store(HALVES - 1, n, n % RING)
            for c in range(CHUNKS):
                sp.wait_ge(s_res, c + 1)
                sp.dma_start(out[:, c * CHUNK:(c + 1) * CHUNK, :], hres[:, c * CHUNK:(c + 1) * CHUNK, :]).then_inc(s_out, 16)
            sp.wait_ge(s_out, 16 * CHUNKS)

        @block.gpsimd
        def _(pool):
            nc.gpsimd.memset(ln_tmp[:, 0:4, :], 0.0).then_inc(s_const, 1)
            nc.gpsimd.iota(iota[:, 0:NB], pattern=[[1, NB]], base=0, channel_multiplier=0,
                           allow_small_or_imprecise_dtypes=True).then_inc(s_iota, 1)
            nc.gpsimd.iota(iota[:, NB:NB + NA], pattern=[[NB, NA]], base=0, channel_multiplier=0,
                           allow_small_or_imprecise_dtypes=True).then_inc(s_iota, 1)
            nc.gpsimd.memset(ident[:, :], 0.0).then_inc(s_sel, 1)
            nc.gpsimd.memset(d_sel[:, :, :], 0.0).then_inc(s_sel, 1)
            nc.gpsimd.memset(neg_half[:, :], -0.5).then_inc(s_sel, 1)
            nc.gpsimd.memset(half_pi[:, :], TWO_PI / 4).then_inc(s_iota, 1)
            nc.gpsimd.memset(lnw[:, NL, :], Z_SCALE).then_inc(s_sel, 1)
            nc.gpsimd.memset(same_layer, 0.0).then_inc(s_same0, 1)
            pool.wait_ge(s_same0, 1)
            for layer in range(NL):
                rows = slice(layer * N, (layer + 1) * N)
                nc.gpsimd.memset(same_layer[rows, rows], 1.0).then_inc(s_same, 1)
            pool.wait_ge(s_same, NL)
            nc.gpsimd.memset(lnb[:, NL, :], 0.0).then_inc(s_sel, 1)
            pool.wait_ge(s_sel, 5)
            nc.gpsimd.affine_select(out=ident[:, :], in_=ident[:, :], compare_op=ALU.not_equal, fill=1.0,
                                    base=0, pattern=[[-1, P]], channel_multiplier=1).then_inc(s_sel, 1)
            nc.gpsimd.affine_select(out=d_sel[:, :, 0:1], in_=d_sel[:, :, 0:1], compare_op=ALU.not_equal, fill=1.0,
                                    base=0, pattern=[[-N, NL], [0, 1]], channel_multiplier=1).then_inc(s_sel, 1)
            pool.wait_ge(s_small, 1)
            pool.wait_ge(s_iota, 2)
            nc.gpsimd.tensor_tensor(p_mag, sm[:, 1, :].unsqueeze(2).to_broadcast([P, H, NA]),
                                    iota[:, NB:NB + NA].unsqueeze(1).to_broadcast([P, H, NA]), ALU.mult).then_inc(s_pmag, 1)
            nc.gpsimd.tensor_tensor(q_re, sm[:, 1, :].unsqueeze(2).to_broadcast([P, H, NB]),
                                    iota[:, 0:NB].unsqueeze(1).to_broadcast([P, H, NB]), ALU.mult).then_inc(s_qmag_in, 1)
            def root(i, rstd=rstd[:, :]):
                pool.wait_ge(s_var, i + 1)
                nc.gpsimd.tensor_tensor(rstd, var[:, :], neg_half[:, :], ALU.pow).then_inc(s_rstd, 1)

            def weigh(i, w):
                pool.wait_ge(s_norm, (i + 1) * CHUNK)
                nc.gpsimd.tensor_tensor(ln_tmp[:, :, :], ln_tmp[:, :, :],
                                        w.to_broadcast([P, CHUNK, H]), ALU.mult).then_inc(s_wmul, 1)
            for i in range(2):
                root(i, rstd_of[:, FIRST_NORMS[i][1]])
            pool.wait_ge(s_qmag_done, 1)
            pool.wait_ge(s_qtrig, 2)
            nc.gpsimd.tensor_tensor(q_re, q_re, q_cnt, ALU.mult).then_inc(s_qready, 1)
            nc.gpsimd.tensor_tensor(q_im, q_im, q_cnt, ALU.mult).then_inc(s_qready, 1)
            pool.wait_ge(s_qready, 2)
            nc.gpsimd.memset(cp_blk, 0.0).then_inc(s_blk0, 1)
            for i in range(2, 2 * CHUNKS):
                root(i, rstd_of[:, FIRST_NORMS[i][1]])
            with pool.Fori(0, NL) as layer:
                for c in range(CHUNKS):
                    root(2 * CHUNKS + layer * CHUNKS + c)
                    if c == 0:
                        pool.wait_ge(s_lnw_cur, layer + 1)
                    weigh(CHUNKS + layer * CHUNKS + c, lnw_cur[:, :, :])
            pool.wait_ge(s_conv, SLOTS + NL * GROUPS)
            nc.gpsimd.iota(rank, pattern=[[-1, E]], base=E, channel_multiplier=0,
                           allow_small_or_imprecise_dtypes=True).then_inc(s_mc, 1)
            nc.gpsimd.iota(tile_no, pattern=[[1, XT]], base=0, channel_multiplier=0,
                           allow_small_or_imprecise_dtypes=True).then_inc(s_mc, 1)
            nc.gpsimd.memset(ones8, 1.0).then_inc(s_mc, 1)
            nc.gpsimd.memset(all_ones, 1.0).then_inc(s_mc, 1)
            pool.wait_ge(s_mc, 4)
            nc.gpsimd.affine_select(out=below, in_=all_ones, compare_op=ALU.is_gt, fill=0.0,
                                    base=0, pattern=[[1, P]], channel_multiplier=-1).then_inc(s_mc, 1)
            done = 2 * CHUNKS + NL * CHUNKS

            def scatter(c):
                pool.wait_ge(s_slots, c // 2 + 1)
                pool.wait_ge(s_zlo, c + 1)
                if c == 0:
                    pool.wait_ge(s_fill, 16 * HALVES)
                for k in range(2):
                    for t in range(c * CHUNK, (c + 1) * CHUNK):
                        nc.gpsimd.indirect_dma_start(
                            out=z_sorted[c // 2][:, :], out_offset=bass.IndirectOffsetOnAxis(ap=slot[:, k, t:t + 1], axis=0),
                            in_=z_pair[c][:, t - c * CHUNK, :, :].rearrange("p k h -> p (k h)"), in_offset=None).then_inc(s_scat[c], 16)

            def gather(c):
                for k in range(4):
                    pool.wait_ge(s_yt[k], 16 * (c // 2 + 1) * (XT // 4))
                for k in range(2):
                    for t in range(c * CHUNK, (c + 1) * CHUNK):
                        nc.gpsimd.indirect_dma_start(
                            out=y_of[c // 2][:, k, t % HTILES, :], out_offset=None, in_=y_sorted[c // 2][:, :],
                            in_offset=bass.IndirectOffsetOnAxis(ap=slot[:, k, t:t + 1], axis=0)
                        ).then_inc(s_gath[c], 16)
            for c in range(3):
                root(done + c, rstd_of[:, c])
            scatter(0)
            root(done + 3, rstd_of[:, 3])
            scatter(1)
            scatter(2)
            scatter(3)
            pool.wait_ge(s_z2, CHUNKS)
            gather(0)
            gather(1)
            for c in range(1, CHUNKS):
                pool.wait_ge(s_scat[c], 16 * 2 * CHUNK)
            gather(2)
            root(done + CHUNKS)
            root(done + CHUNKS + 1)
            gather(3)
            root(done + CHUNKS + 2)
            root(done + CHUNKS + 3)

        @block.scalar
        def _(act):
            A = nc.scalar.activation
            act.wait_ge(s_par, 16 * (4 + NL))
            A(sm[:, 0, :], par[:, 1, :], ACT.Exp).then_inc(s_exp1, 1)
            A(sm[:, 2, :], par[:, 0, :], ACT.Exp).then_inc(s_exp1, 1)
            act.wait_ge(s_small, 1)
            A(sm[:, 3, :], sm[:, 1, :], ACT.Tanh, scale=0.5).then_inc(s_exp1, 1)
            act.wait_ge(s_pmag, 1)
            A(p_mag, p_mag, ACT.Exp).then_inc(s_pmag_done, 1)
            act.wait_ge(s_qmag_in, 1)
            act.wait_ge(s_qcyc, 1)
            A(q_cnt, q_re, ACT.Exp).then_inc(s_qmag_done, 1)
            act.wait_ge(s_iota, 3)
            act.wait_ge(s_pcyc, 2)
            A(sm[:, 5, :], sm[:, 4, :], ACT.Sin).then_inc(s_e2, 1)
            A(sm[:, 6, :], sm[:, 4, :], ACT.Sin, scale=0.5).then_inc(s_e2, 1)
            A(sm[:, 7, :], sm[:, 4, :], ACT.Abs).then_inc(s_act, 1)
            A(p_sin, p_ang, ACT.Sin).then_inc(s_ptrig, 1)
            act.wait_ge(s_ptrig, 1)
            A(p_ang, p_ang, ACT.Abs).then_inc(s_act, 1)
            act.wait_ge(s_act, 2)
            A(sm[:, 8, :], sm[:, 7, :], ACT.Sin, bias=half_pi[:, 0:1], scale=-1.0).then_inc(s_e2, 1)
            A(p_cnt, p_ang, ACT.Sin, bias=half_pi[:, 0:1], scale=-1.0).then_inc(s_ptrig, 1)
            act.wait_ge(s_qcyc, 2)
            A(q_im, q_ang, ACT.Sin, scale=-1.0).then_inc(s_qtrig, 1)
            act.wait_ge(s_qtrig, 1)
            A(q_ang, q_ang, ACT.Abs).then_inc(s_act, 1)
            act.wait_ge(s_act, 3)
            act.wait_ge(s_qmag_done, 1)
            A(q_re, q_ang, ACT.Sin, bias=half_pi[:, 0:1], scale=-1.0).then_inc(s_qtrig, 1)
            act.wait_ge(s_cp, 1)
            act.wait_ge(s_blk0, 1)
            for g in range(H // 16):
                act.wait_ge(s_kps, g + 1)
                for layer in range(NL):
                    rows = slice(layer * N, (layer + 1) * N)
                    for k, src in ((0, cp_re), (1, cp_im)):
                        A(cp_blk[rows, g % 2, k, :, layer, :], src[rows, g * 16:(g + 1) * 16, :],
                          ACT.Copy).then_inc(s_blk, 1)
            act.wait_ge(s_wts, 16 * 5)
            A(bo_half[:, :, :], bo[:, :, :], ACT.Copy, scale=0.5).then_inc(s_bh, 1)
            act.wait_ge(s_bh, 1)
            act.wait_ge(s_pwT, 1)
            A(unscale[:, :], bank[3][:, 0:P:N], ACT.Copy).then_inc(s_unscale, 1)
            act.wait_ge(s_unscale, 1)

            def normalize(i, tiles):
                act.wait_ge(s_norm_in, i + 1)
                for k in range(CHUNK):
                    A(ln_tmp[:, k, :], tiles(k), ACT.Identity, scale=rstd[:, k:k + 1],
                      bias=shift[:, k:k + 1]).then_inc(s_norm, 1)

            def high_part(i, c, src=ln_tmp[:, :, :]):
                act.wait_ge(s_zf, i + 1)
                A(z_conv[:, :, 0, c * CHUNK:(c + 1) * CHUNK].rearrange("p h t -> p t h"), src,
                  ACT.Copy).then_inc(s_z1, 1)
            for c in range(CHUNKS + 1):
                if c < CHUNKS:
                    act.wait_ge(s_norm_in, c + 1)
                    if c >= 2:
                        act.wait_ge(s_z, c - 1)
                    for k in range(CHUNK):
                        A(ln_bufs[c % 2][:, k, :], hres[:, c * CHUNK + k, :], ACT.Identity, scale=rstd_of[:, c, k:k + 1],
                          bias=shift_of[:, c, k:k + 1]).then_inc(s_norm, 1)
                if c > 0:
                    high_part(c - 1, c - 1, ln_bufs[(c - 1) % 2])
            act.wait_ge(s_brow, 16)
            act.wait_ge(s_lnw, 2)
            with act.Fori(0, NL) as layer:
                for half, scale in ((0, 0.5), (1, 1.0)):
                    cols = slice(half * H, (half + 1) * H)
                    A(wo_cur[:, cols], wo[:, bass.ds(layer, 1), cols].rearrange("p a n -> p (a n)"), ACT.Copy,
                      scale=scale).then_inc(s_wo, 1)
                A(bu_cur[:, :], b_row[:, bass.ds(layer, 1), :].rearrange("p a n -> p (a n)"), ACT.Copy,
                  scale=0.5).then_inc(s_wo, 1)
                A(bo_cur[:, :], bo_half[:, bass.ds(layer, 1), :].rearrange("p a n -> p (a n)"), ACT.Copy).then_inc(s_bo, 1)
                A(unscale_cur[:, :], unscale[:, bass.ds(layer, 1)], ACT.Copy).then_inc(s_bo, 1)
                A(lnw_cur[:, :, :], lnw[:, bass.ds(layer + 1, 1), :], ACT.Copy).then_inc(s_lnw_cur, 1)
                act.wait_ge(s_bo, (layer + 1) * 2)

                def gelu(q):
                    act.wait_ge(s_yT, layer * QUADS + q + 1)
                    ap = bank[q % 2][:, :]
                    back = bass.AP(ap.tensor, ap.offset + P - 1, [list(ap.ap[0]), [P, 4], [-1, P]])
                    A(g_act[:, q % 2, :, :], back, ACT.Gelu_apprx_tanh, scale=unscale_cur[:, 0:1]).then_inc(s_gelu, 1)

                def tanh(q):
                    act.wait_ge(s_w, layer * QUADS + q + 1)
                    act.wait_ge(s_glu, layer * QUADS + q + 1)
                    A(g_tanh[:, q % 2, :], bank[4 + q % 2][:, :], ACT.Tanh, scale=0.5,
                      bias=bo_cur[:, 1:2]).then_inc(s_glu_in, 1)
                for q in range(QUADS + 6):
                    if q < QUADS:
                        gelu(q)
                    if 0 < q <= QUADS:
                        tanh(q - 1)
                    c, k = divmod(q - 7, 4)
                    if k == 0 and 0 <= c < CHUNKS:
                        normalize(CHUNKS + layer * CHUNKS + c, lambda k: hres[:, c * CHUNK + k, :])
                    c, k = divmod(q - 9, 4)
                    if k == 0 and 0 <= c < CHUNKS:
                        high_part(CHUNKS + layer * CHUNKS + c, c)
            A(ident16, ident[:, :], ACT.Copy).then_inc(s_id16, 1)
            for c in range(CHUNKS):
                if c >= 2:
                    act.wait_ge(s_ew, 16 * (c - 1))
                    pairs, stage = ((w1_16, w1_stage), (w2_16, w2_stage))[c - 2]
                    A(pairs[:, 0], stage, ACT.Copy, scale=W_SCALE).then_inc(s_whi, 1)
                for q in range(c * 4, c * 4 + 4):
                    act.wait_ge(s_z2T, q + 1)
                    A(z2T[:, q % 2, :], bank[q % 2][:, :], ACT.Copy).then_inc(s_z2sb, 1)
                act.wait_ge(s_z2, c + 1)
                if c > 0:
                    act.wait_ge(s_zlo, c)
                A(z_pair[c][:, :, 0, :], ybuf[:, c * CHUNK:(c + 1) * CHUNK, :], ACT.Copy, scale=Z_SCALE).then_inc(s_zhi, 1)
                act.wait_ge(s_lread, c + 1)
                A(route[:, 1], route[:, 0], ACT.Exp).then_inc(s_rexp, 1)

            def step(first, n, k, div):
                if n_at(n) < XT:
                    act.wait_ge(s_hid, n + (first + 1))
                    A(gate_act[:, k % 2, :], bank[2 + k % 2 * 2][:, :], ACT.Silu,
                      scale=1.0 / (Z_SCALE * W_SCALE)).then_inc(s_silu, 1)
                if n_at(n) >= 2:
                    m = (k - 2) % 4
                    act.wait_ge(s_yps, n + (first - 1))
                    rounds = div(-2, 4) + first // 4
                    if not (isinstance(rounds, int) and rounds < 1):
                        act.wait_ge(s_yt[m], rounds * 16)
                    A(y_tile[:, m, :], bank[6 + m % 2][:, 0:2 * H], ACT.Copy,
                      scale=1.0 / (I_SCALE * W_SCALE)).then_inc(s_yout, 1)
                if n_at(n) < XT:
                    act.wait_ge(s_inner, n + (first + 1))
                    A(inner16[:, k % 4, 0, :], inner[:, k % 2, :], ACT.Copy,
                      scale=I_SCALE / (Z_SCALE * W_SCALE)).then_inc(s_ihi, 1)
            for half in range(HALVES):
                tile_steps(act, lambda n, k, div: step(half * XT, n, k, div))

        @block.tensor
        def _(pe):
            MM = nc.tensor.matmul
            pe.wait_ge(s_same, NL)
            pe.wait_ge(s_bound_in, 1)
            MM(bank[2][:, 0:H], same_layer, sm[:, 0, :], start=True, stop=True).then_inc(s_bound, 1)
            pe.wait_ge(s_pw, 1)
            nc.tensor.transpose(bank[3][:, 0:P], sm[:, 0, :], ident[:, :]).then_inc(s_pwT, 1)
            pe.wait_ge(s_sel, 7)
            pe.sem_inc(s_kps, 2)
            pe.wait_ge(s_dpad, 1)
            pe.wait_ge(s_qready, 2)
            with pe.Fori(0, 4) as g2:
                for s in range(2):
                    pe.wait_ge(s_blk, (g2 * 2 + s + 1) * 2 * NL)
                    pe.wait_ge(s_ksb, g2 * 2 + s + 1)
                    MM(bank[s][0:NL * NA, :], d_sel[:, :, :].rearrange("p l a -> p (l a)"),
                       d_row[:, bass.ds((g2 * 2 + s) * 16, 16), :], start=True, stop=False)
                    for c in range(16):
                        for k, q in ((0, q_re), (1, q_im)):
                            last = MM(bank[s][0:NL * NA, c * NB:(c + 1) * NB],
                                      cp_blk[:, s, k, c, :, :].rearrange("p l a -> p (l a)"),
                                      q[:, bass.ds((g2 * 2 + s) * 16 + c, 1), :].rearrange("p a b -> p (a b)"),
                                      start=False, stop=(c == 15 and k == 1))
                    last.then_inc(s_kps, 1)
            pe.wait_ge(s_ones, 1)
            pe.sem_inc(s_conv, SLOTS)
            pe.wait_ge(s_wts, 16 * 5)
            with pe.Fori(0, NL) as layer:
                pe.wait_ge(s_z, (layer + 1) * CHUNKS)
                for g in range(GROUPS):
                    pe.wait_ge(s_toep[g % SLOTS], (layer * (GROUPS // SLOTS) + g // SLOTS + 1) * 16)
                    pe.wait_ge(s_y, layer * GROUPS + g + 1)
                    for c in range(GROUP):
                        dst = bank[(g % 2) * 2 + c // 4][:, :].rearrange("p (c k t) -> p c k t", c=4, k=2)[:, c % 4]
                        for d in range(J):
                            for k in range(2):
                                last = MM(dst[:, :, d * B:], toep16[:, g % SLOTS, c, d * P:(d + 1) * P, k],
                                          z_conv[:, g * GROUP + c, :, 0:TILES - d * B],
                                          start=(d == 0 and k == 0), stop=(d == J - 1 and k == 1))
                    last.then_inc(s_conv, 1)
                pe.wait_ge(s_y, 2 + (layer + 1) * GROUPS)
                pe.wait_ge(s_wo, 3 * (layer + 1))

                def forward(q):
                    for t in range(4):
                        last = nc.tensor.transpose(bank[q % 2][:, t * P:(t + 1) * P], ybuf[:, q * 4 + t, :], ident[:, :])
                    last.then_inc(s_yT, 1)

                def weights(q):
                    pe.wait_ge(s_gelu, layer * QUADS + q + 1)
                    pe.wait_ge(s_glu, layer * QUADS + q + 1)
                    g = g_act[:, q % 2, :, :].rearrange("p a t -> p (a t)")
                    MM(bank[4 + q % 2][:, :], wo_cur[:, H:2 * H], g, start=True, stop=True)
                    MM(bank[2 + q % 2][:, :], wo_cur[:, 0:H], g, start=True, stop=False)
                    MM(bank[2 + q % 2][:, :], bu_cur[:, :], ones[:, :], start=False, stop=True).then_inc(s_w, 1)

                def backward(q):
                    pe.wait_ge(s_glu, 2 + layer * QUADS + q + 1)
                    pe.wait_ge(s_hadd, layer * QUADS + q + 1)
                    for t in range(4):
                        last = nc.tensor.transpose(bank[6 + q % 2][:, t * P:(t + 1) * P],
                                                   g_out[:, q % 2, t * P:(t + 1) * P], ident[:, :])
                    last.then_inc(s_back, 1)
                forward(0)
                for q in range(QUADS + 2):
                    if q + 1 < QUADS:
                        forward(q + 1)
                    if q < QUADS:
                        weights(q)
                    if q >= 2:
                        backward(q - 2)
            pe.wait_ge(s_mc, 5)
            for c in range(CHUNKS):
                pe.wait_ge(s_z2, c + 1)
                for q in range(c * 4, c * 4 + 5):
                    if q < c * 4 + 4:
                        if q >= 2:
                            pe.wait_ge(s_z2sb, q - 1)
                        for t in range(4):
                            last = nc.tensor.transpose(bank[q % 2][:, t * P:(t + 1) * P], ybuf[:, q * 4 + t, :], ident[:, :])
                        last.then_inc(s_z2T, 1)
                    if q > c * 4:
                        pe.wait_ge(s_z2sb, q)
                        if q == c * 4 + 1 and c > 0:
                            pe.wait_ge(s_lread, c)
                        for t in range(4):
                            at_t = ((q - 1) % 4 * 4 + t) * E
                            last = MM(bank[6][:, at_t:at_t + E], z2T[:, (q - 1) % 2, t * P:(t + 1) * P], router_sb[:, :],
                                      start=True, stop=True)
                last.then_inc(s_logits, 1)
                if c % 2 == 0:
                    continue
                pe.wait_ge(s_mask, c + 1)
                if c > 1:
                    pe.wait_ge(s_slots, c // 2)
                MM(bank[7][:, 0:HTILES * E], below, mask.rearrange("p t e -> p (t e)"), start=True, stop=False)
                for t in range(HTILES - 1):
                    MM(bank[7][:, (t + 1) * E:HTILES * E].rearrange("p (t e) -> p t e", e=E), all_ones,
                       mask[:, t:t + 1, :].to_broadcast([P, HTILES - 1 - t, E]), start=False, stop=(t == HTILES - 2))
                for t in range(HTILES):
                    last = MM(bank[7][:, HTILES * E:HTILES * E + E], all_ones, mask[:, t, :],
                              start=(t == 0), stop=(t == HTILES - 1))
                last.then_inc(s_prefix, 1)
            pe.wait_ge(s_wlo, 2)
            pe.wait_ge(s_id16, 1)
            pe.wait_ge(s_slots, HALVES)
            PARTS = ((0, 0), (0, 1), (1, 0))

            def transpose_in(k, rounds):
                pe.wait_ge(s_xt[k], rounds * 16)
                for px in range(2):
                    for t in range(2):
                        last = MM(bank[k % 2][:, (px * 2 + t) * P:(px * 2 + t + 1) * P], x_tile[:, k, t, px, :],
                                  ident16, start=True, stop=True)
                last.then_inc(s_xT, 1)

            experts = {}

            def expert(half, k, n):
                experts[k] = pe.value_load(owner[0:1, half, bass.ds(n, 1)], min_val=0, max_val=(E - 1) * WE)

            def step(first, half, n, k, div):
                in_loop = not isinstance(n, int)
                if n_at(n) < XT - 1:
                    transpose_in((k + 1) % RING, div(1, RING) + (first // RING + 1))
                if n_at(n) < XT:
                    expert(half, k, n)
                    e = experts[k]
                    pe.wait_ge(s_xTsb, n + (first + 1))
                    if in_loop or first + n >= 2:
                        pe.wait_ge(s_inner, n + (first - 1))
                    for piece in range(2 * I // P):
                        out = bank[2 + k % 2 * 2 + piece // 2]
                        for i, (pw, px) in enumerate(PARTS):
                            last = MM(out[:, piece % 2 * XP:(piece % 2 + 1) * XP],
                                      w1_row[:, pw, bass.ds(e + piece * P, P)],
                                      xT[:, k % 2, px * XP:(px + 1) * XP], start=(i == 0), stop=(i == 2))
                    last.then_inc(s_hid, 1)
                if n_at(n) >= 2:
                    m = (k - 2) % RING
                    if in_loop and k in (2, 3) or n_at(n) in (6 + (XT - 10) // RING * RING, 7 + (XT - 10) // RING * RING):
                        expert(half, m, n - 2)
                    e = experts[m]
                    pe.wait_ge(s_ilo, n + (first - 1))
                    if in_loop or first + n >= 4:
                        pe.wait_ge(s_yout, n + (first - 3))
                    for t in range(2):
                        for piece in range(I // P):
                            for i, (px, pw) in enumerate(PARTS):
                                at_tok = piece * XP + t * P
                                last = MM(bank[6 + m % 2][:, t * H:(t + 1) * H], inner16[:, m, px, at_tok:at_tok + P],
                                          w2_row[:, bass.ds(e + (pw * 2 + piece) * H, H)],
                                          start=(piece == 0 and i == 0), stop=(piece == 1 and i == 2))
                    last.then_inc(s_yps, 1)
            for half in range(HALVES):
                transpose_in(0, half * XT // RING + 1)
                tile_steps(pe, lambda n, k, div: step(half * XT, half, n, k, div))

        @block.vector
        def _(dve):
            V = nc.vector
            TT, STT, TS = V.tensor_tensor, V.scalar_tensor_tensor, V.tensor_scalar
            dve.sem_inc(s_ksb, 2)
            dve.sem_inc(s_glu, 2)
            dve.sem_inc(s_hadd, 2)
            st = Steps(dve, s_dve)

            def turns(ang, cnt, after_count=None):
                st.done(TS(cnt, ang, 1.0 / TWO_PI, ROUND, ALU.mult, ALU.add))
                st.after()
                st.done(TS(cnt, cnt, ROUND, None, ALU.subtract))
                st.after()
                st.done(STT(ang, cnt, -TWO_PI_HI, ang, ALU.mult, ALU.add))
                st.after()
                st.done(STT(ang, cnt, -TWO_PI_LO, ang, ALU.mult, ALU.add))
                st.after()
                if after_count is not None:
                    dve.sem_inc(after_count, 1)
                return TS(ang, ang, PI, -PI, ALU.min, ALU.max)

            def over(v, n):
                return v.unsqueeze(2).to_broadcast([P, H, n])

            def moments(sp, tiles, mean=mean[:, :], roots=None):
                if tiles is not None:
                    for k in range(CHUNK):
                        sp.done(V.bn_stats(stats[:, k, :], tiles(k)))
                sp.after()
                sp.done(TT(mean, stats[:, :, 1], stats[:, :, 4], ALU.add))
                sp.done(TT(diff[:, :], stats[:, :, 1], stats[:, :, 4], ALU.subtract))
                sp.done(TT(m2[:, :], stats[:, :, 2], stats[:, :, 5], ALU.add))
                sp.after()
                sp.done(TS(mean, mean, 0.5, None, ALU.mult))
                sp.done(STT(diff[:, :], diff[:, :], 0.25, diff[:, :], ALU.mult, ALU.mult))
                sp.done(TS(m2[:, :], m2[:, :], 1.0 / H, EPS, ALU.mult, ALU.add))
                sp.after()
                if roots is not None:
                    dve.wait_ge(s_rstd, roots)
                TT(var[:, :], m2[:, :], diff[:, :], ALU.add).then_inc(s_var, 1)

            def first_norm(i):
                which, c = FIRST_NORMS[i]
                tile = lambda k: hres[:, c * CHUNK + k, :]
                if which == "h":
                    dve.wait_ge(s_rstd, FIRST_NORMS.index(("x", c)) + 1)
                    for k in range(CHUNK):
                        st.done(TS(tile(k), tile(k), mean_of[:, c, k:k + 1], rstd_of[:, c, k:k + 1], ALU.subtract, ALU.mult))
                    st.after()
                moments(st, tile, mean_of[:, c], i if i > 0 else None)

            st.done(V.memset(d_row, 0.0))
            dve.wait_ge(s_exp1, 2)
            STT(sm[:, 1, :], sm[:, 2, :], -1.0, sm[:, 0, :], ALU.mult, ALU.mult).then_inc(s_small, 1)
            st.done(TT(sm[:, 9, :], par[:, 2, :], sm[:, 0, :], ALU.mult))
            st.after()
            st.done(V.tensor_copy(sm[:, 4, :], sm[:, 9, :]))
            dve.wait_ge(s_iota, 3)
            st.done(TT(p_ang, over(sm[:, 9, :], NA), iota[:, NB:NB + NA].unsqueeze(1).to_broadcast([P, H, NA]), ALU.mult))
            st.done(TT(q_ang, over(sm[:, 9, :], NB), iota[:, 0:NB].unsqueeze(1).to_broadcast([P, H, NB]), ALU.mult))
            st.after()
            turns(sm[:, 4, :], sm[:, 10, :]).then_inc(s_pcyc, 1)
            turns(p_ang, p_cnt).then_inc(s_pcyc, 1)
            turns(q_ang, q_cnt, s_qcyc).then_inc(s_qcyc, 1)
            dve.wait_ge(s_x, 16)
            first_norm(0)
            first_norm(1)
            t, sin_y, sin_h, cos_y, e_re, e_im = (sm[:, k, :] for k in (3, 5, 6, 8, 12, 13))
            aim = par[:, 2, :]
            dve.wait_ge(s_exp1, 3)
            dve.wait_ge(s_e2, 3)
            st.done(TS(sm[:, 10, :], t, -1.0, 1.0, ALU.mult, ALU.add))
            st.after()
            st.done(V.reciprocal(sm[:, 10, :], sm[:, 10, :]))
            st.after()
            st.done(STT(sm[:, 11, :], t, 2.0, sm[:, 10, :], ALU.mult, ALU.mult))
            st.done(STT(sm[:, 14, :], sin_h, -2.0, sin_h, ALU.mult, ALU.mult))
            st.after()
            st.done(TT(e_re, sm[:, 11, :], cos_y, ALU.mult))
            st.done(STT(e_im, sm[:, 11, :], 1.0, sin_y, ALU.add, ALU.mult))
            st.after()
            st.done(TT(e_re, e_re, sm[:, 14, :], ALU.add))
            st.after()
            st.done(STT(sm[:, 14, :], e_re, -1.0, sm[:, 2, :], ALU.mult, ALU.mult))
            st.done(TT(sm[:, 15, :], e_im, aim, ALU.mult))
            st.done(STT(sm[:, 10, :], e_im, -1.0, sm[:, 2, :], ALU.mult, ALU.mult))
            st.done(TT(sm[:, 11, :], e_re, aim, ALU.mult))
            st.done(TT(sm[:, 7, :], sm[:, 2, :], sm[:, 2, :], ALU.mult))
            st.done(TT(sm[:, 4, :], aim, aim, ALU.mult))
            st.after()
            st.done(TT(sm[:, 14, :], sm[:, 14, :], sm[:, 15, :], ALU.add))
            st.done(TT(sm[:, 10, :], sm[:, 10, :], sm[:, 11, :], ALU.subtract))
            st.done(TT(sm[:, 7, :], sm[:, 7, :], sm[:, 4, :], ALU.add))
            st.after()
            st.done(V.reciprocal(sm[:, 7, :], sm[:, 7, :]))
            st.after()
            st.done(STT(sm[:, 14, :], sm[:, 14, :], 2.0, sm[:, 7, :], ALU.mult, ALU.mult))
            st.done(STT(sm[:, 10, :], sm[:, 10, :], 2.0, sm[:, 7, :], ALU.mult, ALU.mult))
            st.after()
            st.done(TT(sm[:, 11, :], par[:, 3, :], sm[:, 14, :], ALU.mult))
            st.done(TT(sm[:, 12, :], par[:, 4, :], sm[:, 10, :], ALU.mult))
            st.done(TT(sm[:, 13, :], par[:, 3, :], sm[:, 10, :], ALU.mult))
            st.done(TT(sm[:, 15, :], par[:, 4, :], sm[:, 14, :], ALU.mult))
            st.after()
            st.done(TT(sm[:, 11, :], sm[:, 11, :], sm[:, 12, :], ALU.subtract))
            st.done(TT(sm[:, 13, :], sm[:, 13, :], sm[:, 15, :], ALU.add))
            st.after()
            def magnitude(out, a):
                return TS(out.bitcast(U32), a.bitcast(U32), 0x7FFFFFFF, None, ALU.bitwise_and)

            def power(out, a):
                return TS(out.bitcast(U32), a.bitcast(U32), 0x7F800000, None, ALU.bitwise_and)
            dve.wait_ge(s_scale, 16 * 3 * NL)
            st.done(magnitude(sm[:, 14, :], sm[:, 11, :]))
            st.done(magnitude(sm[:, 15, :], sm[:, 13, :]))
            for k in (5, 6):
                st.done(magnitude(par[:, k, :], par[:, k, :]))
            st.done(magnitude(sm[:, 10, :], par[:, 7, :]))
            st.after()
            TT(sm[:, 0, :], sm[:, 14, :], sm[:, 15, :], ALU.add).then_inc(s_bound_in, 1)
            st.done(STT(par[:, 5, :], par[:, 5, :], 12.0, par[:, 6, :], ALU.mult, ALU.add))
            st.after()
            st.done(TS(par[:, 5, :], par[:, 5, :], 1e-30, None, ALU.max))
            st.after()
            st.done(power(par[:, 5, :], par[:, 5, :]))
            dve.wait_ge(s_bound, 1)
            st.done(TT(sm[:, 10, :], bank[2][:, 0:H], sm[:, 10, :], ALU.add))
            st.after()
            st.done(TS(sm[:, 10, :], sm[:, 10, :], 1e-30, None, ALU.max))
            st.after()
            st.done(power(sm[:, 10, :], sm[:, 10, :]))
            st.after()
            STT(sm[:, 0, :], sm[:, 10, :], 1.0 / (K_SCALE * Z_SCALE), par[:, 5, :], ALU.mult, ALU.mult).then_inc(s_pw, 1)
            st.done(V.reciprocal(sm[:, 14, :], sm[:, 10, :]))
            st.after()
            st.done(STT(sm[:, 11, :], sm[:, 14, :], K_SCALE, sm[:, 11, :], ALU.mult, ALU.mult))
            st.done(STT(sm[:, 13, :], sm[:, 14, :], K_SCALE, sm[:, 13, :], ALU.mult, ALU.mult))
            STT(d_row[:, :, 0:1], sm[:, 14, :].unsqueeze(2), K_SCALE, par[:, 7, :].unsqueeze(2),
                ALU.mult, ALU.mult).then_inc(s_dpad, 1)
            st.after()
            dve.wait_ge(s_pmag_done, 1)
            dve.wait_ge(s_ptrig, 2)
            st.done(TT(p_cnt, p_cnt, p_mag, ALU.mult))
            st.done(TT(p_sin, p_sin, p_mag, ALU.mult))
            st.after()
            c_r, c_i = over(sm[:, 11, :], NA), over(sm[:, 13, :], NA)
            st.done(TT(p_t1, c_r, p_cnt, ALU.mult))
            st.done(TT(p_t2, c_i, p_sin, ALU.mult))
            st.done(TT(p_ang, c_r, p_sin, ALU.mult))
            st.done(TT(p_mag, c_i, p_cnt, ALU.mult))
            st.after()
            st.done(TT(cp_re, p_t1, p_t2, ALU.subtract))
            TT(cp_im, p_ang, p_mag, ALU.add).then_inc(s_cp, 1)
            def prepare(sp, i, chunk_no):
                dve.wait_ge(s_rstd, chunk_no + 1)
                STT(shift[:, :], mean[:, :], -1.0, rstd[:, :], ALU.mult, ALU.mult).then_inc(s_norm_in, 1)

            def bias(i, which, buf=ln_tmp[:, :, :]):
                dve.wait_ge(s_wmul, i + 1)
                TT(buf, buf, lnb[:, which, :].to_broadcast([P, CHUNK, H]),
                   ALU.add).then_inc(s_zf, 1)

            def low_part(i, c, buf=ln_tmp[:, :, :]):
                dve.wait_ge(s_z1, i + 1)
                hi, lo = (z_conv[:, :, k, c * CHUNK:(c + 1) * CHUNK].rearrange("p h t -> p t h") for k in range(2))
                TT(lo, buf, hi, ALU.subtract).then_inc(s_z, 1)

            def row(buf, t):
                return buf[:, bass.ds(t, 1), :].rearrange("p a h -> p (a h)")

            dve.wait_ge(s_qtrig, 2)
            for g in range(H // 16):
                if g < 2 * CHUNKS - 2:
                    first_norm(2 + g)
                dve.wait_ge(s_kps, 2 + g + 1)
                k_ps = bank[g % 2][0:NL * NA, :].rearrange("p (c b) -> p c b", b=NB)
                part = [k_sb[:, g * 16:(g + 1) * 16, :, k] for k in range(2)]
                V.tensor_copy(part[0], k_ps).then_inc(s_k1, 1)
                dve.wait_ge(s_k1, g + 1)
                TT(part[1], k_ps, part[0], ALU.subtract).then_inc(s_ksb, 1)
            V.memset(ones, 1.0).then_inc(s_ones, 1)
            dve.wait_ge(s_kz, 16)
            dve.wait_ge(s_fill, 16 * HALVES)
            for c in range(2):
                dve.wait_ge(s_rstd, FIRST_NORMS.index(("h", c)) + 1)
            dve.wait_ge(s_rstd, 2 * CHUNKS)
            st.after()
            STT(shift_of[:, 0], mean_of[:, 0], -1.0, rstd_of[:, 0], ALU.mult, ALU.mult).then_inc(s_norm_in, 1)
            dve.wait_ge(s_wts, 16 * 5)
            dve.wait_ge(s_pwT, 1)
            st.done(magnitude(sm[:, 0:NL, :], lnw[:, 0:NL, :]))
            st.done(magnitude(sm[:, NL:2 * NL, :], lnb[:, 0:NL, :]))
            st.after()
            st.done(STT(sm[:, 0:NL, :], sm[:, 0:NL, :], 12.0, sm[:, NL:2 * NL, :], ALU.mult, ALU.add))
            st.after()
            st.done(TS(sm[:, 0:NL, :], sm[:, 0:NL, :], 1e-30, None, ALU.max))
            st.after()
            st.done(power(sm[:, 0:NL, :], sm[:, 0:NL, :]))
            st.after()
            st.done(V.reciprocal(sm[:, 0:NL, :], sm[:, 0:NL, :]))
            st.after()
            for row_of in (lnw, lnb):
                st.done(STT(row_of[:, 0:NL, :], row_of[:, 0:NL, :], Z_SCALE, sm[:, 0:NL, :], ALU.mult, ALU.mult))
            st.after()
            dve.sem_inc(s_lnw, 2)
            for c in range(1, CHUNKS):
                STT(shift_of[:, c], mean_of[:, c], -1.0, rstd_of[:, c], ALU.mult, ALU.mult).then_inc(s_norm_in, 1)
            for c in range(CHUNKS + 1):
                if c < CHUNKS:
                    buf = ln_bufs[c % 2]
                    dve.wait_ge(s_norm, (c + 1) * CHUNK)
                    TT(buf, buf, lnw[:, 0:1, :].to_broadcast([P, CHUNK, H]), ALU.mult).then_inc(s_wmul, 1)
                    bias(c, slice(0, 1), buf)
                if c > 0:
                    low_part(c - 1, c - 1, ln_bufs[(c - 1) % 2])

            LAYER_STEPS = CHUNKS * 22
            dve.sem_inc(s_y, 2)
            with dve.Fori(0, NL) as layer:
                sp = Steps(dve, s_lay_dve, layer * LAYER_STEPS)
                for g in range(GROUPS):
                    dve.wait_ge(s_conv, SLOTS + layer * GROUPS + g + 1)
                    for half in range(2):
                        src = bank[(g % 2) * 2 + half][:, :].rearrange("p (c k t) -> p c t k", c=4, k=2)
                        dst = ybuf[:, :, g * GROUP + half * 4:g * GROUP + half * 4 + 4].rearrange("p t c -> p c t")
                        last = V.tensor_reduce(dst, src, AX.X, ALU.add)
                    last.then_inc(s_y, 1)

                def glu(q):
                    dve.wait_ge(s_glu_in, layer * QUADS + q + 1)
                    STT(g_out[:, q % 2, :], g_tanh[:, q % 2, :], 1.0, bank[2 + q % 2][:, :],
                        ALU.add, ALU.mult).then_inc(s_glu, 1)

                def residual(q):
                    dve.wait_ge(s_back, layer * QUADS + q + 1)
                    h4 = hres[:, q * 4:(q + 1) * 4, :].rearrange("p t h -> p (t h)")
                    TT(h4, bank[6 + q % 2][:, :], h4, ALU.add).then_inc(s_hadd, 1)
                    dve.wait_ge(s_hadd, 2 + layer * QUADS + q + 1)
                    for k in range(4):
                        sp.done(V.bn_stats(stats[:, (q % 4) * 4 + k, :], hres[:, q * 4 + k, :]))
                for q in range(QUADS + 7):
                    c, k = divmod(q - 10, 4)
                    if k == 0 and 0 <= c < CHUNKS:
                        low_part(CHUNKS + layer * CHUNKS + c, c)
                    if 2 <= q < QUADS + 2:
                        residual(q - 2)
                        if q % 4 == 1:
                            moments(sp, None)
                    if q < QUADS:
                        glu(q)
                    c, k = divmod(q - 6, 4)
                    if k == 0 and 0 <= c < CHUNKS:
                        prepare(sp, CHUNKS + layer * CHUNKS + c, 2 * CHUNKS + layer * CHUNKS + c)
                    c, k = divmod(q - 8, 4)
                    if k == 0 and 0 <= c < CHUNKS:
                        bias(CHUNKS + layer * CHUNKS + c, bass.ds(layer + 1, 1))
                assert sp.n == LAYER_STEPS, sp.n

            dve.wait_ge(s_x2, 16)
            dve.wait_ge(s_z, (NL + 1) * CHUNKS)
            st.after()
            done = 2 * CHUNKS + NL * CHUNKS
            def residual_x(c):
                tiles = slice(c * CHUNK, (c + 1) * CHUNK)
                hi, lo = (z_conv[:, :, k, tiles].rearrange("p h t -> p t h") for k in range(2))
                st.done(TT(ln_tmp[:, :, :], hi, lo, ALU.add))
                st.after()
                st.done(STT(hres[:, tiles, :].rearrange("p t h -> p (t h)"), ln_tmp[:, :, :].rearrange("p t h -> p (t h)"),
                            1.0 / Z_SCALE, ybuf[:, tiles, :].rearrange("p t h -> p (t h)"), ALU.mult, ALU.add))
                st.after()
                moments(st, lambda k: hres[:, c * CHUNK + k, :], mean_of[:, c], done + c)

            def normal_x(c):
                dve.wait_ge(s_rstd, done + c + 1)
                for k in range(CHUNK):
                    last = TS(ybuf[:, c * CHUNK + k, :], hres[:, c * CHUNK + k, :], mean_of[:, c, k:k + 1], rstd_of[:, c, k:k + 1],
                              ALU.subtract, ALU.mult)
                    if k < CHUNK - 1:
                        st.done(last)
                last.then_inc(s_z2, 1)

            def choose(c):
                tiles = slice(c * CHUNK, (c + 1) * CHUNK)
                R = [route[:, k] for k in range(12)]
                one = [route[:, k, :, 0:1] for k in range(12)]

                def wide(v):
                    return v.to_broadcast([P, CHUNK, E])
                if c == 0:
                    dve.wait_ge(s_mc, 5)
                dve.wait_ge(s_logits, c + 1)
                gates = bank[6][:, 0:CHUNK * E].rearrange("p (t e) -> p t e", e=E)
                st.done(V.tensor_reduce(one[2], gates, AX.X, ALU.max))
                st.after()
                TT(R[0], gates, wide(one[2]), ALU.subtract).then_inc(s_lread, 1)
                dve.wait_ge(s_rexp, c + 1)
                st.done(V.tensor_reduce(one[3], R[1], AX.X, ALU.add))
                st.after()
                st.done(V.reciprocal(one[4], one[3]))
                st.after()
                st.done(TT(R[5], R[1], wide(one[4]), ALU.mult))
                st.after()
                left = R[5]
                half, in_half = c // 2, slice(c % 2 * CHUNK, (c % 2 + 1) * CHUNK)
                R[10], R[11] = hot_of[:, 0, in_half], hot_of[:, 1, in_half]
                if c == 2:
                    dve.wait_ge(s_prefix, 1)
                for hot in (10, 11):
                    st.done(V.tensor_reduce(one[7], left, AX.X, ALU.max))
                    st.after()
                    st.done(TT(R[8], left, wide(one[7]), ALU.is_equal))
                    st.after()
                    st.done(TT(R[8], R[8], rank.unsqueeze(1).to_broadcast([P, CHUNK, E]), ALU.mult))
                    st.after()
                    st.done(V.tensor_reduce(one[9], R[8], AX.X, ALU.max))
                    st.after()
                    st.done(TT(R[hot], R[8], wide(one[9]), ALU.is_equal))
                    st.after()
                    if hot == 10:
                        st.done(STT(R[6], R[hot], -2.0, R[5], ALU.mult, ALU.add))
                        st.after()
                        left = R[6]
                TT(mask[:, in_half], R[10], R[11], ALU.add).then_inc(s_mask, 1)
                dve.wait_ge(s_zhi, c + 1)
                STT(z_pair[c][:, :, 1, :], ybuf[:, tiles, :], Z_SCALE, z_pair[c][:, :, 0, :],
                    ALU.mult, ALU.subtract).then_inc(s_zlo, 1)
                for k in range(2):
                    st.done(TT(R[8 + k], R[10 + k], R[5], ALU.mult))
                st.after()
                for k in range(2):
                    st.done(V.tensor_reduce(weight[:, k, tiles].unsqueeze(2), R[8 + k], AX.X, ALU.add))

            def places(half):
                dve.wait_ge(s_prefix, half + 1)
                count = bank[7][:, HTILES * E:HTILES * E + E]
                st.done(TS(n_tiles, count, 1.0 / XP, (XP - 1.0) / XP - 0.5 + 0.5 / XP, ALU.mult, ALU.add))
                st.after()
                st.done(TS(n_tiles, n_tiles, ROUND, None, ALU.add))
                st.after()
                st.done(TS(n_tiles, n_tiles, ROUND, None, ALU.subtract))
                st.after()
                st.done(V.tensor_tensor_scan(ends, ones8, n_tiles, 0.0, ALU.mult, ALU.add))
                st.after()
                st.done(TT(base, ends, n_tiles, ALU.subtract))
                st.done(TT(past[0:1], tile_no[0:1].unsqueeze(2).to_broadcast([1, XT, E]),
                           ends[0:1].unsqueeze(1).to_broadcast([1, XT, E]), ALU.is_ge))
                st.after()
                st.done(TS(base, base, float(XP), None, ALU.mult))
                st.done(V.tensor_reduce(owner_f[0:1].unsqueeze(2), past[0:1], AX.X, ALU.add))
                st.after()
                st.done(TS(owner[0:1, half, :], owner_f[0:1], E - 1.0, float(WE), ALU.min, ALU.mult))
                ranks = bank[7][:, 0:HTILES * E].rearrange("p (t e) -> p t e", e=E)
                st.done(TT(place, ranks, base.unsqueeze(1).to_broadcast([P, HTILES, E]), ALU.add))
                st.after()
                for k in range(2):
                    st.done(TT(hot_of[:, k], hot_of[:, k], place, ALU.mult))
                st.after()
                for k in range(2):
                    st.done(V.tensor_reduce(slot_f[:, k, :].unsqueeze(2), hot_of[:, k], AX.X, ALU.add))
                st.after()
                V.tensor_copy(slot[:, :, half * HTILES:(half + 1) * HTILES], slot_f[:, :, :]).then_inc(s_slots, 1)

            def low_weights(k):
                dve.wait_ge(s_whi, k + 1)
                pairs, stage = ((w1_16, w1_stage), (w2_16, w2_stage))[k]
                STT(pairs[:, 1], stage, W_SCALE, pairs[:, 0], ALU.mult, ALU.subtract).then_inc(s_wlo, 1)

            residual_x(0)
            residual_x(1)
            normal_x(0)
            residual_x(2)
            normal_x(1)
            choose(0)
            choose(1)
            places(0)
            residual_x(3)
            normal_x(2)
            low_weights(0)
            choose(2)
            normal_x(3)
            low_weights(1)
            choose(3)
            places(1)

            def xT_copy(n, k):
                dve.wait_ge(s_xT, n + 1)
                if not (isinstance(n, int) and n < 2):
                    dve.wait_ge(s_hid, n - 1)
                V.tensor_copy(xT[:, k % 2, :], bank[k % 2][:, :]).then_inc(s_xTsb, 1)

            def step(first, n, k, div):
                if n_at(n) < XT - 1:
                    xT_copy(n + (first + 1), k + 1)
                if 1 <= n_at(n) < XT + 1:
                    dve.wait_ge(s_ihi, n + first)
                    STT(inner16[:, (k - 1) % 4, 1, :], inner[:, (k - 1) % 2, :], I_SCALE / (Z_SCALE * W_SCALE),
                        inner16[:, (k - 1) % 4, 0, :], ALU.mult, ALU.subtract).then_inc(s_ilo, 1)
                if n_at(n) < XT:
                    dve.wait_ge(s_silu, n + (first + 1))
                    if not (isinstance(n, int) and first + n < 2):
                        dve.wait_ge(s_ilo, n + (first - 1))
                    TT(inner[:, k % 2, :], bank[3 + k % 2 * 2][:, :], gate_act[:, k % 2, :], ALU.mult).then_inc(s_inner, 1)
            for half in range(HALVES):
                xT_copy(half * XT, 0)
                tile_steps(dve, lambda n, k, div: step(half * XT, n, k, div))
            for c in range(CHUNKS):
                dve.wait_ge(s_gath[c], 16 * 2 * CHUNK)
                at_c = slice(c % 2 * CHUNK, (c % 2 + 1) * CHUNK)
                y1, y2 = y_of[c // 2][:, 0, at_c], y_of[c // 2][:, 1, at_c]
                w = [weight[:, k, c * CHUNK:(c + 1) * CHUNK].unsqueeze(2).to_broadcast([P, CHUNK, H]) for k in range(2)]
                st.done(TT(y1, y1, w[0], ALU.mult))
                st.done(TT(y2, y2, w[1], ALU.mult))
                st.after()
                st.done(TT(y1, y1, y2, ALU.add))
                st.after()
                moments(st, lambda k: y1[:, k, :])
                dve.wait_ge(s_rstd, done + CHUNKS + c + 1)
                wide_mean, wide_rstd = (v[:, :].unsqueeze(2).to_broadcast([P, CHUNK, H]) for v in (mean, rstd))
                st.done(TT(y1, y1, wide_mean, ALU.subtract))
                st.after()
                st.done(TT(y1, y1, wide_rstd, ALU.mult))
                st.after()
                tiles = slice(c * CHUNK, (c + 1) * CHUNK)
                TT(hres[:, tiles, :], y1, hres[:, tiles, :], ALU.add).then_inc(s_res, 1)


_NAMES = ("x", "a_re_log", "a_im", "c_re", "c_im", "log_dt", "d_skip", "ln_w", "ln_b", "w_out", "b_out", "b_rows",
          "w1", "w2", "router")


def kernel(**inputs):
    import numpy as np
    import concourse.bacc as bacc
    from concourse.bass_utils import run_bass_kernel_spmd

    g = {k: np.asarray(v) for k, v in inputs.items()}
    x = g["L0_attn_x"].reshape(B, J, P, H)[:, :, ::-1, :].transpose(2, 1, 0, 3).reshape(P, TILES, H)
    modes = {k: g["L0_attn_" + k].transpose(0, 2, 1).reshape(NL * N, H) for k in ("A_re_log", "A_im", "C_re", "C_im")}
    laid = [x, modes["A_re_log"], modes["A_im"], modes["C_re"], modes["C_im"],
            g["L0_attn_log_dt"], g["L0_attn_D_skip"], g["L0_attn_ln_w"], g["L0_attn_ln_b"],
            g["L0_attn_W_out"].transpose(2, 0, 1), g["L0_attn_b_out"].reshape(NL, 2, H).transpose(2, 0, 1),
            g["L0_attn_b_out"].reshape(NL, 2, H), g["L0_ffn_w1"].transpose(2, 0, 1),
            g["L0_ffn_w2"].reshape(E, H, 2, P).transpose(3, 0, 2, 1),
            g["L0_ffn_router_w"].T]
    nc = bacc.Bacc("TRN2", target_bir_lowering=False, num_devices=1)
    arrays, args = {}, []
    for name, a in zip(_NAMES, laid):
        a = np.ascontiguousarray(a)
        arrays[f"in_{name}"] = a
        args.append(nc.dram_tensor(f"in_{name}", a.shape, mybir.dt.from_np(a.dtype), kind="ExternalInput").ap())
    args.append(nc.dram_tensor("out_0", (P, TILES, H), F32, kind="ExternalOutput").ap())
    build(nc, *args)
    r = run_bass_kernel_spmd(nc, [arrays], core_ids=[0])
    o = np.asarray(r.results[0]["out_0"]).reshape(P, J, B, H).transpose(2, 1, 0, 3)[:, :, ::-1, :]
    return np.ascontiguousarray(o).reshape(B, L, H)
```

```python
import concourse.bass as bass
from concourse import mybir
from contextlib import ExitStack

P = 128
NL, H, N = 4, 128, 32
B, L = 16, 512
J = L // P
TILES = J * B
CHUNK = 16
CHUNKS = TILES // CHUNK
PART = 8
NORMS = TILES // PART
QUADS = TILES // 4
E, I = 8, 256
SEGMENTS = (range(0, 1), range(1, 3), range(3, 4))
SEGS = len(SEGMENTS)
SEG_OF = [g for g, chunks in enumerate(SEGMENTS) for _ in chunks]
SEG_TILES = [len(chunks) * CHUNK for chunks in SEGMENTS]
MOST = max(SEG_TILES)
XP = 2 * P
XTS = [2 * P * tiles // XP + E for tiles in SEG_TILES]
FIRSTS = [sum(XTS[:g]) for g in range(SEGS)]
MOST_X = max(XTS)
UNROLL = 8
RING = 4
NA, NB = 16, 32
GROUP = 4
GROUPS = H // GROUP
SLOTS = 8
KPAD = 128
KROW = KPAD + L
EPS = 1e-5
F32 = mybir.dt.float32
F16 = mybir.dt.float16
BF16 = mybir.dt.bfloat16
I32 = mybir.dt.int32
U32 = mybir.dt.uint32
ALU = mybir.AluOpType
ACT = mybir.ActivationFunctionType
AX = mybir.AxisListType
TWO_PI = 6.283185307179586
TWO_PI_HI = 6.28125
TWO_PI_LO = TWO_PI - TWO_PI_HI
Z_SCALE = 1024.0
K_SCALE = 8192.0
W_SCALE = 256.0
I_SCALE = 16.0
ROUND = 12582912.0
PI = 3.1415925

FIRST_NORMS = [(which, c) for which in "xh" for c in range(TILES // CHUNK)]


class Steps:

    def __init__(self, eng, sem, base=0):
        self.eng, self.sem, self.base, self.n = eng, sem, base, 0

    def done(self, ins):
        ins.then_inc(self.sem, 1)
        self.n += 1

    def after(self):
        self.eng.wait_ge(self.sem, self.base + self.n)


def n_at(n):
    return n if isinstance(n, int) else min(XTS) // 2


def tile_steps(eng, xt, step):
    def straight(n, new_turn=False):
        step(n, n % RING, lambda o, d: (n + o) // d, new_turn)
    turns = (xt - 1 - 6) // UNROLL
    for n in range(6):
        straight(n)
    with eng.Fori(0, turns) as i:
        for n in range(6, 6 + UNROLL):
            step(i * UNROLL + n, n % RING, lambda o, d, n=n: i * (UNROLL // d) + (n + o) // d, n < 8)
    for n in range(6 + turns * UNROLL, xt + 2):
        straight(n, n < 8 + turns * UNROLL)


def build(nc, x, a_re_log, a_im, c_re, c_im, log_dt, d_skip, ln_w, ln_b, w_out, b_out, b_rows, w1, w2, router, out):
    kd = nc.dram_tensor("kernels_dram", [NL, H, KROW, 2], F16)
    z_sorted = [nc.dram_tensor(f"z_sorted{g}", [XTS[g] * XP, 2 * H], F16) for g in range(SEGS)]
    y_sorted = [nc.dram_tensor(f"y_sorted{g}", [XTS[g] * XP, H], F32) for g in range(SEGS)]
    ctx = ExitStack()
    with ctx:
        def sb(name, shape):
            return ctx.enter_context(nc.sbuf_tensor(name, shape, F32))

        def sem(name):
            return ctx.enter_context(nc.semaphore(name))

        bank = [ctx.enter_context(nc.psum_tensor(f"bank{i}", [P, 512], F32)) for i in range(8)]

        hres = sb("hres", [P, TILES, H])
        zbuf = sb("zbuf", [P, TILES * H])
        ybuf = sb("ybuf", [P, TILES, H])
        toep = sb("toep", [P, SLOTS, GROUP, L])
        toep16 = toep[:, :, :, :].bitcast(F16).rearrange("p s g (l k) -> p s g l k", k=2)
        z_conv = zbuf[:, :].bitcast(F16).rearrange("p (h k t) -> p h k t", h=H, k=2)
        z_tok = zbuf[:, :].rearrange("p (t h) -> p t h", h=H)
        toep_flat = toep[:, :, :, :].rearrange("p s g l -> p (s g l)")

        ln_tmp = sb("ln_tmp", [P, CHUNK, H])
        stats = sb("stats", [P, CHUNK, 6])
        mean = sb("mean", [P, CHUNK])
        diff = sb("diff", [P, CHUNK])
        m2 = sb("m2", [P, CHUNK])
        var = sb("var", [P, CHUNK])
        rstd = sb("rstd", [P, CHUNK])
        mean_of, rstd_of, shift_of = (sb(name, [P, CHUNKS, CHUNK]) for name in ("mean_of", "rstd_of", "shift_of"))
        neg_half = sb("neg_half", [P, CHUNK])
        lnw = sb("lnw", [P, NL + 1, H])
        lnb = sb("lnb", [P, NL + 1, H])
        ident = sb("ident", [P, P])
        wo = sb("wo", [P, NL, 2 * H])
        wo_cur = sb("wo_cur", [P, 2 * H])
        bo = sb("bo", [P, NL, 2])
        bo_half = sb("bo_half", [P, NL, 2])
        bo_cur = sb("bo_cur", [P, 2])
        lnw_cur = sb("lnw_cur", [P, 1, H])
        bu_cur = sb("bu_cur", [1, H])
        same_layer = ln_tmp[:, 12, :]
        unscale = sb("unscale", [P, NL])
        unscale_cur = sb("unscale_cur", [P, 1])
        glu_work = sb("glu_work", [P, 4, 2, 512])
        g_act = glu_work[:, 0].rearrange("p s (t n) -> p s t n", t=4)
        g_tanh, g_out = glu_work[:, 1], glu_work[:, 2]
        ones = glu_work[0:1, 3, 0, :]
        b_row = glu_work[0:1, 3, 1, :].rearrange("p (l h) -> p l h", l=NL)
        half_pi = sb("half_pi", [P, 1])

        def shift_part(p):
            return shift_of[:, p // 2, p % 2 * PART:(p % 2 + 1) * PART]

        def mean_part(p):
            return mean_of[:, p // 2, p % 2 * PART:(p % 2 + 1) * PART]

        def rstd_part(p):
            return rstd_of[:, p // 2, p % 2 * PART:(p % 2 + 1) * PART]

        def var_part(p):
            return var[:, p % 2 * PART:(p % 2 + 1) * PART]
        NORM_TILES = TILES - PART // 2

        par = ln_tmp[:, 4:12, :]
        sm = sb("sm", [P, 16, H])
        d_row = glu_work[:].rearrange("p a b n -> p (a b n)").rearrange("p (h b) -> p h b", h=H)
        d_sel = sb("d_sel", [P, NL, NA])
        iota = sb("iota", [P, NB + NA])
        def big(buf, at, n):
            return buf[:, at:at + H * n].rearrange("p (h n) -> p h n", h=H)
        q_re = big(zbuf, 0, NB)
        q_im = big(zbuf, H * NB, NB)
        ybuf_flat = ybuf[:, :, :].rearrange("p t h -> p (t h)")
        cp_re = big(ybuf_flat, 0, NA)
        cp_im = big(ybuf_flat, H * NA, NA)
        q_ang = big(ybuf_flat, 2 * H * NA, NB)
        q_cnt = big(toep_flat, 6 * H * NA, NB)
        p_ang = big(toep_flat, 0, NA)
        p_cnt = big(toep_flat, H * NA, NA)
        p_mag = big(toep_flat, 2 * H * NA, NA)
        p_sin = big(toep_flat, 3 * H * NA, NA)
        p_t1 = big(toep_flat, 4 * H * NA, NA)
        p_t2 = big(toep_flat, 5 * H * NA, NA)
        cp_blk = toep_flat[:, 6 * H * NA:8 * H * NA].rearrange("p (s k c l a) -> p s k c l a", s=2, k=2, c=16, l=NL)
        k_sb = q_ang[0:NL * NA].bitcast(F16).rearrange("p h (b k) -> p h b k", k=2)
        zeros = ln_tmp[:, 0:4, :]
        norm_bufs = [ln_tmp[:, 0:PART, :], ln_tmp[:, PART:CHUNK, :], sm[:, 0:PART, :], sm[:, PART:CHUNK, :]]

        router_sb = sb("router_sb", [P, E])
        at = [0]

        def part(n, *dims):
            piece = toep_flat[:, at[0]:at[0] + n]
            at[0] += n
            return piece
        w1_stage = glu_work[:].rearrange("p a b n -> p (a b n)").rearrange("p (e n) -> p e n", e=E)
        w2_stage = glu_work[:, 0:2].rearrange("p a b n -> p (a b n)").rearrange("p (e n) -> p e n", e=E)
        w1_16 = part(E * 2 * I).bitcast(F16).rearrange("p (k e n) -> p k e n", k=2, e=E)
        w2_16 = part(E * 2 * H).bitcast(F16).rearrange("p (e k n) -> p k e n", k=2, e=E)
        WE = 2 * I
        w1_row = toep_flat[:, 0:E * WE].bitcast(F16).rearrange("p (k m) -> p k m", k=2)
        w2_row = toep_flat[:, E * WE:E * WE + E * 2 * H].bitcast(F16)
        z_pair = [part(CHUNK * H)] + [ybuf[:, c * CHUNK:(c + 1) * CHUNK, :].rearrange("p t h -> p (t h)")
                                      for c in range(CHUNKS - 1)]
        z_pair = [z.bitcast(F16).rearrange("p (t k h) -> p t k h", k=2, h=H) for z in z_pair]
        ident16 = part(P // 2).bitcast(F16)
        route = part(12 * CHUNK * E).rearrange("p (k t e) -> p k t e", k=12, e=E)
        z2T = part(1024).rearrange("p (s n) -> p s n", s=2)
        x_tile = part(RING * 2 * H).bitcast(F16).rearrange("p (s t k h) -> p s t k h", s=RING, t=2, k=2)
        xT = part(2 * XP).bitcast(F16).rearrange("p (s n) -> p s n", s=2)
        y_tile = part(4 * 2 * H).rearrange("p (s n) -> p s n", s=4)
        tile_work = glu_work[:].rearrange("p a b n -> p (a b n)").rearrange("p (s n) -> p s n", n=I // P * XP)
        gate_act, inner = tile_work[:, 0:2], tile_work[:, 2:4]
        inner16 = tile_work[:, 4:8].bitcast(F16).rearrange("p s (k n) -> p s k n", k=2)
        slot = part(2 * TILES).bitcast(U32).rearrange("p (k t) -> p k t", k=2)
        weight = part(2 * TILES).rearrange("p (k t) -> p k t", k=2)
        slot_f = part(2 * MOST).rearrange("p (k t) -> p k t", k=2)
        hot_of = part(2 * MOST * E).rearrange("p (k t e) -> p k t e", k=2, e=E)
        place = part(MOST * E).rearrange("p (t e) -> p t e", e=E)
        n_tiles, ends, base = (part(E) for _ in range(3))
        past = part(MOST_X * E).rearrange("p (i e) -> p i e", e=E)
        owner_f = part(MOST_X)
        owner = part(SEGS * MOST_X).bitcast(I32).rearrange("p (c i) -> p c i", c=SEGS)
        mask = part(MOST * E // 2).bitcast(BF16).rearrange("p (t e) -> p t e", e=E)
        below = part(P // 2).bitcast(BF16)
        all_ones = part(P // 2).bitcast(BF16)
        tile_no = part(MOST_X)
        ones8 = part(E)
        rank = part(E)
        assert at[0] <= SLOTS * GROUP * L, at[0]

        def y_of(k, t, n=1):
            g = SEG_OF[t // CHUNK]
            if g == 0:
                buf, at_t = z_tok, k * CHUNK + t
            elif g == 1:
                buf, at_t = (z_tok, 2 * CHUNK + t - CHUNK) if k == 0 else (ybuf, t - CHUNK)
            else:
                buf, at_t = ybuf, 2 * CHUNK + k * CHUNK + t - 3 * CHUNK
            return buf[:, at_t:at_t + n, :]

        s_x, s_par, s_wts, s_scale = sem("x_loaded"), sem("par_loaded"), sem("weights_loaded"), sem("scale_rows_loaded")
        s_const, s_iota, s_sel = sem("const_ready"), sem("iota_ready"), sem("sel_ready")
        s_dve, s_lay_dve = sem("dve_steps"), sem("layer_dve_steps")
        s_act, s_wo, s_bo, s_bh = sem("act_steps"), sem("wo_ready"), sem("bo_ready"), sem("bo_halved")
        s_exp1, s_small, s_pmag, s_pcyc = sem("exp_small"), sem("small_ready"), sem("p_mag_in"), sem("p_cycles")
        s_e2 = sem("act_small_done")
        s_qmag_in, s_pmag_done, s_qmag_done = sem("q_mag_in"), sem("p_mag_done"), sem("q_mag_done")
        s_qcyc, s_ptrig, s_qtrig = sem("q_cycles"), sem("p_trig"), sem("q_trig")
        s_cp, s_qready, s_dpad = sem("cp_ready"), sem("q_ready"), sem("dpad_ready")
        s_blk, s_kps, s_ksb = sem("blk_staged"), sem("kernel_psum"), sem("kernel_evacuated")
        s_blk0 = sem("blk_zeroed")
        s_same0, s_same, s_bound_in, s_bound, s_pw, s_pwT, s_unscale = (
            sem("same_layer_zeroed"), sem("same_layer_ready"), sem("bound_terms"), sem("bound_psum"),
            sem("unscale_rows"), sem("unscale_psum"), sem("unscale_ready"))
        s_norm_in, s_norm, s_wmul, s_zf, s_z1 = (sem("norm_in"), sem("normalized"), sem("weighted"),
                                                 sem("z_float"), sem("z_high"))
        s_ones = sem("ones_ready")
        s_brow = sem("b_rows_loaded")
        s_lnw_cur = sem("lnw_cur_ready")
        s_lnw, s_k1 = sem("ln_weights_scaled"), sem("kernel_high")
        s_kd, s_kz = sem("kernels_stored"), sem("pad_stored")
        s_var, s_rstd = sem("ln_var"), sem("ln_rstd")
        s_toep = [sem(f"toep_loaded{s}") for s in range(SLOTS)]
        s_z, s_conv, s_y = sem("z_ready"), sem("conv_done"), sem("y_ready")
        s_yT, s_gelu, s_w, s_glu_in = sem("yT_done"), sem("gelu_done"), sem("w_done"), sem("glu_in")
        s_glu, s_back, s_hadd = sem("glu_done"), sem("back_done"), sem("h_added")
        s_x2, s_z2, s_z2T, s_z2sb = sem("x_reloaded"), sem("z2_ready"), sem("z2T_psum"), sem("z2T_ready")
        s_logits, s_lread, s_rexp, s_mask = sem("logits"), sem("logits_read"), sem("router_exp"), sem("mask_ready")
        s_prefix, s_slots, s_mc = sem("prefix_psum"), sem("slots_ready"), sem("moe_const")
        s_fill, s_ew = sem("sorted_zeroed"), sem("expert_weights")
        s_scat = [sem(f"scattered{c}") for c in range(CHUNKS)]
        s_gath = [sem(f"gathered{p}") for p in range(NORMS)]
        s_xt = [sem(f"x_tile_loaded{k}") for k in range(RING)]
        s_id16, s_whi, s_wlo, s_zhi, s_zlo = sem("ident16_ready"), sem("weights_high"), sem("weights_low"), sem("z_pair_high"), sem("z_pair_low")
        s_yt = [sem(f"expert_y_stored{k}") for k in range(4)]
        s_xT, s_xTsb, s_hid, s_silu, s_inner = (sem("xT_psum"), sem("xT_ready"), sem("hidden_psum"),
                                                sem("silu_done"), sem("inner_ready"))
        s_ihi, s_ilo, s_yps, s_yout = (sem("inner_high"), sem("inner_low"), sem("expert_y_psum"), sem("expert_y_ready"))
        s_w1y, s_last_in, s_last = sem("first_weighted"), sem("last_norm_in"), sem("last_normalized")
        s_h_in, s_h = sem("first_norm_in"), sem("h_ready")
        s_wscaled = sem("weights_scaled")
        s_res, s_out = sem("result_ready"), sem("out_stored")

        block = ctx.enter_context(nc.Block())

        @block.sync
        def _(sp):
            sp.dma_start(par[:, 0, :], a_re_log).then_inc(s_par, 16)
            for layer in range(NL):
                sp.dma_start(par[layer * N:(layer + 1) * N, 1, :],
                             bass.AP(log_dt.tensor, layer * H, [[0, N], [1, H]])).then_inc(s_par, 16)
            sp.dma_start(par[:, 2, :], a_im).then_inc(s_par, 16)
            sp.dma_start(par[:, 3, :], c_re).then_inc(s_par, 16)
            sp.dma_start(par[:, 4, :], c_im).then_inc(s_par, 16)
            for k, row_of in ((5, ln_w), (6, ln_b), (7, d_skip)):
                for layer in range(NL):
                    sp.dma_start(par[layer * N:(layer + 1) * N, k, :],
                                 bass.AP(row_of.tensor, layer * H, [[0, N], [1, H]])).then_inc(s_scale, 16)
            sp.dma_start(hres[:, :, :], x).then_inc(s_x, 16)
            sp.dma_start(lnw[:, 0:NL, :], bass.AP(ln_w.tensor, 0, [[0, P], [H, NL], [1, H]])).then_inc(s_wts, 16)
            sp.dma_start(lnb[:, 0:NL, :], bass.AP(ln_b.tensor, 0, [[0, P], [H, NL], [1, H]])).then_inc(s_wts, 16)
            sp.dma_start(wo[:, :, :], w_out).then_inc(s_wts, 16)
            sp.dma_start(bo[:, :, :], b_out).then_inc(s_wts, 16)
            sp.dma_start(router_sb[:, :], router).then_inc(s_wts, 16)
            sp.wait_ge(s_const, 1)
            sp.dma_start(kd[:, :, 0:KPAD, :].rearrange("l h k i -> h l (k i)"),
                         zeros.bitcast(F16)).then_inc(s_kz, 16)
            for g in range(SEGS):
                sp.dma_start(z_sorted[g][:, :].rearrange("(p n k) h -> p n (k h)", p=P, k=4),
                             ln_tmp[:, 0:4, :].rearrange("p a h -> p (a h)").bitcast(F16).unsqueeze(1)
                             .to_broadcast([P, XTS[g] * XP // P // 4, 8 * H])).then_inc(s_fill, 16)
            sp.wait_ge(s_ksb, 2 + H // 16)
            sp.dma_start(b_row, b_rows[:, 0, :].rearrange("(o l) h -> o l h", o=1)).then_inc(s_brow, 16)
            for layer in range(NL):
                sp.dma_start(kd[layer, :, KPAD:KROW, :].rearrange("h (a b) k -> a h (b k)", b=NB),
                             k_sb[layer * NA:(layer + 1) * NA].rearrange("p h b k -> p h (b k)")).then_inc(s_kd, 16)
            sp.wait_ge(s_kd, 16 * NL)
            sp.wait_ge(s_kz, 16)
            with sp.Fori(0, NL) as layer:
                with sp.Fori(0, GROUPS // SLOTS) as g:
                    for s in range(SLOTS):
                        sp.wait_ge(s_conv, layer * GROUPS + g * SLOTS + s + 1)
                        first = KPAD - (P - 1)
                        src = bass.AP(kd, layer * (H * KROW * 2) + g * (SLOTS * GROUP * KROW * 2)
                                      + (s * GROUP * KROW + first) * 2, [[2, P], [KROW * 2, GROUP], [1, 2 * L]])
                        sp.dma_start(toep16[:, s].rearrange("p g l k -> p g (l k)"), src).then_inc(s_toep[s], 16)
            sp.wait_ge(s_yT, NL * TILES // 4)
            sp.dma_start(ybuf[:, :, :], x).then_inc(s_x2, 16)
            sp.wait_ge(s_back, NL * QUADS)
            sp.dma_start(w1_stage, w1).then_inc(s_ew, 16)
            sp.wait_ge(s_wlo, 1)
            sp.dma_start(w2_stage, w2.rearrange("p e c n -> p e (c n)")).then_inc(s_ew, 16)

            def rows(buf, n):
                return buf[bass.ds(n * XP, XP), :].rearrange("(p t) h -> p (t h)", t=2)

            def load(g, n, k, transposed):
                if transposed is not None:
                    sp.wait_ge(s_xT, transposed)
                sp.dma_start(x_tile[:, k].rearrange("p t k h -> p (t k h)"), rows(z_sorted[g], n)).then_inc(s_xt[k], 16)

            def store(g, n, k):
                sp.wait_ge(s_yout, n + (FIRSTS[g] + 1))
                sp.dma_start(rows(y_sorted[g], n), y_tile[:, k, :]).then_inc(s_yt[k], 16)

            def wait_sorted(g):
                for c in SEGMENTS[g]:
                    sp.wait_ge(s_scat[c], 16 * 2 * CHUNK)
            LAG = 3
            wait_sorted(0)
            for k in range(RING):
                load(0, k, k, None)
            for g in range(SEGS):
                first, xt = FIRSTS[g], XTS[g]
                for n in range(RING):
                    load(g, n + RING, n, first + n + 1)
                    if n >= LAG:
                        store(g, n - LAG, n - LAG)
                    elif g > 0:
                        store(g - 1, XTS[g - 1] + n - LAG, (n - LAG) % RING)
                with sp.Fori(0, xt // RING - 2) as i:
                    for k in range(RING):
                        load(g, i * RING + (2 * RING + k), k, i * RING + (first + RING + k + 1))
                        store(g, i * RING + (RING + k - LAG), (k - LAG) % RING)
                for k in range(RING):
                    n = xt - RING + k
                    if g + 1 < SEGS:
                        if k == 0:
                            wait_sorted(g + 1)
                        load(g + 1, k, k, first + n + 1)
                    store(g, n - LAG, (k - LAG) % RING)
            for n in range(XTS[-1] - LAG, XTS[-1]):
                store(SEGS - 1, n, n % RING)
            for p in range(NORMS):
                tiles = slice(p * PART, (p + 1) * PART)
                sp.wait_ge(s_res, p + 1)
                sp.dma_start(out[:, tiles, :], hres[:, tiles, :]).then_inc(s_out, 16)
            sp.wait_ge(s_out, 16 * NORMS)

        @block.gpsimd
        def _(pool):
            nc.gpsimd.memset(ln_tmp[:, 0:4, :], 0.0).then_inc(s_const, 1)
            nc.gpsimd.iota(iota[:, 0:NB], pattern=[[1, NB]], base=0, channel_multiplier=0,
                           allow_small_or_imprecise_dtypes=True).then_inc(s_iota, 1)
            nc.gpsimd.iota(iota[:, NB:NB + NA], pattern=[[NB, NA]], base=0, channel_multiplier=0,
                           allow_small_or_imprecise_dtypes=True).then_inc(s_iota, 1)
            nc.gpsimd.memset(ident[:, :], 0.0).then_inc(s_sel, 1)
            nc.gpsimd.memset(d_sel[:, :, :], 0.0).then_inc(s_sel, 1)
            nc.gpsimd.memset(neg_half[:, :], -0.5).then_inc(s_sel, 1)
            nc.gpsimd.memset(half_pi[:, :], TWO_PI / 4).then_inc(s_iota, 1)
            nc.gpsimd.memset(lnw[:, NL, :], Z_SCALE).then_inc(s_sel, 1)
            nc.gpsimd.memset(same_layer, 0.0).then_inc(s_same0, 1)
            pool.wait_ge(s_same0, 1)
            for layer in range(NL):
                rows = slice(layer * N, (layer + 1) * N)
                nc.gpsimd.memset(same_layer[rows, rows], 1.0).then_inc(s_same, 1)
            pool.wait_ge(s_same, NL)
            nc.gpsimd.memset(lnb[:, NL, :], 0.0).then_inc(s_sel, 1)
            pool.wait_ge(s_sel, 5)
            nc.gpsimd.affine_select(out=ident[:, :], in_=ident[:, :], compare_op=ALU.not_equal, fill=1.0,
                                    base=0, pattern=[[-1, P]], channel_multiplier=1).then_inc(s_sel, 1)
            nc.gpsimd.affine_select(out=d_sel[:, :, 0:1], in_=d_sel[:, :, 0:1], compare_op=ALU.not_equal, fill=1.0,
                                    base=0, pattern=[[-N, NL], [0, 1]], channel_multiplier=1).then_inc(s_sel, 1)
            pool.wait_ge(s_small, 1)
            pool.wait_ge(s_iota, 2)
            nc.gpsimd.tensor_tensor(p_mag, sm[:, 1, :].unsqueeze(2).to_broadcast([P, H, NA]),
                                    iota[:, NB:NB + NA].unsqueeze(1).to_broadcast([P, H, NA]), ALU.mult).then_inc(s_pmag, 1)
            nc.gpsimd.tensor_tensor(q_re, sm[:, 1, :].unsqueeze(2).to_broadcast([P, H, NB]),
                                    iota[:, 0:NB].unsqueeze(1).to_broadcast([P, H, NB]), ALU.mult).then_inc(s_qmag_in, 1)
            def root(i, rstd=rstd[:, :], var=var[:, :]):
                pool.wait_ge(s_var, i + 1)
                nc.gpsimd.tensor_tensor(rstd, var, neg_half[:, 0:var.shape[1]], ALU.pow).then_inc(s_rstd, 1)

            for i in range(2):
                root(i, rstd_of[:, FIRST_NORMS[i][1]])
            pool.wait_ge(s_qmag_done, 1)
            pool.wait_ge(s_qtrig, 2)
            nc.gpsimd.tensor_tensor(q_re, q_re, q_cnt, ALU.mult).then_inc(s_qready, 1)
            nc.gpsimd.tensor_tensor(q_im, q_im, q_cnt, ALU.mult).then_inc(s_qready, 1)
            pool.wait_ge(s_qready, 2)
            nc.gpsimd.memset(cp_blk, 0.0).then_inc(s_blk0, 1)
            for i in range(2, 2 * CHUNKS):
                root(i, rstd_of[:, FIRST_NORMS[i][1]])
            with pool.Fori(0, NL) as layer:
                def root_part(p):
                    root(2 * CHUNKS + layer * NORMS + p, rstd_part(p), var_part(p))
                root_part(0)
                root_part(1)
                pool.wait_ge(s_lnw_cur, layer + 1)
                for p in range(NORMS - 1):
                    pool.wait_ge(s_norm, TILES + layer * NORM_TILES + (p + 1) * PART)
                    nc.gpsimd.tensor_tensor(norm_bufs[p % 4], norm_bufs[p % 4],
                                            lnw_cur[:, :, :].to_broadcast([P, PART, H]), ALU.mult).then_inc(s_wmul, 1)
                    if p + 2 < NORMS:
                        root_part(p + 2)
            pool.wait_ge(s_conv, SLOTS + NL * GROUPS)
            nc.gpsimd.iota(rank, pattern=[[-1, E]], base=E, channel_multiplier=0,
                           allow_small_or_imprecise_dtypes=True).then_inc(s_mc, 1)
            nc.gpsimd.iota(tile_no, pattern=[[1, MOST_X]], base=0, channel_multiplier=0,
                           allow_small_or_imprecise_dtypes=True).then_inc(s_mc, 1)
            nc.gpsimd.memset(ones8, 1.0).then_inc(s_mc, 1)
            nc.gpsimd.memset(all_ones, 1.0).then_inc(s_mc, 1)
            pool.wait_ge(s_mc, 4)
            nc.gpsimd.affine_select(out=below, in_=all_ones, compare_op=ALU.is_gt, fill=0.0,
                                    base=0, pattern=[[1, P]], channel_multiplier=-1).then_inc(s_mc, 1)
            done = 2 * CHUNKS + NL * NORMS

            def scatter(c, ks=range(2)):
                pool.wait_ge(s_slots, SEG_OF[c] + 1)
                pool.wait_ge(s_zlo, c + 1)
                if c == 0:
                    pool.wait_ge(s_fill, 16 * SEGS)
                for k in ks:
                    for t in range(c * CHUNK, (c + 1) * CHUNK):
                        nc.gpsimd.indirect_dma_start(
                            out=z_sorted[SEG_OF[c]][:, :], out_offset=bass.IndirectOffsetOnAxis(ap=slot[:, k, t:t + 1], axis=0),
                            in_=z_pair[c][:, t - c * CHUNK, :, :].rearrange("p k h -> p (k h)"), in_offset=None).then_inc(s_scat[c], 16)

            def gather(p, k, at=0, n=PART):
                g = SEG_OF[p * PART // CHUNK]
                if p * PART + at == SEGMENTS[g][0] * CHUNK and k == 0:
                    for i in range(4):
                        pool.wait_ge(s_yt[i], 16 * ((FIRSTS[g] + XTS[g]) // 4))
                for t in range(p * PART + at, p * PART + at + n):
                    nc.gpsimd.indirect_dma_start(
                        out=y_of(k, t)[:, 0, :], out_offset=None, in_=y_sorted[g][:, :],
                        in_offset=bass.IndirectOffsetOnAxis(ap=slot[:, k, t:t + 1], axis=0)).then_inc(s_gath[p], 16)

            def low_weights(k):
                pool.wait_ge(s_whi, k + 1)
                pairs, stage = ((w1_16, w1_stage), (w2_16, w2_stage))[k]
                nc.gpsimd.tensor_tensor(pairs[:, 1], stage, pairs[:, 0], ALU.subtract).then_inc(s_wlo, 1)
            root(done, rstd_of[:, 0])
            root(done + 1, rstd_of[:, 1])
            root(done + 2, rstd_of[:, 2])
            low_weights(0)
            scatter(0, [0])
            root(done + 3, rstd_of[:, 3])
            scatter(0, [1])
            low_weights(1)
            for c in range(1, CHUNKS):
                scatter(c)
            pool.wait_ge(s_z2, TILES)
            for p in range(2):
                for k in range(2):
                    gather(p, k)
            for c in range(1, CHUNKS):
                pool.wait_ge(s_scat[c], 16 * 2 * CHUNK)
            for p in range(2, NORMS - 2):
                for k in range(2):
                    gather(p, k)

            def last_root(r):
                root(done + CHUNKS + r, rstd_part(r), var_part(r))
            r = 0
            for p in range(NORMS - 2, NORMS):
                for k in range(2):
                    for at_t in range(0, PART, 4):
                        gather(p, k, at_t, 4)
                        if r < NORMS - 2:
                            last_root(r)
                            r += 1
            for r in range(NORMS - 2, NORMS):
                last_root(r)

        @block.scalar
        def _(act):
            A = nc.scalar.activation
            act.wait_ge(s_par, 16 * (4 + NL))
            A(sm[:, 0, :], par[:, 1, :], ACT.Exp).then_inc(s_exp1, 1)
            A(sm[:, 2, :], par[:, 0, :], ACT.Exp).then_inc(s_exp1, 1)
            act.wait_ge(s_small, 1)
            A(sm[:, 3, :], sm[:, 1, :], ACT.Tanh, scale=0.5).then_inc(s_exp1, 1)
            act.wait_ge(s_pmag, 1)
            A(p_mag, p_mag, ACT.Exp).then_inc(s_pmag_done, 1)
            act.wait_ge(s_qmag_in, 1)
            act.wait_ge(s_qcyc, 1)
            A(q_cnt, q_re, ACT.Exp).then_inc(s_qmag_done, 1)
            act.wait_ge(s_iota, 3)
            act.wait_ge(s_pcyc, 2)
            A(sm[:, 5, :], sm[:, 4, :], ACT.Sin).then_inc(s_e2, 1)
            A(sm[:, 6, :], sm[:, 4, :], ACT.Sin, scale=0.5).then_inc(s_e2, 1)
            A(sm[:, 7, :], sm[:, 4, :], ACT.Abs).then_inc(s_act, 1)
            A(p_sin, p_ang, ACT.Sin).then_inc(s_ptrig, 1)
            act.wait_ge(s_ptrig, 1)
            A(p_ang, p_ang, ACT.Abs).then_inc(s_act, 1)
            act.wait_ge(s_act, 2)
            A(sm[:, 8, :], sm[:, 7, :], ACT.Sin, bias=half_pi[:, 0:1], scale=-1.0).then_inc(s_e2, 1)
            A(p_cnt, p_ang, ACT.Sin, bias=half_pi[:, 0:1], scale=-1.0).then_inc(s_ptrig, 1)
            act.wait_ge(s_qcyc, 2)
            A(q_im, q_ang, ACT.Sin, scale=-1.0).then_inc(s_qtrig, 1)
            act.wait_ge(s_qtrig, 1)
            A(q_ang, q_ang, ACT.Abs).then_inc(s_act, 1)
            act.wait_ge(s_act, 3)
            act.wait_ge(s_qmag_done, 1)
            A(q_re, q_ang, ACT.Sin, bias=half_pi[:, 0:1], scale=-1.0).then_inc(s_qtrig, 1)
            act.wait_ge(s_cp, 1)
            act.wait_ge(s_blk0, 1)
            for g in range(H // 16):
                act.wait_ge(s_kps, g + 1)
                for layer in range(NL):
                    rows = slice(layer * N, (layer + 1) * N)
                    for k, src in ((0, cp_re), (1, cp_im)):
                        A(cp_blk[rows, g % 2, k, :, layer, :], src[rows, g * 16:(g + 1) * 16, :],
                          ACT.Copy).then_inc(s_blk, 1)
                act.wait_ge(s_h_in, g // 2 + 1)
                for k in range(PART):
                    tile = hres[:, g * PART + k, :]
                    A(tile, tile, ACT.Identity, scale=rstd_part(g)[:, k:k + 1],
                      bias=shift_part(g)[:, k:k + 1]).then_inc(s_h, 1)
            act.wait_ge(s_wts, 16 * 5)
            A(bo_half[:, :, :], bo[:, :, :], ACT.Copy, scale=0.5).then_inc(s_bh, 1)
            act.wait_ge(s_bh, 1)
            act.wait_ge(s_pwT, 1)
            A(unscale[:, :], bank[3][:, 0:P:N], ACT.Copy).then_inc(s_unscale, 1)
            act.wait_ge(s_unscale, 1)

            def high_part(i, tiles, src):
                act.wait_ge(s_zf, i + 1)
                A(z_conv[:, :, 0, tiles].rearrange("p h t -> p t h"), src, ACT.Copy).then_inc(s_z1, 1)
            for p in range(NORMS + 1):
                if p < NORMS:
                    act.wait_ge(s_norm_in, p + 1)
                    if p >= 4:
                        act.wait_ge(s_z, p - 3)
                    for k in range(PART):
                        A(norm_bufs[p % 4][:, k, :], hres[:, p * PART + k, :], ACT.Identity,
                          scale=rstd_part(p)[:, k:k + 1], bias=shift_part(p)[:, k:k + 1]).then_inc(s_norm, 1)
                if p > 0:
                    high_part(p - 1, slice((p - 1) * PART, p * PART), norm_bufs[(p - 1) % 4])
            act.wait_ge(s_brow, 16)
            act.wait_ge(s_lnw, 2)
            with act.Fori(0, NL) as layer:
                for half, scale in ((0, 0.5), (1, 1.0)):
                    cols = slice(half * H, (half + 1) * H)
                    A(wo_cur[:, cols], wo[:, bass.ds(layer, 1), cols].rearrange("p a n -> p (a n)"), ACT.Copy,
                      scale=scale).then_inc(s_wo, 1)
                A(bu_cur[:, :], b_row[:, bass.ds(layer, 1), :].rearrange("p a n -> p (a n)"), ACT.Copy,
                  scale=0.5).then_inc(s_wo, 1)
                A(bo_cur[:, :], bo_half[:, bass.ds(layer, 1), :].rearrange("p a n -> p (a n)"), ACT.Copy).then_inc(s_bo, 1)
                A(unscale_cur[:, :], unscale[:, bass.ds(layer, 1)], ACT.Copy).then_inc(s_bo, 1)
                A(lnw_cur[:, :, :], lnw[:, bass.ds(layer + 1, 1), :], ACT.Copy).then_inc(s_lnw_cur, 1)
                act.wait_ge(s_bo, (layer + 1) * 2)

                def gelu(q):
                    act.wait_ge(s_yT, layer * QUADS + q + 1)
                    ap = bank[q % 2][:, :]
                    back = bass.AP(ap.tensor, ap.offset + P - 1, [list(ap.ap[0]), [P, 4], [-1, P]])
                    A(g_act[:, q % 2, :, :], back, ACT.Gelu_apprx_tanh, scale=unscale_cur[:, 0:1]).then_inc(s_gelu, 1)

                def tanh(q):
                    act.wait_ge(s_w, layer * QUADS + q + 1)
                    act.wait_ge(s_glu, layer * QUADS + q + 1)
                    A(g_tanh[:, q % 2, :], bank[4 + q % 2][:, :], ACT.Tanh, scale=0.5,
                      bias=bo_cur[:, 1:2]).then_inc(s_glu_in, 1)

                def normalize(p, half):
                    act.wait_ge(s_norm_in, (layer + 1) * NORMS + p + 1)
                    if p >= 4:
                        act.wait_ge(s_z, (layer + 1) * NORMS + p - 3)
                    for k in range(half * 4, half * 4 + 4):
                        A(norm_bufs[p % 4][:, k, :], hres[:, p * PART + k, :], ACT.Identity,
                          scale=rstd_part(p)[:, k:k + 1], bias=shift_part(p)[:, k:k + 1]).then_inc(s_norm, 1)
                for q in range(QUADS + 9):
                    if q < QUADS:
                        gelu(q)
                    if 0 < q <= QUADS:
                        tanh(q - 1)
                    p, half = divmod(q - 6, 2)
                    if 0 <= p < NORMS and (p, half) != (NORMS - 1, 1):
                        normalize(p, half)
                    p, k = divmod(q - 10, 2)
                    if k == 0 and 0 <= p < NORMS:
                        high_part((layer + 1) * NORMS + p, slice(p * PART, (p + 1) * PART), norm_bufs[p % 4])
            A(ident16, ident[:, :], ACT.Copy).then_inc(s_id16, 1)
            for c in range(CHUNKS):
                if c < 2:
                    act.wait_ge(s_ew, 16 * (c + 1))
                    pairs, stage = ((w1_16, w1_stage), (w2_16, w2_stage))[c]
                    A(stage, stage, ACT.Copy, scale=W_SCALE).then_inc(s_wscaled, 1)
                    act.wait_ge(s_wscaled, c + 1)
                    A(pairs[:, 0], stage, ACT.Copy).then_inc(s_whi, 1)
                for q in range(c * 4, c * 4 + 4):
                    act.wait_ge(s_z2T, q + 1)
                    A(z2T[:, q % 2, :], bank[q % 2][:, :], ACT.Copy).then_inc(s_z2sb, 1)
                act.wait_ge(s_z2, (c + 1) * CHUNK)
                if c > 0:
                    act.wait_ge(s_zlo, c)
                A(z_pair[c][:, :, 0, :], ybuf[:, c * CHUNK:(c + 1) * CHUNK, :], ACT.Copy, scale=Z_SCALE).then_inc(s_zhi, 1)
                act.wait_ge(s_lread, c + 1)
                A(route[:, 1], route[:, 0], ACT.Exp).then_inc(s_rexp, 1)

            def step(first, xt, n, k, div):
                if n_at(n) < xt:
                    act.wait_ge(s_hid, n + (first + 1))
                    A(gate_act[:, k % 2, :], bank[2 + k % 2 * 2][:, :], ACT.Silu,
                      scale=1.0 / (Z_SCALE * W_SCALE)).then_inc(s_silu, 1)
                if n_at(n) >= 2:
                    m = (k - 2) % 4
                    act.wait_ge(s_yps, n + (first - 1))
                    rounds = div(-2, 4) + first // 4
                    if not (isinstance(rounds, int) and rounds < 1):
                        act.wait_ge(s_yt[m], rounds * 16)
                    A(y_tile[:, m, :], bank[6 + m % 2][:, 0:2 * H], ACT.Copy,
                      scale=1.0 / (I_SCALE * W_SCALE)).then_inc(s_yout, 1)
                if n_at(n) < xt:
                    act.wait_ge(s_inner, n + (first + 1))
                    A(inner16[:, k % 4, 0, :], inner[:, k % 2, :], ACT.Copy,
                      scale=I_SCALE / (Z_SCALE * W_SCALE)).then_inc(s_ihi, 1)
            for g in range(SEGS):
                tile_steps(act, XTS[g], lambda n, k, div, _: step(FIRSTS[g], XTS[g], n, k, div))
            for p in range(NORMS + 2):
                if p < NORMS:
                    act.wait_ge(s_gath[p], 16 * 2 * PART)
                    for t in range(PART):
                        y1 = y_of(0, p * PART, PART)[:, t, :]
                        A(y1, y1, ACT.Copy, scale=weight[:, 0, p * PART + t:p * PART + t + 1]).then_inc(s_w1y, 1)
                if p > 1:
                    act.wait_ge(s_last_in, p - 1)
                    for t in range(PART):
                        y1 = y_of(0, (p - 2) * PART, PART)[:, t, :]
                        A(y1, y1, ACT.Identity, scale=rstd_part(p - 2)[:, t:t + 1],
                          bias=shift_part(p - 2)[:, t:t + 1]).then_inc(s_last, 1)

        @block.tensor
        def _(pe):
            MM = nc.tensor.matmul
            pe.wait_ge(s_same, NL)
            pe.wait_ge(s_bound_in, 1)
            MM(bank[2][:, 0:H], same_layer, sm[:, 0, :], start=True, stop=True).then_inc(s_bound, 1)
            pe.wait_ge(s_pw, 1)
            nc.tensor.transpose(bank[3][:, 0:P], sm[:, 0, :], ident[:, :]).then_inc(s_pwT, 1)
            pe.wait_ge(s_sel, 7)
            pe.sem_inc(s_kps, 2)
            pe.wait_ge(s_dpad, 1)
            pe.wait_ge(s_qready, 2)
            with pe.Fori(0, 4) as g2:
                for s in range(2):
                    pe.wait_ge(s_blk, (g2 * 2 + s + 1) * 2 * NL)
                    pe.wait_ge(s_ksb, g2 * 2 + s + 1)
                    MM(bank[s][0:NL * NA, :], d_sel[:, :, :].rearrange("p l a -> p (l a)"),
                       d_row[:, bass.ds((g2 * 2 + s) * 16, 16), :], start=True, stop=False)
                    for c in range(16):
                        for k, q in ((0, q_re), (1, q_im)):
                            last = MM(bank[s][0:NL * NA, c * NB:(c + 1) * NB],
                                      cp_blk[:, s, k, c, :, :].rearrange("p l a -> p (l a)"),
                                      q[:, bass.ds((g2 * 2 + s) * 16 + c, 1), :].rearrange("p a b -> p (a b)"),
                                      start=False, stop=(c == 15 and k == 1))
                    last.then_inc(s_kps, 1)
            pe.wait_ge(s_ones, 1)
            pe.sem_inc(s_conv, SLOTS)
            pe.wait_ge(s_wts, 16 * 5)
            with pe.Fori(0, NL) as layer:
                pe.wait_ge(s_z, (layer + 1) * NORMS)
                for g in range(GROUPS):
                    pe.wait_ge(s_toep[g % SLOTS], (layer * (GROUPS // SLOTS) + g // SLOTS + 1) * 16)
                    pe.wait_ge(s_y, layer * GROUPS + g + 1)
                    for c in range(GROUP):
                        dst = bank[g % 4][:, :].rearrange("p (c k t) -> p c k t", c=GROUP, k=2)[:, c]
                        for d in range(J):
                            for k in range(2):
                                last = MM(dst[:, :, d * B:], toep16[:, g % SLOTS, c, d * P:(d + 1) * P, k],
                                          z_conv[:, g * GROUP + c, :, 0:TILES - d * B],
                                          start=(d == 0 and k == 0), stop=(d == J - 1 and k == 1))
                    last.then_inc(s_conv, 1)
                pe.wait_ge(s_y, 4 + (layer + 1) * GROUPS)
                pe.wait_ge(s_wo, 3 * (layer + 1))

                def forward(q):
                    for t in range(4):
                        last = nc.tensor.transpose(bank[q % 2][:, t * P:(t + 1) * P], ybuf[:, q * 4 + t, :], ident[:, :])
                    last.then_inc(s_yT, 1)

                def weights(q):
                    pe.wait_ge(s_gelu, layer * QUADS + q + 1)
                    pe.wait_ge(s_glu, layer * QUADS + q + 1)
                    g = g_act[:, q % 2, :, :].rearrange("p a t -> p (a t)")
                    MM(bank[4 + q % 2][:, :], wo_cur[:, H:2 * H], g, start=True, stop=True)
                    MM(bank[2 + q % 2][:, :], wo_cur[:, 0:H], g, start=True, stop=False)
                    MM(bank[2 + q % 2][:, :], bu_cur[:, :], ones[:, :], start=False, stop=True).then_inc(s_w, 1)

                def backward(q):
                    pe.wait_ge(s_glu, 2 + layer * QUADS + q + 1)
                    pe.wait_ge(s_hadd, layer * QUADS + q + 1)
                    for t in range(4):
                        last = nc.tensor.transpose(bank[6 + q % 2][:, t * P:(t + 1) * P],
                                                   g_out[:, q % 2, t * P:(t + 1) * P], ident[:, :])
                    last.then_inc(s_back, 1)
                forward(0)
                for q in range(QUADS + 2):
                    if q + 1 < QUADS:
                        forward(q + 1)
                    if q < QUADS:
                        weights(q)
                    if q >= 2:
                        backward(q - 2)
            pe.wait_ge(s_mc, 5)
            for c in range(CHUNKS):
                pe.wait_ge(s_z2, (c + 1) * CHUNK)
                for q in range(c * 4, c * 4 + 5):
                    if q < c * 4 + 4:
                        if q >= 2:
                            pe.wait_ge(s_z2sb, q - 1)
                        for t in range(4):
                            last = nc.tensor.transpose(bank[q % 2][:, t * P:(t + 1) * P], ybuf[:, q * 4 + t, :], ident[:, :])
                        last.then_inc(s_z2T, 1)
                    if q > c * 4:
                        pe.wait_ge(s_z2sb, q)
                        if q == c * 4 + 1 and c > 0:
                            pe.wait_ge(s_lread, c)
                        for t in range(4):
                            at_t = ((q - 1) % 4 * 4 + t) * E
                            last = MM(bank[6][:, at_t:at_t + E], z2T[:, (q - 1) % 2, t * P:(t + 1) * P], router_sb[:, :],
                                      start=True, stop=True)
                last.then_inc(s_logits, 1)
                g = SEG_OF[c]
                if c != SEGMENTS[g][-1]:
                    continue
                tiles = SEG_TILES[g]
                pe.wait_ge(s_mask, c + 1)
                if g > 0:
                    pe.wait_ge(s_slots, g)
                MM(bank[7][:, 0:tiles * E], below, mask[:, 0:tiles].rearrange("p t e -> p (t e)"), start=True, stop=False)
                for t in range(tiles - 1):
                    MM(bank[7][:, (t + 1) * E:tiles * E].rearrange("p (t e) -> p t e", e=E), all_ones,
                       mask[:, t:t + 1, :].to_broadcast([P, tiles - 1 - t, E]), start=False, stop=(t == tiles - 2))
                for t in range(tiles):
                    last = MM(bank[7][:, tiles * E:tiles * E + E], all_ones, mask[:, t, :],
                              start=(t == 0), stop=(t == tiles - 1))
                last.then_inc(s_prefix, 1)
            pe.wait_ge(s_wlo, 2)
            pe.wait_ge(s_id16, 1)
            pe.wait_ge(s_slots, SEGS)
            PARTS = ((0, 0), (0, 1), (1, 0))

            def transpose_in(k, rounds):
                pe.wait_ge(s_xt[k], rounds * 16)
                for px in range(2):
                    for t in range(2):
                        last = MM(bank[k % 2][:, (px * 2 + t) * P:(px * 2 + t + 1) * P], x_tile[:, k, t, px, :],
                                  ident16, start=True, stop=True)
                last.then_inc(s_xT, 1)

            experts = {}

            def expert(g, k, n):
                experts[k] = pe.value_load(owner[0:1, g, bass.ds(n, 1)], min_val=0, max_val=(E - 1) * WE)

            def step(first, xt, g, n, k, div, new_turn):
                in_loop = not isinstance(n, int)
                if n_at(n) < xt - 1:
                    transpose_in((k + 1) % RING, div(1, RING) + (first // RING + 1))
                if n_at(n) < xt:
                    expert(g, k, n)
                    e = experts[k]
                    pe.wait_ge(s_xTsb, n + (first + 1))
                    if in_loop or first + n >= 2:
                        pe.wait_ge(s_inner, n + (first - 1))
                    for piece in range(2 * I // P):
                        out = bank[2 + k % 2 * 2 + piece // 2]
                        for i, (pw, px) in enumerate(PARTS):
                            last = MM(out[:, piece % 2 * XP:(piece % 2 + 1) * XP],
                                      w1_row[:, pw, bass.ds(e + piece * P, P)],
                                      xT[:, k % 2, px * XP:(px + 1) * XP], start=(i == 0), stop=(i == 2))
                    last.then_inc(s_hid, 1)
                if n_at(n) >= 2:
                    m = (k - 2) % RING
                    if new_turn:
                        expert(g, m, n - 2)
                    e = experts[m]
                    pe.wait_ge(s_ilo, n + (first - 1))
                    if in_loop or first + n >= 4:
                        pe.wait_ge(s_yout, n + (first - 3))
                    for t in range(2):
                        for piece in range(I // P):
                            for i, (px, pw) in enumerate(PARTS):
                                at_tok = piece * XP + t * P
                                last = MM(bank[6 + m % 2][:, t * H:(t + 1) * H], inner16[:, m, px, at_tok:at_tok + P],
                                          w2_row[:, bass.ds(e + (pw * 2 + piece) * H, H)],
                                          start=(piece == 0 and i == 0), stop=(piece == 1 and i == 2))
                    last.then_inc(s_yps, 1)
            for g in range(SEGS):
                transpose_in(0, FIRSTS[g] // RING + 1)
                tile_steps(pe, XTS[g], lambda n, k, div, new_turn: step(FIRSTS[g], XTS[g], g, n, k, div, new_turn))

        @block.vector
        def _(dve):
            V = nc.vector
            TT, STT, TS = V.tensor_tensor, V.scalar_tensor_tensor, V.tensor_scalar
            dve.sem_inc(s_ksb, 2)
            dve.sem_inc(s_glu, 2)
            dve.sem_inc(s_hadd, 2)
            st = Steps(dve, s_dve)

            def turns(ang, cnt, after_count=None):
                st.done(TS(cnt, ang, 1.0 / TWO_PI, ROUND, ALU.mult, ALU.add))
                st.after()
                st.done(TS(cnt, cnt, ROUND, None, ALU.subtract))
                st.after()
                st.done(STT(ang, cnt, -TWO_PI_HI, ang, ALU.mult, ALU.add))
                st.after()
                st.done(STT(ang, cnt, -TWO_PI_LO, ang, ALU.mult, ALU.add))
                st.after()
                if after_count is not None:
                    dve.sem_inc(after_count, 1)
                return TS(ang, ang, PI, -PI, ALU.min, ALU.max)

            def over(v, n):
                return v.unsqueeze(2).to_broadcast([P, H, n])

            def moments(sp, tiles, mean=mean[:, :], roots=None, at=slice(0, CHUNK)):
                if tiles is not None:
                    for k in range(CHUNK):
                        sp.done(V.bn_stats(stats[:, k, :], tiles(k)))
                sp.after()
                sp.done(TT(mean, stats[:, at, 1], stats[:, at, 4], ALU.add))
                sp.done(TT(diff[:, at], stats[:, at, 1], stats[:, at, 4], ALU.subtract))
                sp.done(TT(m2[:, at], stats[:, at, 2], stats[:, at, 5], ALU.add))
                sp.after()
                sp.done(TS(mean, mean, 0.5, None, ALU.mult))
                sp.done(STT(diff[:, at], diff[:, at], 0.25, diff[:, at], ALU.mult, ALU.mult))
                sp.done(TS(m2[:, at], m2[:, at], 1.0 / H, EPS, ALU.mult, ALU.add))
                sp.after()
                if roots is not None:
                    dve.wait_ge(s_rstd, roots)
                TT(var[:, at], m2[:, at], diff[:, at], ALU.add).then_inc(s_var, 1)

            def first_moments(i):
                which, c = FIRST_NORMS[i]
                if which == "h":
                    dve.wait_ge(s_h, (c + 1) * CHUNK)
                moments(st, lambda k: hres[:, c * CHUNK + k, :], mean_of[:, c], i if i > 0 else None)

            def first_shift(c):
                dve.wait_ge(s_rstd, c + 1)
                STT(shift_of[:, c], mean_of[:, c], -1.0, rstd_of[:, c], ALU.mult, ALU.mult).then_inc(s_h_in, 1)

            st.done(V.memset(d_row, 0.0))
            dve.wait_ge(s_exp1, 2)
            STT(sm[:, 1, :], sm[:, 2, :], -1.0, sm[:, 0, :], ALU.mult, ALU.mult).then_inc(s_small, 1)
            st.done(TT(sm[:, 9, :], par[:, 2, :], sm[:, 0, :], ALU.mult))
            st.after()
            st.done(V.tensor_copy(sm[:, 4, :], sm[:, 9, :]))
            dve.wait_ge(s_iota, 3)
            st.done(TT(p_ang, over(sm[:, 9, :], NA), iota[:, NB:NB + NA].unsqueeze(1).to_broadcast([P, H, NA]), ALU.mult))
            st.done(TT(q_ang, over(sm[:, 9, :], NB), iota[:, 0:NB].unsqueeze(1).to_broadcast([P, H, NB]), ALU.mult))
            st.after()
            turns(sm[:, 4, :], sm[:, 10, :]).then_inc(s_pcyc, 1)
            turns(p_ang, p_cnt).then_inc(s_pcyc, 1)
            turns(q_ang, q_cnt, s_qcyc).then_inc(s_qcyc, 1)
            dve.wait_ge(s_x, 16)
            first_moments(0)
            first_moments(1)
            t, sin_y, sin_h, cos_y, e_re, e_im = (sm[:, k, :] for k in (3, 5, 6, 8, 12, 13))
            aim = par[:, 2, :]
            dve.wait_ge(s_exp1, 3)
            dve.wait_ge(s_e2, 3)
            st.done(TS(sm[:, 10, :], t, -1.0, 1.0, ALU.mult, ALU.add))
            st.after()
            st.done(V.reciprocal(sm[:, 10, :], sm[:, 10, :]))
            st.after()
            st.done(STT(sm[:, 11, :], t, 2.0, sm[:, 10, :], ALU.mult, ALU.mult))
            st.done(STT(sm[:, 14, :], sin_h, -2.0, sin_h, ALU.mult, ALU.mult))
            st.after()
            st.done(TT(e_re, sm[:, 11, :], cos_y, ALU.mult))
            st.done(STT(e_im, sm[:, 11, :], 1.0, sin_y, ALU.add, ALU.mult))
            st.after()
            st.done(TT(e_re, e_re, sm[:, 14, :], ALU.add))
            st.after()
            st.done(STT(sm[:, 14, :], e_re, -1.0, sm[:, 2, :], ALU.mult, ALU.mult))
            st.done(TT(sm[:, 15, :], e_im, aim, ALU.mult))
            st.done(STT(sm[:, 10, :], e_im, -1.0, sm[:, 2, :], ALU.mult, ALU.mult))
            st.done(TT(sm[:, 11, :], e_re, aim, ALU.mult))
            st.done(TT(sm[:, 7, :], sm[:, 2, :], sm[:, 2, :], ALU.mult))
            st.done(TT(sm[:, 4, :], aim, aim, ALU.mult))
            st.after()
            st.done(TT(sm[:, 14, :], sm[:, 14, :], sm[:, 15, :], ALU.add))
            st.done(TT(sm[:, 10, :], sm[:, 10, :], sm[:, 11, :], ALU.subtract))
            st.done(TT(sm[:, 7, :], sm[:, 7, :], sm[:, 4, :], ALU.add))
            st.after()
            st.done(V.reciprocal(sm[:, 7, :], sm[:, 7, :]))
            st.after()
            st.done(STT(sm[:, 14, :], sm[:, 14, :], 2.0, sm[:, 7, :], ALU.mult, ALU.mult))
            st.done(STT(sm[:, 10, :], sm[:, 10, :], 2.0, sm[:, 7, :], ALU.mult, ALU.mult))
            st.after()
            st.done(TT(sm[:, 11, :], par[:, 3, :], sm[:, 14, :], ALU.mult))
            st.done(TT(sm[:, 12, :], par[:, 4, :], sm[:, 10, :], ALU.mult))
            st.done(TT(sm[:, 13, :], par[:, 3, :], sm[:, 10, :], ALU.mult))
            st.done(TT(sm[:, 15, :], par[:, 4, :], sm[:, 14, :], ALU.mult))
            st.after()
            st.done(TT(sm[:, 11, :], sm[:, 11, :], sm[:, 12, :], ALU.subtract))
            st.done(TT(sm[:, 13, :], sm[:, 13, :], sm[:, 15, :], ALU.add))
            st.after()
            def magnitude(out, a):
                return TS(out.bitcast(U32), a.bitcast(U32), 0x7FFFFFFF, None, ALU.bitwise_and)

            def power(out, a):
                return TS(out.bitcast(U32), a.bitcast(U32), 0x7F800000, None, ALU.bitwise_and)
            dve.wait_ge(s_scale, 16 * 3 * NL)
            st.done(magnitude(sm[:, 14, :], sm[:, 11, :]))
            st.done(magnitude(sm[:, 15, :], sm[:, 13, :]))
            for k in (5, 6):
                st.done(magnitude(par[:, k, :], par[:, k, :]))
            st.done(magnitude(sm[:, 10, :], par[:, 7, :]))
            st.after()
            TT(sm[:, 0, :], sm[:, 14, :], sm[:, 15, :], ALU.add).then_inc(s_bound_in, 1)
            st.done(STT(par[:, 5, :], par[:, 5, :], 12.0, par[:, 6, :], ALU.mult, ALU.add))
            st.after()
            st.done(TS(par[:, 5, :], par[:, 5, :], 1e-30, None, ALU.max))
            st.after()
            st.done(power(par[:, 5, :], par[:, 5, :]))
            dve.wait_ge(s_bound, 1)
            st.done(TT(sm[:, 10, :], bank[2][:, 0:H], sm[:, 10, :], ALU.add))
            st.after()
            st.done(TS(sm[:, 10, :], sm[:, 10, :], 1e-30, None, ALU.max))
            st.after()
            st.done(power(sm[:, 10, :], sm[:, 10, :]))
            st.after()
            STT(sm[:, 0, :], sm[:, 10, :], 1.0 / (K_SCALE * Z_SCALE), par[:, 5, :], ALU.mult, ALU.mult).then_inc(s_pw, 1)
            st.done(V.reciprocal(sm[:, 14, :], sm[:, 10, :]))
            st.after()
            st.done(STT(sm[:, 11, :], sm[:, 14, :], K_SCALE, sm[:, 11, :], ALU.mult, ALU.mult))
            st.done(STT(sm[:, 13, :], sm[:, 14, :], K_SCALE, sm[:, 13, :], ALU.mult, ALU.mult))
            STT(d_row[:, :, 0:1], sm[:, 14, :].unsqueeze(2), K_SCALE, par[:, 7, :].unsqueeze(2),
                ALU.mult, ALU.mult).then_inc(s_dpad, 1)
            st.after()
            dve.wait_ge(s_pmag_done, 1)
            dve.wait_ge(s_ptrig, 2)
            st.done(TT(p_cnt, p_cnt, p_mag, ALU.mult))
            st.done(TT(p_sin, p_sin, p_mag, ALU.mult))
            st.after()
            c_r, c_i = over(sm[:, 11, :], NA), over(sm[:, 13, :], NA)
            st.done(TT(p_t1, c_r, p_cnt, ALU.mult))
            st.done(TT(p_t2, c_i, p_sin, ALU.mult))
            st.done(TT(p_ang, c_r, p_sin, ALU.mult))
            st.done(TT(p_mag, c_i, p_cnt, ALU.mult))
            st.after()
            st.done(TT(cp_re, p_t1, p_t2, ALU.subtract))
            TT(cp_im, p_ang, p_mag, ALU.add).then_inc(s_cp, 1)
            def bias(i, which, buf):
                dve.wait_ge(s_wmul, i + 1)
                TT(buf, buf, lnb[:, which, :].to_broadcast([P, buf.shape[1], H]),
                   ALU.add).then_inc(s_zf, 1)

            def low_part(i, tiles, buf):
                dve.wait_ge(s_z1, i + 1)
                hi, lo = (z_conv[:, :, k, tiles].rearrange("p h t -> p t h") for k in range(2))
                TT(lo, buf, hi, ALU.subtract).then_inc(s_z, 1)

            def row(buf, t):
                return buf[:, bass.ds(t, 1), :].rearrange("p a h -> p (a h)")

            def ln_rows():
                dve.wait_ge(s_wts, 16 * 5)
                dve.wait_ge(s_pwT, 1)
                st.done(magnitude(sm[:, 0:NL, :], lnw[:, 0:NL, :]))
                st.done(magnitude(sm[:, NL:2 * NL, :], lnb[:, 0:NL, :]))
                st.after()
                st.done(STT(sm[:, 0:NL, :], sm[:, 0:NL, :], 12.0, sm[:, NL:2 * NL, :], ALU.mult, ALU.add))
                st.after()
                st.done(TS(sm[:, 0:NL, :], sm[:, 0:NL, :], 1e-30, None, ALU.max))
                st.after()
                st.done(power(sm[:, 0:NL, :], sm[:, 0:NL, :]))
                st.after()
                st.done(V.reciprocal(sm[:, 0:NL, :], sm[:, 0:NL, :]))
                st.after()
                for row_of in (lnw, lnb):
                    st.done(STT(row_of[:, 0:NL, :], row_of[:, 0:NL, :], Z_SCALE, sm[:, 0:NL, :], ALU.mult, ALU.mult))
                st.after()
                dve.sem_inc(s_lnw, 2)

            dve.wait_ge(s_qtrig, 2)
            first_shift(0)
            first_shift(1)
            for g in range(H // 16):
                if g in (1, 2):
                    first_shift(g + 1)
                if g in (0, 1):
                    first_moments(2 + g)
                elif g % 2 == 0:
                    first_moments(CHUNKS + g // 2 - 1)
                elif g == 3:
                    ln_rows()
                dve.wait_ge(s_kps, 2 + g + 1)
                k_ps = bank[g % 2][0:NL * NA, :].rearrange("p (c b) -> p c b", b=NB)
                part = [k_sb[:, g * 16:(g + 1) * 16, :, k] for k in range(2)]
                V.tensor_copy(part[0], k_ps).then_inc(s_k1, 1)
                dve.wait_ge(s_k1, g + 1)
                TT(part[1], k_ps, part[0], ALU.subtract).then_inc(s_ksb, 1)
            V.memset(ones, 1.0).then_inc(s_ones, 1)
            dve.wait_ge(s_kz, 16)
            dve.wait_ge(s_fill, 16 * SEGS)
            dve.wait_ge(s_rstd, 2 * CHUNKS - 1)
            for p in range(NORMS - 2):
                STT(shift_part(p), mean_part(p), -1.0, rstd_part(p), ALU.mult, ALU.mult).then_inc(s_norm_in, 1)
            first_moments(2 * CHUNKS - 1)
            dve.wait_ge(s_rstd, 2 * CHUNKS)
            for p in range(NORMS - 2, NORMS):
                STT(shift_part(p), mean_part(p), -1.0, rstd_part(p), ALU.mult, ALU.mult).then_inc(s_norm_in, 1)
            for p in range(NORMS + 1):
                if p < NORMS:
                    buf = norm_bufs[p % 4]
                    dve.wait_ge(s_norm, (p + 1) * PART)
                    TT(buf, buf, lnw[:, 0:1, :].to_broadcast([P, PART, H]), ALU.mult).then_inc(s_wmul, 1)
                    bias(p, slice(0, 1), buf)
                if p > 0:
                    low_part(p - 1, slice((p - 1) * PART, p * PART), norm_bufs[(p - 1) % 4])

            LAYER_STEPS = TILES + 6 * NORMS + PART // 2
            dve.sem_inc(s_y, 4)
            with dve.Fori(0, NL) as layer:
                sp = Steps(dve, s_lay_dve, layer * LAYER_STEPS)
                for g in range(GROUPS):
                    dve.wait_ge(s_conv, SLOTS + layer * GROUPS + g + 1)
                    V.tensor_reduce(ybuf[:, :, g * GROUP:(g + 1) * GROUP].rearrange("p t c -> p c t"),
                                    bank[g % 4][:, :].rearrange("p (c k t) -> p c t k", c=GROUP, k=2),
                                    AX.X, ALU.add).then_inc(s_y, 1)

                def glu(q):
                    dve.wait_ge(s_glu_in, layer * QUADS + q + 1)
                    STT(g_out[:, q % 2, :], g_tanh[:, q % 2, :], 1.0, bank[2 + q % 2][:, :],
                        ALU.add, ALU.mult).then_inc(s_glu, 1)

                def residual(q):
                    dve.wait_ge(s_back, layer * QUADS + q + 1)
                    h4 = hres[:, q * 4:(q + 1) * 4, :].rearrange("p t h -> p (t h)")
                    TT(h4, bank[6 + q % 2][:, :], h4, ALU.add).then_inc(s_hadd, 1)
                    dve.wait_ge(s_hadd, 2 + layer * QUADS + q + 1)
                    for k in range(4):
                        sp.done(V.bn_stats(stats[:, q % 4 * 4 + k, :], hres[:, q * 4 + k, :]))
                for q in range(QUADS + 9):
                    p, k = divmod(q - 4, 2)
                    if k == 0 and 0 <= p < NORMS:
                        dve.wait_ge(s_rstd, 2 * CHUNKS + layer * NORMS + p + 1)
                        STT(shift_part(p), mean_part(p), -1.0, rstd_part(p), ALU.mult, ALU.mult).then_inc(s_norm_in, 1)
                    if 2 <= q < QUADS + 2:
                        residual(q - 2)
                        if q % 2 == 1:
                            p = (q - 3) // 2
                            moments(sp, None, mean_part(p), None, slice(p % 2 * PART, (p % 2 + 1) * PART))
                    if q < QUADS:
                        glu(q)
                    p, k = divmod(q - 8, 2)
                    if k == 0 and 0 <= p < NORMS:
                        buf, i = norm_bufs[p % 4], (layer + 1) * NORMS + p
                        if p == NORMS - 1:
                            dve.wait_ge(s_norm, TILES + (layer + 1) * NORM_TILES)
                            sp.after()
                            TT(buf, buf, lnw_cur[:, :, :].to_broadcast([P, PART, H]), ALU.mult).then_inc(s_wmul, 1)
                        bias(i, bass.ds(layer + 1, 1), buf)
                    p, k = divmod(q - 10, 2)
                    if k == 0 and 0 <= p < NORMS:
                        low_part((layer + 1) * NORMS + p, slice(p * PART, (p + 1) * PART), norm_bufs[p % 4])
                    if q == QUADS + 3:
                        p = NORMS - 1
                        for k in range(PART // 2, PART):
                            sp.done(TS(norm_bufs[p % 4][:, k, :], hres[:, p * PART + k, :], mean_part(p)[:, k:k + 1],
                                       rstd_part(p)[:, k:k + 1], ALU.subtract, ALU.mult))
                assert sp.n == LAYER_STEPS, sp.n

            dve.wait_ge(s_x2, 16)
            dve.wait_ge(s_z, (NL + 1) * NORMS)
            st.after()
            done = 2 * CHUNKS + NL * NORMS
            def residual_x(c):
                tiles = slice(c * CHUNK, (c + 1) * CHUNK)
                hi, lo = (z_conv[:, :, k, tiles].rearrange("p h t -> p t h") for k in range(2))
                st.done(TT(ln_tmp[:, :, :], hi, lo, ALU.add))
                st.after()
                st.done(STT(hres[:, tiles, :].rearrange("p t h -> p (t h)"), ln_tmp[:, :, :].rearrange("p t h -> p (t h)"),
                            1.0 / Z_SCALE, ybuf[:, tiles, :].rearrange("p t h -> p (t h)"), ALU.mult, ALU.add))
                st.after()
                moments(st, lambda k: hres[:, c * CHUNK + k, :], mean_of[:, c], done + c)

            def normal_x(c):
                dve.wait_ge(s_rstd, done + c + 1)
                for k in range(CHUNK):
                    TS(ybuf[:, c * CHUNK + k, :], hres[:, c * CHUNK + k, :], mean_of[:, c, k:k + 1], rstd_of[:, c, k:k + 1],
                       ALU.subtract, ALU.mult).then_inc(s_z2, 1)

            def choose(c):
                tiles = slice(c * CHUNK, (c + 1) * CHUNK)
                R = [route[:, k] for k in range(12)]
                one = [route[:, k, :, 0:1] for k in range(12)]

                def wide(v):
                    return v.to_broadcast([P, CHUNK, E])
                if c == 0:
                    dve.wait_ge(s_mc, 5)
                dve.wait_ge(s_logits, c + 1)
                gates = bank[6][:, 0:CHUNK * E].rearrange("p (t e) -> p t e", e=E)
                st.done(V.tensor_reduce(one[2], gates, AX.X, ALU.max))
                st.after()
                TT(R[0], gates, wide(one[2]), ALU.subtract).then_inc(s_lread, 1)
                dve.wait_ge(s_rexp, c + 1)
                st.done(V.tensor_reduce(one[3], R[1], AX.X, ALU.add))
                st.after()
                st.done(V.reciprocal(one[4], one[3]))
                st.after()
                st.done(TT(R[5], R[1], wide(one[4]), ALU.mult))
                st.after()
                left = R[5]
                g = SEG_OF[c]
                at_c = (c - SEGMENTS[g][0]) * CHUNK
                in_seg = slice(at_c, at_c + CHUNK)
                R[10], R[11] = hot_of[:, 0, in_seg], hot_of[:, 1, in_seg]
                if g > 0 and at_c == 0:
                    dve.wait_ge(s_prefix, g)
                for hot in (10, 11):
                    st.done(V.tensor_reduce(one[7], left, AX.X, ALU.max))
                    st.after()
                    st.done(TT(R[8], left, wide(one[7]), ALU.is_equal))
                    st.after()
                    st.done(TT(R[8], R[8], rank.unsqueeze(1).to_broadcast([P, CHUNK, E]), ALU.mult))
                    st.after()
                    st.done(V.tensor_reduce(one[9], R[8], AX.X, ALU.max))
                    st.after()
                    st.done(TT(R[hot], R[8], wide(one[9]), ALU.is_equal))
                    st.after()
                    if hot == 10:
                        st.done(STT(R[6], R[hot], -2.0, R[5], ALU.mult, ALU.add))
                        st.after()
                        left = R[6]
                TT(mask[:, in_seg], R[10], R[11], ALU.add).then_inc(s_mask, 1)
                dve.wait_ge(s_zhi, c + 1)
                STT(z_pair[c][:, :, 1, :], ybuf[:, tiles, :], Z_SCALE, z_pair[c][:, :, 0, :],
                    ALU.mult, ALU.subtract).then_inc(s_zlo, 1)
                for k in range(2):
                    st.done(TT(R[8 + k], R[10 + k], R[5], ALU.mult))
                st.after()
                for k in range(2):
                    st.done(V.tensor_reduce(weight[:, k, tiles].unsqueeze(2), R[8 + k], AX.X, ALU.add))

            def places(g):
                tiles, xt = SEG_TILES[g], XTS[g]
                dve.wait_ge(s_prefix, g + 1)
                count = bank[7][:, tiles * E:tiles * E + E]
                st.done(TS(n_tiles, count, 1.0 / XP, (XP - 1.0) / XP - 0.5 + 0.5 / XP, ALU.mult, ALU.add))
                st.after()
                st.done(TS(n_tiles, n_tiles, ROUND, None, ALU.add))
                st.after()
                st.done(TS(n_tiles, n_tiles, ROUND, None, ALU.subtract))
                st.after()
                st.done(V.tensor_tensor_scan(ends, ones8, n_tiles, 0.0, ALU.mult, ALU.add))
                st.after()
                st.done(TT(base, ends, n_tiles, ALU.subtract))
                st.done(TT(past[0:1, 0:xt], tile_no[0:1, 0:xt].unsqueeze(2).to_broadcast([1, xt, E]),
                           ends[0:1].unsqueeze(1).to_broadcast([1, xt, E]), ALU.is_ge))
                st.after()
                st.done(TS(base, base, float(XP), None, ALU.mult))
                st.done(V.tensor_reduce(owner_f[0:1, 0:xt].unsqueeze(2), past[0:1, 0:xt], AX.X, ALU.add))
                st.after()
                st.done(TS(owner[0:1, g, 0:xt], owner_f[0:1, 0:xt], E - 1.0, float(WE), ALU.min, ALU.mult))
                ranks = bank[7][:, 0:tiles * E].rearrange("p (t e) -> p t e", e=E)
                st.done(TT(place[:, 0:tiles], ranks, base.unsqueeze(1).to_broadcast([P, tiles, E]), ALU.add))
                st.after()
                for k in range(2):
                    st.done(TT(hot_of[:, k, 0:tiles], hot_of[:, k, 0:tiles], place[:, 0:tiles], ALU.mult))
                st.after()
                for k in range(2):
                    st.done(V.tensor_reduce(slot_f[:, k, 0:tiles].unsqueeze(2), hot_of[:, k, 0:tiles], AX.X, ALU.add))
                st.after()
                V.tensor_copy(slot[:, :, SEGMENTS[g][0] * CHUNK:SEGMENTS[g][0] * CHUNK + tiles], slot_f[:, :, 0:tiles]).then_inc(s_slots, 1)

            residual_x(0)
            residual_x(1)
            normal_x(0)
            residual_x(2)
            choose(0)
            places(0)
            normal_x(1)
            residual_x(3)
            choose(1)
            normal_x(2)
            normal_x(3)
            choose(2)
            places(1)
            choose(3)
            places(2)

            def xT_copy(n, k):
                dve.wait_ge(s_xT, n + 1)
                if not (isinstance(n, int) and n < 2):
                    dve.wait_ge(s_hid, n - 1)
                V.tensor_copy(xT[:, k % 2, :], bank[k % 2][:, :]).then_inc(s_xTsb, 1)

            def step(first, xt, n, k, div):
                if n_at(n) < xt - 1:
                    xT_copy(n + (first + 1), k + 1)
                if 1 <= n_at(n) < xt + 1:
                    dve.wait_ge(s_ihi, n + first)
                    STT(inner16[:, (k - 1) % 4, 1, :], inner[:, (k - 1) % 2, :], I_SCALE / (Z_SCALE * W_SCALE),
                        inner16[:, (k - 1) % 4, 0, :], ALU.mult, ALU.subtract).then_inc(s_ilo, 1)
                if n_at(n) < xt:
                    dve.wait_ge(s_silu, n + (first + 1))
                    if not (isinstance(n, int) and first + n < 2):
                        dve.wait_ge(s_ilo, n + (first - 1))
                    TT(inner[:, k % 2, :], bank[3 + k % 2 * 2][:, :], gate_act[:, k % 2, :], ALU.mult).then_inc(s_inner, 1)
            for g in range(SEGS):
                xT_copy(FIRSTS[g], 0)
                tile_steps(dve, XTS[g], lambda n, k, div, _: step(FIRSTS[g], XTS[g], n, k, div))
            def weighted_sum(p):
                y1, y2 = (y_of(k, p * PART, PART) for k in range(2))
                dve.wait_ge(s_gath[p], 16 * 2 * PART)
                dve.wait_ge(s_w1y, (p + 1) * PART)
                for k in range(PART):
                    at_t = p * PART + k
                    st.done(STT(y1[:, k, :], y2[:, k, :], weight[:, 1, at_t:at_t + 1], y1[:, k, :], ALU.mult, ALU.add))
                st.after()
                at = p % 2 * PART
                for k in range(PART):
                    st.done(V.bn_stats(stats[:, at + k, :], y1[:, k, :]))
                moments(st, None, mean_part(p), None, slice(at, at + PART))

            def last_shift(p):
                dve.wait_ge(s_rstd, done + CHUNKS + p + 1)
                STT(shift_part(p), mean_part(p), -1.0, rstd_part(p), ALU.mult, ALU.mult).then_inc(s_last_in, 1)

            def result(p):
                tiles = slice(p * PART, (p + 1) * PART)
                dve.wait_ge(s_last, (p + 1) * PART)
                TT(hres[:, tiles, :], y_of(0, p * PART, PART), hres[:, tiles, :], ALU.add).then_inc(s_res, 1)
            for p in range(NORMS + 2):
                if p < NORMS:
                    weighted_sum(p)
                if 0 < p <= NORMS:
                    last_shift(p - 1)
                if p > 1:
                    result(p - 2)


_NAMES = ("x", "a_re_log", "a_im", "c_re", "c_im", "log_dt", "d_skip", "ln_w", "ln_b", "w_out", "b_out", "b_rows",
          "w1", "w2", "router")


def kernel(**inputs):
    import numpy as np
    import concourse.bacc as bacc
    from concourse.bass_utils import run_bass_kernel_spmd

    g = {k: np.asarray(v) for k, v in inputs.items()}
    x = g["L0_attn_x"].reshape(B, J, P, H)[:, :, ::-1, :].transpose(2, 1, 0, 3).reshape(P, TILES, H)
    modes = {k: g["L0_attn_" + k].transpose(0, 2, 1).reshape(NL * N, H) for k in ("A_re_log", "A_im", "C_re", "C_im")}
    laid = [x, modes["A_re_log"], modes["A_im"], modes["C_re"], modes["C_im"],
            g["L0_attn_log_dt"], g["L0_attn_D_skip"], g["L0_attn_ln_w"], g["L0_attn_ln_b"],
            g["L0_attn_W_out"].transpose(2, 0, 1), g["L0_attn_b_out"].reshape(NL, 2, H).transpose(2, 0, 1),
            g["L0_attn_b_out"].reshape(NL, 2, H), g["L0_ffn_w1"].transpose(2, 0, 1),
            g["L0_ffn_w2"].reshape(E, H, 2, P).transpose(3, 0, 2, 1),
            g["L0_ffn_router_w"].T]
    nc = bacc.Bacc("TRN2", target_bir_lowering=False, num_devices=1)
    arrays, args = {}, []
    for name, a in zip(_NAMES, laid):
        a = np.ascontiguousarray(a)
        arrays[f"in_{name}"] = a
        args.append(nc.dram_tensor(f"in_{name}", a.shape, mybir.dt.from_np(a.dtype), kind="ExternalInput").ap())
    args.append(nc.dram_tensor("out_0", (P, TILES, H), F32, kind="ExternalOutput").ap())
    build(nc, *args)
    r = run_bass_kernel_spmd(nc, [arrays], core_ids=[0])
    o = np.asarray(r.results[0]["out_0"]).reshape(P, J, B, H).transpose(2, 1, 0, 3)[:, :, ::-1, :]
    return np.ascontiguousarray(o).reshape(B, L, H)
```
